# Optimizing a Trainium2 kernel written in Bass

```python
import numpy as np
import jax
import jax.numpy as jnp

def _softmax(x, axis=-1):
    return jax.nn.softmax(x, axis=axis)

def _gelu(x):
    return jax.nn.gelu(x, approximate=True)

def _silu(x):
    return jax.nn.silu(x)

def _sigmoid(x):
    return jax.nn.sigmoid(x)

def _layernorm(x, axis=-1, eps=1e-05):
    m = jnp.mean(x, axis=axis, keepdims=True)
    v = jnp.var(x, axis=axis, keepdims=True)
    return (x - m) / jnp.sqrt(v + eps)

def _scatter_add(tgt, idx, src, axis=0):
    return tgt.at[idx].add(src)

def _segment_sum(src, seg, n):
    return jax.ops.segment_sum(src, seg, n)
kernel_name = 'mk_macaron_d1_jaxref_r8_9150ee'

def setup_inputs(seed: int=0):
    np.random.seed(seed)
    _w = jnp.asarray

    def _L0_attn_setup():
        import jax, jax.numpy as jnp
        import numpy as np
        NUM_HEAD = 16
        D_Q = 64
        D_KV = 64
        ROPE_BASE = 10000.0

        def _cos_sin(seq_len, dim):
            pos = jnp.arange(seq_len, dtype=jnp.float32)[:, None]
            ids = jnp.arange(dim // 2, dtype=jnp.float32)
            theta = ROPE_BASE ** (-2.0 * ids) / (dim // 2)
            r = pos * theta[None, :]
            return (jnp.cos(r), jnp.sin(r))

        def _rope(x, cos, sin):
            b, s, d = x.shape
            xv = x.reshape(b, s, d // 2, 2)
            x0, x1 = (xv[..., 0], xv[..., 1])
            out = jnp.stack([x0 * cos - x1 * sin, x1 * cos + x0 * sin], axis=-1)
            return out.reshape(b, s, d)
        key = jax.random.key(seed)
        ks = jax.random.split(key, 10)
        d_model, d_q, d_kv = (128, D_Q, D_KV)
        b, s = (2, 256)
        w = lambda k, i, o: jax.random.normal(k, (i, o), dtype=jnp.float32) * 0.02
        return {'x': jax.random.normal(ks[0], (b, s, d_model), dtype=jnp.float32), 'Wd_q_w': w(ks[1], d_model, d_q), 'Wd_q_b': jnp.zeros((d_q,), jnp.float32), 'Wu_q_w': w(ks[2], d_q, d_model), 'Wu_q_b': jnp.zeros((d_model,), jnp.float32), 'Wq_r_w': w(ks[3], d_q, d_model), 'Wq_r_b': jnp.zeros((d_model,), jnp.float32), 'Wk_r_w': w(ks[4], d_model, d_model), 'Wk_r_b': jnp.zeros((d_model,), jnp.float32), 'Wd_kv_w': w(ks[5], d_model, d_kv), 'Wd_kv_b': jnp.zeros((d_kv,), jnp.float32), 'Wu_k_w': w(ks[6], d_kv, d_model), 'Wu_k_b': jnp.zeros((d_model,), jnp.float32), 'Wu_v_w': w(ks[7], d_kv, d_model), 'Wu_v_b': jnp.zeros((d_model,), jnp.float32), 'Wo_w': w(ks[8], d_model, d_model), 'Wo_b': jnp.zeros((d_model,), jnp.float32)}
    _L0_attn_in = _L0_attn_setup()

    def _L0_ffn_setup():
        import jax, jax.numpy as jnp
        import numpy as np
        NUM_EXPERTS_TOTAL = 9
        TOP_K = 2
        key = jax.random.key(seed)
        k0, k1, k2, k3, k4 = jax.random.split(key, 5)
        B, S, H, I = (2, 256, 128, 352)
        E = NUM_EXPERTS_TOTAL
        x = jax.random.normal(k0, (B, S, H), dtype=jnp.float32)
        Wr = jax.random.normal(k1, (H, E), dtype=jnp.float32) * 0.02
        Wg = jax.random.normal(k2, (E, H, I), dtype=jnp.float32) * 0.02
        Wu = jax.random.normal(k3, (E, H, I), dtype=jnp.float32) * 0.02
        Wd = jax.random.normal(k4, (E, I, H), dtype=jnp.float32) * 0.02
        return {'x': x, 'Wr': Wr, 'Wg': Wg, 'Wu': Wu, 'Wd': Wd}
    _L0_ffn_in = _L0_ffn_setup()
    _d = {'L0_attn_x': _L0_attn_in['x'], 'L0_attn_Wd_q_w': _L0_attn_in['Wd_q_w'], 'L0_attn_Wd_q_b': _L0_attn_in['Wd_q_b'], 'L0_attn_Wu_q_w': _L0_attn_in['Wu_q_w'], 'L0_attn_Wu_q_b': _L0_attn_in['Wu_q_b'], 'L0_attn_Wq_r_w': _L0_attn_in['Wq_r_w'], 'L0_attn_Wq_r_b': _L0_attn_in['Wq_r_b'], 'L0_attn_Wk_r_w': _L0_attn_in['Wk_r_w'], 'L0_attn_Wk_r_b': _L0_attn_in['Wk_r_b'], 'L0_attn_Wd_kv_w': _L0_attn_in['Wd_kv_w'], 'L0_attn_Wd_kv_b': _L0_attn_in['Wd_kv_b'], 'L0_attn_Wu_k_w': _L0_attn_in['Wu_k_w'], 'L0_attn_Wu_k_b': _L0_attn_in['Wu_k_b'], 'L0_attn_Wu_v_w': _L0_attn_in['Wu_v_w'], 'L0_attn_Wu_v_b': _L0_attn_in['Wu_v_b'], 'L0_attn_Wo_w': _L0_attn_in['Wo_w'], 'L0_attn_Wo_b': _L0_attn_in['Wo_b'], 'L0_ffn_Wr': _L0_ffn_in['Wr'], 'L0_ffn_Wg': _L0_ffn_in['Wg'], 'L0_ffn_Wu': _L0_ffn_in['Wu'], 'L0_ffn_Wd': _L0_ffn_in['Wd']}
    _x0 = _d['L0_attn_x']
    _d['L0_attn_x'] = jax.random.normal(jax.random.fold_in(jax.random.key(seed), 1), (1, 2048, 128), dtype=_x0.dtype)
    del _x0
    return _d

def reference(L0_attn_x, L0_attn_Wd_q_w, L0_attn_Wd_q_b, L0_attn_Wu_q_w, L0_attn_Wu_q_b, L0_attn_Wq_r_w, L0_attn_Wq_r_b, L0_attn_Wk_r_w, L0_attn_Wk_r_b, L0_attn_Wd_kv_w, L0_attn_Wd_kv_b, L0_attn_Wu_k_w, L0_attn_Wu_k_b, L0_attn_Wu_v_w, L0_attn_Wu_v_b, L0_attn_Wo_w, L0_attn_Wo_b, L0_ffn_Wr, L0_ffn_Wg, L0_ffn_Wu, L0_ffn_Wd):

    def _L0_attn_ref(x, Wd_q_w, Wd_q_b, Wu_q_w, Wu_q_b, Wq_r_w, Wq_r_b, Wk_r_w, Wk_r_b, Wd_kv_w, Wd_kv_b, Wu_k_w, Wu_k_b, Wu_v_w, Wu_v_b, Wo_w, Wo_b):
        import jax, jax.numpy as jnp
        import numpy as np
        NUM_HEAD = 16
        D_Q = 64
        D_KV = 64
        ROPE_BASE = 10000.0

        def _cos_sin(seq_len, dim):
            pos = jnp.arange(seq_len, dtype=jnp.float32)[:, None]
            ids = jnp.arange(dim // 2, dtype=jnp.float32)
            theta = ROPE_BASE ** (-2.0 * ids) / (dim // 2)
            r = pos * theta[None, :]
            return (jnp.cos(r), jnp.sin(r))

        def _rope(x, cos, sin):
            b, s, d = x.shape
            xv = x.reshape(b, s, d // 2, 2)
            x0, x1 = (xv[..., 0], xv[..., 1])
            out = jnp.stack([x0 * cos - x1 * sin, x1 * cos + x0 * sin], axis=-1)
            return out.reshape(b, s, d)
        b, s, d_model = x.shape
        h = NUM_HEAD
        hd = d_model // h
        scale = jnp.sqrt(jnp.float32(h + D_KV + D_Q))

        def heads(t):
            return t.reshape(b, s, h, hd).transpose(0, 2, 1, 3)
        cos, sin = _cos_sin(s, d_model)
        ct_q = x @ Wd_q_w + Wd_q_b
        qt_c = heads(ct_q @ Wu_q_w + Wu_q_b)
        qt_r = heads(_rope(ct_q @ Wq_r_w + Wq_r_b, cos, sin))
        query = qt_c + qt_r
        ct_kv = x @ Wd_kv_w + Wd_kv_b
        kt_c = heads(ct_kv @ Wu_k_w + Wu_k_b)
        kt_r = heads(_rope(x @ Wk_r_w + Wk_r_b, cos, sin))
        key = kt_c + kt_r
        value = heads(ct_kv @ Wu_v_w + Wu_v_b)
        attn = jnp.einsum('bhqd,bhkd->bhqk', query, key) / scale
        attn = jax.nn.softmax(attn, axis=-1)
        out = jnp.einsum('bhqk,bhkd->bhqd', attn, value)
        out = out.transpose(0, 2, 1, 3).reshape(b, s, d_model)
        return out @ Wo_w + Wo_b

    def _L0_ffn_ref(x, Wr, Wg, Wu, Wd):
        import jax, jax.numpy as jnp
        import numpy as np
        NUM_EXPERTS_TOTAL = 9
        TOP_K = 2
        B, S, H = x.shape
        E = NUM_EXPERTS_TOTAL
        T = B * S
        logits = jnp.einsum('bsh,he->bse', x, Wr)
        probs = jax.nn.softmax(logits, axis=-1)
        topk_w, topk_idx = jax.lax.top_k(probs, TOP_K)
        topk_w = topk_w / jnp.sum(topk_w, axis=-1, keepdims=True)
        xf = x.reshape(T, H)
        wf = topk_w.reshape(T, TOP_K)
        idxf = topk_idx.reshape(T, TOP_K)
        cw = jnp.zeros((T, E), dtype=x.dtype).at[jnp.arange(T)[:, None], idxf].add(wf)
        gate = jax.nn.silu(jnp.einsum('th,ehi->tei', xf, Wg))
        hidden = gate * jnp.einsum('th,ehi->tei', xf, Wu)
        out = jnp.einsum('tei,eih,te->th', hidden, Wd, cw)
        return out.reshape(B, S, H)
    x = L0_attn_x
    x = x + 0.5 * _L0_ffn_ref(_layernorm(x, axis=-1), L0_ffn_Wr, L0_ffn_Wg, L0_ffn_Wu, L0_ffn_Wd)
    x = x + _L0_attn_ref(_layernorm(x, axis=-1), L0_attn_Wd_q_w, L0_attn_Wd_q_b, L0_attn_Wu_q_w, L0_attn_Wu_q_b, L0_attn_Wq_r_w, L0_attn_Wq_r_b, L0_attn_Wk_r_w, L0_attn_Wk_r_b, L0_attn_Wd_kv_w, L0_attn_Wd_kv_b, L0_attn_Wu_k_w, L0_attn_Wu_k_b, L0_attn_Wu_v_w, L0_attn_Wu_v_b, L0_attn_Wo_w, L0_attn_Wo_b)
    x = x + 0.5 * _L0_ffn_ref(_layernorm(x, axis=-1), L0_ffn_Wr, L0_ffn_Wg, L0_ffn_Wu, L0_ffn_Wd)
    return x

_drawn_inputs = setup_inputs


def setup_inputs(seed=0):
    import zlib

    import numpy as np

    out = dict(_drawn_inputs(seed))
    spreads = {'L0_attn_Wd_q_b': (0.0, 0.8),
     'L0_attn_Wu_q_b': (0.0, 0.8),
     'L0_attn_Wq_r_b': (0.0, 0.8),
     'L0_attn_Wk_r_b': (0.0, 2.0),
     'L0_attn_Wd_kv_b': (0.0, 0.8),
     'L0_attn_Wu_k_b': (0.0, 2.0),
     'L0_attn_Wu_v_b': (0.0, 0.368),
     'L0_attn_Wo_b': (0.0, 0.1)}
    factors = {'L0_attn_Wd_q_w': 8.0,
     'L0_attn_Wu_q_w': 8.0,
     'L0_attn_Wq_r_w': 8.0,
     'L0_attn_Wk_r_w': 8.0,
     'L0_attn_Wd_kv_w': 8.0,
     'L0_attn_Wu_k_w': 8.0,
     'L0_attn_Wu_v_w': 8.0,
     'L0_attn_Wo_w': 2.673,
     'L0_ffn_Wr': 8.0,
     'L0_ffn_Wg': 8.0,
     'L0_ffn_Wu': 8.0,
     'L0_ffn_Wd': 8.0}
    for name, (base, spread) in spreads.items():
        noise = np.random.default_rng([zlib.crc32(name.encode()), seed]).standard_normal(out[name].shape)
        drawn = base * np.exp(spread * noise) if base else spread * noise
        out[name] = jnp.asarray(drawn.astype(out[name].dtype))
    for name, factor in factors.items():
        out[name] = (out[name] * factor).astype(out[name].dtype)
    return out
```

```python
from contextlib import ExitStack

import numpy as np

import concourse.bass as bass
from concourse import mybir

F32 = mybir.dt.float32
F16 = mybir.dt.float16
BF16 = mybir.dt.bfloat16
I32 = mybir.dt.int32
ALU = mybir.AluOpType
ACT = mybir.ActivationFunctionType
AX = mybir.AxisListType

P = 128
T = 2048
D = 128
NT = T // P
E = 9
F = 352
K2 = 2
SLOT_TILES = (K2 * T + E * (P - 1)) // P
FCH = [(0, 128), (128, 128), (256, 96)]
LN_EPS = 1e-5
SCORE_SAFE = 60.0
RING = 4
NO_ROW = K2 * T

H = 16
HD = 8
DQ = 64
ROPE_BASE = 10000.0
SCORE_SCALE = float(1.0 / np.sqrt(np.float32(H + 64 + DQ)))
CH = 512
NC = T // CH
PARTS = 3
ROWS = PARTS * PARTS * HD
SHIFT_ROW = ROWS
KR = 96
SLOTS = 3
GB = 3
AW = {n: i for i, n in enumerate(["ct", "uq", "qr", "qrs", "uk", "kr", "krs", "uv", "wo"])}
AB = {n: i for i, n in enumerate(["ct", "uq", "qr", "qrs", "uk", "kr", "krs"])}

CONST_COLS = {}
_at = 0
for _n, _w in [("ident", P), ("lower", P), ("ones", P), ("iota", P), ("emark", E), ("jramp", SLOT_TILES),
               ("thresh", NT * K2), ("tri", E * E), ("token", K2 * NT), ("kmark", K2 * NT), ("hsum", 2 * 32)]:
    CONST_COLS[_n] = (_at, _w)
    _at += _w
CONST_W = _at


def constant_array():
    c = np.zeros((P, CONST_W), np.float32)

    def put(name, value):
        a, w = CONST_COLS[name]
        c[:, a:a + w] = value

    p = np.arange(P)
    put("ident", np.eye(P))
    put("lower", (p[:, None] < p[None, :]))
    put("ones", 1.0)
    put("iota", p[None, :])
    put("emark", np.arange(E)[None, :] - E)
    put("jramp", np.arange(SLOT_TILES)[None, :])
    put("thresh", P * np.arange(NT * K2)[None, :])
    e = np.arange(E)
    put("tri", (e[None, :] < e[:, None]).reshape(1, -1))
    put("token", np.tile(NT * p[:, None] + np.arange(NT)[None, :], (1, K2)))
    put("kmark", np.repeat(-(np.arange(K2) + 1.0) * T, NT)[None, :])
    head = (p[:, None] // HD == np.arange(H)[None, :])
    none = np.zeros((P, H))
    put("hsum", np.concatenate([head, none, none, head], axis=1))
    return c


def rope_arrays():
    ids = np.arange(D // 2, dtype=np.float32)
    theta = (np.float32(ROPE_BASE) ** (np.float32(-2.0) * ids) / np.float32(D // 2)).astype(np.float32)
    col = np.arange(T)
    pos = (NT * (col % P) + col // P).astype(np.float32)
    r = (pos[None, :] * np.repeat(theta, 2)[:, None]).astype(np.float32)
    sign = np.where(np.arange(D) % 2 == 0, -1.0, 1.0)[:, None]
    return np.cos(r).astype(np.float32), (sign * np.sin(r)).astype(np.float32)


def pack_attention(g):
    def at(w, row):
        full = np.zeros((P, D), np.float32)
        full[row:row + w.shape[0]] = w
        return full

    def swap(w):
        return w.reshape(w.shape[:-1] + (D // 2, 2))[..., ::-1].reshape(w.shape)

    g = {n.replace("L0_attn_", ""): np.asarray(v) for n, v in g.items()}
    w = [np.concatenate([g["Wd_q_w"], g["Wd_kv_w"]], axis=1), at(g["Wu_q_w"], 0), at(g["Wq_r_w"], 0), at(swap(g["Wq_r_w"]), 0),
         at(g["Wu_k_w"], DQ), g["Wk_r_w"], swap(g["Wk_r_w"]), at(g["Wu_v_w"], DQ), g["Wo_w"]]
    b = [np.concatenate([g["Wd_q_b"], g["Wd_kv_b"]]), g["Wu_q_b"], g["Wq_r_b"], swap(g["Wq_r_b"]),
         g["Wu_k_b"], g["Wk_r_b"], swap(g["Wk_r_b"])]
    return (np.ascontiguousarray(np.stack(w, axis=1)), np.ascontiguousarray(np.stack(b, axis=1)),
            np.ascontiguousarray(np.stack([g["Wu_v_b"], g["Wo_b"]])))


def macaron_block(nc, ins, const, rope_cos, rope_sin, attn_w, attn_b, attn_rows, out):
    with ExitStack() as ctx:
        def sb(name, shape, dt):
            return ctx.enter_context(nc.sbuf_tensor(name, shape, dt))

        def sem(name):
            return ctx.enter_context(nc.semaphore(name))

        def dram(name, shape, dt):
            return nc.dram_tensor(name, shape, dt, kind="Internal").ap()

        cst = sb("cst", [P, CONST_W], F32)
        X = sb("X", [P, NT, D], F32)
        XN = sb("XN", [P, NT, D], F32)
        XNT = sb("XNT", [P, T], F32)
        Wr = sb("Wr", [P, E], F32)
        Wgu = sb("Wgu", [P, E, 2 * F], F32)
        Wd = sb("Wd", [P, E, 3, D], F32)
        stats = sb("stats", [P, NT, 6], F32)
        mv = sb("mv", [P, NT, 2], F32)
        var = sb("var", [P, NT], F32)
        rstd = sb("rstd", [P, NT], F32)
        newt = sb("newt", [P, NT], F32)
        lower_b = sb("lower_b", [P, P], BF16)
        ones_b = sb("ones_b", [P, P], BF16)
        iota_h = sb("iota_h", [P, P], F16)
        L = sb("L", [P, NT, E], F32)
        tmpE = sb("tmpE", [P, K2, NT, E], F32)
        pick = sb("pick", [P, K2, NT, E], F32)
        top = sb("top", [P, K2, NT], F32)
        first = sb("first", [P, K2, NT], F32)
        both = sb("both", [P, NT, E], BF16)
        wts = sb("wts", [P, K2, NT], F32)
        tot = sb("tot", [P, E], F32)
        over = sb("over", [P, E, NT * K2], F32)
        ntile = sb("ntile", [P, E], F32)
        tri_p = sb("tri_p", [P, E, E], F32)
        tbase = sb("tbase", [P, E], F32)
        tend = sb("tend", [P, E], F32)
        passed = sb("passed", [P, SLOT_TILES, E], F32)
        texp = sb("texp", [P, SLOT_TILES], F32)
        woff = sb("woff", [P, 2, SLOT_TILES], I32)
        slot = sb("slot", [P, NT, E], F32)
        pos = sb("pos", [P, K2 * NT], F32)
        posi = sb("posi", [P, 3, K2 * NT], I32)
        OA = sb("OA", [P, K2 * NT, 2 * SLOT_TILES], F16)
        idx = sb("idx", [P, 2, SLOT_TILES], I32)
        xg = sb("xg", [P, RING, D], F32)
        xgT = sb("xgT", [P, 2, P], F32)
        sg = sb("sg", [P, 2, F], F32)
        hid = sb("hid", [P, 2, F], F32)
        hidT = sb("hidT", [P, 2, 3, P], F32)
        yt = sb("yt", [P, RING, D], F32)
        shared = sb("shared", [P, SLOTS * T], F32)
        Y = shared[:, 0:K2 * T].rearrange("p (k i d) -> p k i d", k=K2, d=D)
        OB = shared[:, K2 * T:].bitcast(F16).rearrange("p (n q) -> p n q", q=P)
        temp = shared[:, 0:10 * CH].rearrange("p (a b n) -> p a b n", a=5, b=2)
        EXP = shared[:, :].rearrange("p (b n) -> p b n", n=T)
        cosT = sb("cosT", [P, T], F32)
        sinT = sb("sinT", [P, T], F32)
        aw = sb("aw", [P, len(AW), D], F32)
        ab = sb("ab", [P, len(AB)], F32)
        bv_rows = sb("bv_rows", [P, D], F32)
        bo_rows = sb("bo_rows", [P, D], F32)
        ct = sb("ct", [P, T], F32)
        parts = sb("parts", [P, 2, PARTS, CH], BF16)
        V = sb("V", [P, NT, D], F32)
        qslot = sb("qslot", [P, SLOTS, T], BF16)
        kslot = sb("kslot", [P, SLOTS, T], BF16)
        vslot = sb("vslot", [P, SLOTS, NT, 32], F32)
        nmax = sb("nmax", [P, 1], F32)
        nrow = sb("nrow", [1, 2 * H], F32)
        bound = sb("bound", [1, H], F32)
        largest = sb("largest", [1, 1], F32)
        safe = sb("safe", [1, 1], I32)
        smax = sb("smax", [P, 2, P], F32)
        snext = sb("snext", [P, 2, P], F32)
        sparts = sb("sparts", [P, PARTS, 2, P], BF16)
        zeros48 = sb("zeros48", [PARTS * H, T], BF16)
        Osb = sb("Osb", [P, CH], F32)
        denom = sb("denom", [P, 4, 4], F32)
        A = XN
        AT = XNT

        PS = ctx.enter_context(nc.psum_tensor("PS", [P, 8, CH], F32))

        xn_dram = [dram(f"xn_dram{f}", [T, D], F32) for f in range(2)]
        qk_dram = [dram(f"qk_dram{n}", [PARTS, P, T], BF16) for n in range(2)]
        shift_dram = dram("shift_dram", [PARTS, H, T], BF16)
        y_dram = [dram(f"y_dram{f}", [K2 * T, D], F32) for f in range(2)]

        def c(name):
            a, w = CONST_COLS[name]
            return cst[:, a:a + w]

        ident = c("ident")

        const_in = sem("const_in")
        x_in = [sem(f"x_in{q}") for q in range(4)]
        denom_done = sem("denom_done")
        wr_in = sem("wr_in")
        wexp_in = sem("wexp_in")
        consts_cast = sem("consts_cast")
        vstep = sem("vstep")

        class LnSems:
            def __init__(self, n):
                self.var = sem(f"{n}_var")
                self.sd = sem(f"{n}_sd")
                self.xn = sem(f"{n}_xn")
                self.T = sem(f"{n}_T")
                self.xnT = sem(f"{n}_xnT")

        class FfnSems:
            def __init__(self, n):
                self.ln = LnSems(n)
                self.xn_out = sem(f"{n}_xn_out")
                self.logits = sem(f"{n}_logits")
                self.top2 = sem(f"{n}_top2")
                self.exp2 = sem(f"{n}_exp2")
                self.both = sem(f"{n}_both")
                self.ranks = sem(f"{n}_ranks")
                self.woff = sem(f"{n}_woff")
                self.onehot = sem(f"{n}_onehot")
                self.slots = sem(f"{n}_slots")
                self.idx = sem(f"{n}_idx")
                self.xg = [sem(f"{n}_xg{s}") for s in range(RING)]
                self.xgT_ps = sem(f"{n}_xgT_ps")
                self.xgT = sem(f"{n}_xgT")
                self.gate = sem(f"{n}_gate")
                self.up = sem(f"{n}_up")
                self.silu = sem(f"{n}_silu")
                self.hid = sem(f"{n}_hid")
                self.hidT_ps = sem(f"{n}_hidT_ps")
                self.hidTa = sem(f"{n}_hidTa")
                self.hidTb = sem(f"{n}_hidTb")
                self.y_ps = sem(f"{n}_y_ps")
                self.y = sem(f"{n}_y")
                self.y_out = [sem(f"{n}_y_out{s}") for s in range(RING)]
                self.y_in = [sem(f"{n}_y_in{q}") for q in range(4)]
                self.xq = sem(f"{n}_xq")

        S = [FfnSems("f0"), FfnSems("f1")]
        aln = LnSems("ln_a")
        rope_in = sem("rope_in")
        aw_in = sem("aw_in")
        ct_ps = sem("ct_ps")
        ct_done = sem("ct_done")
        rot_ps = sem("rot_ps")
        lin_ps = sem("lin_ps")
        mixed = sem("mixed")
        full_q = sem("full_q")
        part0 = sem("part0")
        rest1 = sem("rest1")
        part1 = sem("part1")
        part2 = sem("part2")
        square = sem("square")
        norms = sem("norms")
        parts_out = [sem(f"parts_out{b}") for b in range(2)]
        v_ps = sem("v_ps")
        v_done = sem("v_done")
        pads = sem("pads")
        nmax_done = sem("nmax_done")
        nmax_T = sem("nmax_T")
        safe_done = sem("safe_done")
        const_rows = sem("const_rows")
        shift_in = [sem(f"shift_in{r}") for r in range(SLOTS)]
        m_head = sem("m_head")
        m_score = sem("m_score")
        m_max = sem("m_max")
        m_T = sem("m_T")
        m_step = sem("m_step")
        m_shift = sem("m_shift")
        m_out = sem("m_out")
        head_in = [sem(f"head_in{r}") for r in range(SLOTS)]
        head_v = sem("head_v")
        score = sem("score")
        exped = sem("exped")
        pv = sem("pv")
        o_copied = sem("o_copied")
        o_T = sem("o_T")
        o_norm = sem("o_norm")
        bias_o = sem("bias_o")
        a_T = sem("a_T")
        a_Tc = sem("a_Tc")
        proj = sem("proj")
        x_attn = sem("x_attn")
        out_done = sem("out_done")
        vcount = [0]

        def chain(dve, inst):
            inst.then_inc(vstep, 1)
            vcount[0] += 1
            dve.wait_ge(vstep, vcount[0])

        def layernorm_vector(dve, s, x_ready):
            for i in range(NT):
                x_ready(i)
                last = nc.vector.bn_stats(stats[:, i, :], X[:, i, :])
            chain(dve, last)
            for i in range(NT):
                last = nc.vector.bn_aggr(mv[:, i, :], stats[:, i, :])
            chain(dve, last)
            chain(dve, nc.vector.tensor_scalar(var[:, :], mv[:, :, 1], LN_EPS, None, ALU.add))
            nc.vector.tensor_copy(newt[:, :], var[:, :]).then_inc(s.var, 1)
            dve.wait_ge(s.sd, 1)
            chain(dve, nc.vector.reciprocal(rstd[:, :], newt[:, :]))
            chain(dve, nc.vector.tensor_tensor(newt[:, :], rstd[:, :], rstd[:, :], ALU.mult))
            chain(dve, nc.vector.tensor_tensor(newt[:, :], newt[:, :], var[:, :], ALU.mult))
            chain(dve, nc.vector.tensor_scalar(newt[:, :], newt[:, :], -0.5, 1.5, ALU.mult, ALU.add))
            chain(dve, nc.vector.tensor_tensor(rstd[:, :], rstd[:, :], newt[:, :], ALU.mult))
            for i in range(NT):
                nc.vector.tensor_scalar(XN[:, i, :], X[:, i, :], mv[:, i, 0:1], rstd[:, i:i + 1],
                                        ALU.subtract, ALU.mult).then_inc(s.xn, 1)

        def layernorm_scalar(act, s):
            act.wait_ge(s.var, 1)
            nc.scalar.activation(newt[:, :], newt[:, :], ACT.Sqrt).then_inc(s.sd, 1)
            for g in range(4):
                act.wait_ge(s.T, g + 1)
                nc.scalar.copy(XNT[:, g * CH:(g + 1) * CH], PS[:, g % 2, :]).then_inc(s.xnT, 1)

        def layernorm_tensor(pe, s):
            for g in range(4):
                if g >= 2:
                    pe.wait_ge(s.xnT, g - 1)
                for k in range(4):
                    pe.wait_ge(s.xn, 4 * g + k + 1)
                    last = nc.tensor.transpose(PS[:, g % 2, k * P:(k + 1) * P], XN[:, 4 * g + k, :], ident)
                last.then_inc(s.T, 1)

        def bc(ap, shape):
            return ap.to_broadcast(shape)

        def route_vector(dve, s):
            dve.wait_ge(s.logits, 1)
            chain(dve, nc.vector.tensor_copy(L[:, :, :], PS[:, 2, 0:NT * E].rearrange("p (i e) -> p i e", e=E)))
            src = L[:, :, :]
            for k in range(K2):
                chain(dve, nc.vector.tensor_reduce(top[:, k, :], src, AX.X, ALU.max))
                chain(dve, nc.vector.tensor_tensor(tmpE[:, k], src, bc(top[:, k, :].unsqueeze(2), [P, NT, E]), ALU.is_equal))
                chain(dve, nc.vector.tensor_tensor(tmpE[:, k], tmpE[:, k], bc(c("emark").unsqueeze(1), [P, NT, E]), ALU.mult))
                chain(dve, nc.vector.tensor_reduce(first[:, k, :], tmpE[:, k], AX.X, ALU.min))
                chain(dve, nc.vector.tensor_tensor(pick[:, k], bc(c("emark").unsqueeze(1), [P, NT, E]),
                                                   bc(first[:, k, :].unsqueeze(2), [P, NT, E]), ALU.is_equal))
                if k == 0:
                    chain(dve, nc.vector.scalar_tensor_tensor(L[:, :, :], pick[:, 0], -3.0e38, L[:, :, :], ALU.mult, ALU.add))
            nc.vector.tensor_tensor(both[:, :, :], pick[:, 0], pick[:, 1], ALU.add).then_inc(s.both, 1)
            nc.vector.tensor_tensor(wts[:, 1, :], top[:, 1, :], top[:, 0, :], ALU.subtract).then_inc(s.top2, 1)
            dve.wait_ge(s.ranks, 1)
            chain(dve, nc.vector.tensor_reduce(tot[:, :], PS[:, 4, 0:NT * E].rearrange("p (i e) -> p e i", e=E), AX.X, ALU.add))
            chain(dve, nc.vector.tensor_tensor(over[:, :, :], bc(tot[:, :].unsqueeze(2), [P, E, NT * K2]),
                                               bc(c("thresh").unsqueeze(1), [P, E, NT * K2]), ALU.is_gt))
            chain(dve, nc.vector.tensor_reduce(ntile[:, :], over[:, :, :], AX.X, ALU.add))
            chain(dve, nc.vector.tensor_tensor(tri_p[:, :, :], c("tri").rearrange("p (a b) -> p a b", b=E),
                                               bc(ntile[:, :].unsqueeze(1), [P, E, E]), ALU.mult))
            chain(dve, nc.vector.tensor_reduce(tbase[:, :], tri_p[:, :, :], AX.X, ALU.add))
            nc.vector.tensor_tensor(tend[:, :], tbase[:, :], ntile[:, :], ALU.add)
            chain(dve, nc.vector.tensor_scalar(tbase[:, :], tbase[:, :], float(P), None, ALU.mult))
            chain(dve, nc.vector.tensor_tensor(slot[:, :, :], PS[:, 3, 0:NT * E].rearrange("p (i e) -> p i e", e=E),
                                               bc(tbase[:, :].unsqueeze(1), [P, NT, E]), ALU.add))
            for k in range(K2):
                last = nc.vector.tensor_tensor(tmpE[:, k], pick[:, k], slot[:, :, :], ALU.mult)
            chain(dve, last)
            chain(dve, nc.vector.tensor_reduce(pos[:, :], tmpE[:, :, :, :].rearrange("p k i e -> p (k i) e"), AX.X, ALU.add))
            chain(dve, nc.vector.tensor_copy(posi[:, 0, :], pos[:, :]))
            nc.vector.tensor_scalar(posi[:, 1, :], posi[:, 0, :], 7, None, ALU.arith_shift_right)
            chain(dve, nc.vector.tensor_scalar(posi[:, 2, :], posi[:, 0, :], P - 1, None, ALU.bitwise_and))
            n = K2 * NT
            chain(dve, nc.vector.tensor_tensor(OA[:, :, 0:SLOT_TILES], bc(posi[:, 1, :].unsqueeze(2), [P, n, SLOT_TILES]),
                                               bc(c("jramp").unsqueeze(1), [P, n, SLOT_TILES]), ALU.is_equal))
            chain(dve, nc.vector.tensor_tensor(OA[:, :, SLOT_TILES:], OA[:, :, 0:SLOT_TILES],
                                               bc(c("kmark").unsqueeze(2), [P, n, SLOT_TILES]), ALU.mult))
            chain(dve, nc.vector.tensor_tensor(OA[:, :, 0:SLOT_TILES], OA[:, :, 0:SLOT_TILES],
                                               bc(c("token").unsqueeze(2), [P, n, SLOT_TILES]), ALU.mult))
            for g in range(4):
                a, b = g * n // 4, (g + 1) * n // 4
                nc.vector.tensor_tensor(OB[:, a:b, :], bc(posi[:, 2, a:b].unsqueeze(2), [P, n // 4, P]),
                                        bc(iota_h[:, :].unsqueeze(1), [P, n // 4, P]), ALU.is_equal).then_inc(s.onehot, 1)
            chain(dve, nc.vector.tensor_tensor(passed[:, :, :], bc(tend[:, :].unsqueeze(1), [P, SLOT_TILES, E]),
                                               bc(c("jramp").unsqueeze(2), [P, SLOT_TILES, E]), ALU.is_le))
            chain(dve, nc.vector.tensor_reduce(texp[:, :], passed[:, :, :], AX.X, ALU.add))
            nc.vector.tensor_scalar(woff[:, 0, :], texp[:, :], float(E - 1), float(2 * F), ALU.min, ALU.mult)
            nc.vector.tensor_scalar(woff[:, 1, :], texp[:, :], float(E - 1), float(3 * D), ALU.min, ALU.mult).then_inc(s.woff, 1)
            dve.wait_ge(s.slots, 1)
            chain(dve, nc.vector.tensor_copy(idx[:, 0, :], PS[:, 5, 0:SLOT_TILES]))
            nc.vector.scalar_tensor_tensor(idx[:, 1, :], PS[:, 5, SLOT_TILES:2 * SLOT_TILES], float(NO_ROW), idx[:, 0, :],
                                           ALU.add, ALU.add).then_inc(s.idx, 1)
            dve.wait_ge(s.exp2, 1)
            chain(dve, nc.vector.tensor_scalar(wts[:, 0, :], wts[:, 1, :], 1.0, None, ALU.add))
            chain(dve, nc.vector.reciprocal(wts[:, 0, :], wts[:, 0, :]))
            chain(dve, nc.vector.tensor_scalar(wts[:, 0, :], wts[:, 0, :], 0.5, None, ALU.mult))
            chain(dve, nc.vector.tensor_tensor(wts[:, 1, :], wts[:, 1, :], wts[:, 0, :], ALU.mult))

        def route_scalar(act, s):
            act.wait_ge(s.top2, 1)
            nc.scalar.activation(wts[:, 1, :], wts[:, 1, :], ACT.Exp).then_inc(s.exp2, 1)

        def route_tensor(pe, s):
            for i in range(NT):
                if i % 4 == 0:
                    pe.wait_ge(s.ln.xnT, i // 4 + 1)
                last = nc.tensor.matmul(PS[:, 2, i * E:(i + 1) * E], XNT[:, i * P:(i + 1) * P], Wr[:, :], start=True, stop=True)
            last.then_inc(s.logits, 1)
            pe.wait_ge(s.both, 1)
            m = both[:, :, :].rearrange("p i e -> p (i e)")
            nc.tensor.matmul(PS[:, 4, 0:NT * E], ones_b[:, :], m, start=True, stop=True)
            nc.tensor.matmul(PS[:, 3, 0:NT * E], lower_b[:, :], m, start=True, stop=False)
            for d in range(1, NT):
                last = nc.tensor.matmul(PS[:, 3, d * E:NT * E], ones_b[:, :], m[:, 0:(NT - d) * E], start=False, stop=(d == NT - 1))
            last.then_inc(s.ranks, 1)
            n = K2 * NT
            for q in range(n):
                if q % (n // 4) == 0:
                    pe.wait_ge(s.onehot, q // (n // 4) + 1)
                last = nc.tensor.matmul(PS[:, 5, 0:2 * SLOT_TILES], OB[:, q, :], OA[:, q, :], start=(q == 0), stop=(q == n - 1))
            last.then_inc(s.slots, 1)

        def load_offsets(pe, s, j):
            one = [nc.values_load(woff[0:1, w, j:j + 1] if isinstance(j, int) else woff[0:1, w, bass.ds(j, 1)],
                                  engines=[mybir.EngineType.PE], min_val=0, max_val=(E - 1) * n,
                                  skip_runtime_bounds_check_because="the offset was clamped to the last expert's")
                   for w, n in ((0, 2 * F), (1, 3 * D))]
            return one

        def tile_transpose_x(pe, s, j, r):
            pe.wait_ge(s.xg[r % RING], (j - r % RING) * (16 // RING) + 16)
            if not (isinstance(j, int) and j == 0):
                pe.wait_ge(s.xgT, j)
            nc.tensor.transpose(PS[:, 0, 0:P], xg[:, r % RING, :], ident).then_inc(s.xgT_ps, 1)

        def tile_gate_up(pe, s, j, r):
            off = load_offsets(pe, s, j)[0]
            w = Wgu[:, :, :].rearrange("p e n -> p (e n)")
            pe.wait_ge(s.xgT, j + 1)
            if not (isinstance(j, int) and j == 0):
                pe.wait_ge(s.hid, j)
            nc.tensor.matmul(PS[:, 1, 0:F], xgT[:, r % 2, :], w[:, bass.ds(off, F)], start=True, stop=True).then_inc(s.gate, 1)
            nc.tensor.matmul(PS[:, 2, 0:F], xgT[:, r % 2, :], w[:, bass.ds(off + F, F)], start=True, stop=True).then_inc(s.up, 1)

        def tile_transpose_h(pe, s, j, r):
            pe.wait_ge(s.hid, j + 1)
            if not (isinstance(j, int) and j == 0):
                pe.wait_ge(s.hidTa, j)
                pe.wait_ge(s.hidTb, j)
            for n, (a, w) in enumerate(FCH):
                last = nc.tensor.transpose(PS[0:w, 3 + n // 2 * 3, n % 2 * P:(n % 2 + 1) * P], hid[:, r % 2, a:a + w], ident)
            last.then_inc(s.hidT_ps, 1)

        def tile_down(pe, s, j, r):
            off = load_offsets(pe, s, j)[1]
            wd = Wd[:, :, :, :].rearrange("p e n d -> p (e n d)")
            pe.wait_ge(s.hidTa, j + 1)
            pe.wait_ge(s.hidTb, j + 1)
            if not (isinstance(j, int) and j == 0):
                pe.wait_ge(s.y, j)
            for n, (a, w) in enumerate(FCH):
                last = nc.tensor.matmul(PS[:, 4, 0:D], hidT[0:w, r % 2, n, :], wd[0:w, bass.ds(off + n * D, D)],
                                        start=(n == 0), stop=(n == 2))
            last.then_inc(s.y_ps, 1)

        def experts_tensor(pe, s):
            pe.wait_ge(s.woff, 1)
            tile_transpose_x(pe, s, 0, 0)
            pe.wait_ge(wexp_in, 5 * 16)
            tile_gate_up(pe, s, 0, 0)
            tile_transpose_x(pe, s, 1, 1)

            def tile(j, r, more=2):
                tile_transpose_h(pe, s, j, r)
                if more >= 1:
                    tile_gate_up(pe, s, j + 1, r + 1)
                if more >= 2:
                    tile_transpose_x(pe, s, j + 2, r + 2)
                tile_down(pe, s, j, r)

            with pe.Fori(0, SLOT_TILES // RING - 1) as n:
                for r in range(RING):
                    tile(n * RING + r, r)
            for r in range(RING):
                tile(SLOT_TILES - RING + r, r, more=min(2, RING - 1 - r))

        def experts_scalar(act, s):
            def copy_x(j, r):
                act.wait_ge(s.xgT_ps, j + 1)
                if not (isinstance(j, int) and j < 2):
                    act.wait_ge(s.up, j - 1)
                nc.scalar.copy(xgT[:, r % 2, :], PS[:, 0, 0:P]).then_inc(s.xgT, 1)

            def silu(j, r):
                act.wait_ge(s.gate, j + 1)
                if not (isinstance(j, int) and j < 2):
                    act.wait_ge(s.hid, j - 1)
                nc.scalar.activation(sg[:, r % 2, :], PS[:, 1, 0:F], ACT.Silu).then_inc(s.silu, 1)

            def tile(j, r, more=2):
                act.wait_ge(s.hidT_ps, j + 1)
                if not (isinstance(j, int) and j < 2):
                    act.wait_ge(s.y_ps, j - 1)
                nc.scalar.copy(hidT[0:96, r % 2, 2, :], PS[0:96, 6, 0:P]).then_inc(s.hidTb, 1)
                if more >= 1:
                    silu(j + 1, r + 1)
                if more >= 2:
                    copy_x(j + 2, r + 2)
                act.wait_ge(s.y_ps, j + 1)
                if not (isinstance(j, int) and j < RING):
                    act.wait_ge(s.y_out[r % RING], (j - r) * (16 // RING))
                nc.scalar.copy(yt[:, r % RING, :], PS[:, 4, 0:D]).then_inc(s.y, 1)

            copy_x(0, 0)
            silu(0, 0)
            copy_x(1, 1)
            for r in range(RING):
                tile(r, r)
            with act.Fori(1, SLOT_TILES // RING - 1) as n:
                for r in range(RING):
                    tile(n * RING + r, r)
            for r in range(RING):
                tile(SLOT_TILES - RING + r, r, more=min(2, RING - 1 - r))

        def experts_vector(dve, s):
            def mult(j, r):
                dve.wait_ge(s.up, j + 1)
                dve.wait_ge(s.silu, j + 1)
                if not (isinstance(j, int) and j < 2):
                    dve.wait_ge(s.hidT_ps, j - 1)
                nc.vector.tensor_tensor(hid[:, r % 2, :], PS[:, 2, 0:F], sg[:, r % 2, :], ALU.mult).then_inc(s.hid, 1)

            def tile(j, r, more=1):
                dve.wait_ge(s.hidT_ps, j + 1)
                if not (isinstance(j, int) and j < 2):
                    dve.wait_ge(s.y_ps, j - 1)
                nc.vector.tensor_copy(hidT[:, r % 2, 0:2, :], PS[:, 3, 0:2 * P].rearrange("p (n t) -> p n t", n=2)).then_inc(s.hidTa, 1)
                if more:
                    mult(j + 1, r + 1)

            mult(0, 0)
            tile(0, 0)
            tile(1, 1)
            with dve.Fori(1, SLOT_TILES // 2 - 1) as n:
                for r in range(2):
                    tile(n * 2 + r, r)
            tile(SLOT_TILES - 2, 0)
            tile(SLOT_TILES - 1, 1, more=0)

        def experts_gpsimd(pool, s, f):
            def gather(j):
                if j >= RING:
                    pool.wait_ge(s.xgT_ps, j - RING + 1)
                nc.gpsimd.indirect_dma_start(xg[:, j % RING, :], None, xn_dram[f], bass.IndirectOffsetOnAxis(idx[:, 0, j:j + 1], 0)
                                             ).then_inc(s.xg[j % RING], 16)

            def scatter(j):
                pool.wait_ge(s.y, j + 1)
                nc.gpsimd.indirect_dma_start(y_dram[f], bass.IndirectOffsetOnAxis(idx[:, 1, j:j + 1], 0), yt[:, j % RING, :], None,
                                             bounds_check=NO_ROW - 1, oob_is_err=False).then_inc(s.y_out[j % RING], 16)

            pool.wait_ge(s.idx, 1)
            pool.wait_ge(s.xn_out, 16)
            for j in range(RING):
                gather(j)
            for j in range(SLOT_TILES):
                if j + RING < SLOT_TILES:
                    gather(j + RING)
                scatter(j)

        def ffn_sync(sp, s, f):
            sp.wait_ge(s.ln.xn, NT)
            sp.dma_start(xn_dram[f].rearrange("(p i) d -> p i d", i=NT), XN[:, :, :]).then_inc(s.xn_out, 16)
            for r in range(RING):
                sp.wait_ge(s.y_out[r], 16 * SLOT_TILES // RING)
            yv = y_dram[f].rearrange("(k p i) d -> p k i d", k=K2, i=NT)
            for q in range(4):
                for k in range(K2):
                    sp.dma_start(Y[:, k, 4 * q:4 * q + 4, :], yv[:, 1 - k, 4 * q:4 * q + 4, :]).then_inc(s.y_in[q], 16)

        def combine_vector(dve, s):
            for q in range(4):
                dve.wait_ge(s.y_in[q], 32)
                for i in range(4 * q, 4 * q + 4):
                    last = nc.vector.scalar_tensor_tensor(X[:, i, :], Y[:, 0, i, :], wts[:, 0, i:i + 1], X[:, i, :], ALU.mult, ALU.add)
                chain(dve, last)
                for i in range(4 * q, 4 * q + 4):
                    last = nc.vector.scalar_tensor_tensor(X[:, i, :], Y[:, 1, i, :], wts[:, 1, i:i + 1], X[:, i, :], ALU.mult, ALU.add)
                last.then_inc(s.xq, 1)

        UNITS = 2 * NC
        T1, T2, FULL, REST, SQ = range(5)

        def prepare_tensor(pe):
            def mm(bank, w, rhs):
                return nc.tensor.matmul(PS[:, bank, :], aw[:, AW[w], :], rhs, start=True, stop=True)

            def norm(u):
                c_, half = u // 2, u % 2
                pe.wait_ge(square, u + 1)
                hs = c("hsum")[:, 32 * half:32 * half + 32]
                nc.tensor.matmul(PS[32 * c_:32 * c_ + 32, 1, :], hs, temp[:, SQ, u % 2, :],
                                 start=(half == 0), stop=(half == 1)).then_inc(norms, 1)

            pe.wait_ge(aw_in, 64)
            pe.wait_ge(aln.xnT, NC)
            for c_ in range(NC):
                cols = slice(c_ * CH, (c_ + 1) * CH)
                if c_ >= 1:
                    pe.wait_ge(ct_done, c_)
                mm(2, "ct", XNT[:, cols]).then_inc(ct_ps, 1)
                if c_ >= 1:
                    pe.wait_ge(mixed, 2 * c_ - 1)
                mm(3, "kr", XNT[:, cols])
                mm(4, "krs", XNT[:, cols]).then_inc(rot_ps, 1)
                pe.wait_ge(ct_done, c_ + 1)
                mm(5, "uk", ct[:, cols]).then_inc(lin_ps, 1)
                if c_ >= 1:
                    pe.wait_ge(mixed, 2 * c_)
                mm(6, "qr", ct[:, cols])
                mm(7, "qrs", ct[:, cols]).then_inc(rot_ps, 1)
                mm(0, "uq", ct[:, cols]).then_inc(lin_ps, 1)
                if c_ >= 1:
                    norm(2 * c_ - 2)
                    norm(2 * c_ - 1)
            pe.wait_ge(mixed, UNITS - 1)
            for g in range(4):
                if g >= 2:
                    pe.wait_ge(v_done, g - 1)
                for i in range(4 * g, 4 * g + 4):
                    last = nc.tensor.matmul(PS[:, 2 + g % 2, (i % 4) * P:(i % 4 + 1) * P], ct[:, i * P:(i + 1) * P], aw[:, AW["uv"], :],
                                            start=True, stop=True)
                last.then_inc(v_ps, 1)
            norm(UNITS - 2)
            norm(UNITS - 1)
            pe.wait_ge(nmax_done, 1)
            pe.wait_ge(v_done, 4)
            nc.tensor.transpose(PS[0:1, 2, 0:P], nmax[:, :], ident).then_inc(nmax_T, 1)

        def prepare_scalar(act):
            act.wait_ge(aw_in, 64)

            def compressed(c_):
                act.wait_ge(ct_ps, c_ + 1)
                nc.scalar.activation(ct[:, c_ * CH:(c_ + 1) * CH], PS[:, 2, :], ACT.Identity, bias=ab[:, AB["ct"]:AB["ct"] + 1]).then_inc(ct_done, 1)

            compressed(0)
            for u in range(UNITS):
                if u % 2 == 1 and u // 2 + 1 < NC:
                    compressed(u // 2 + 1)
                act.wait_ge(full_q, u + 1)
                if u >= 2:
                    act.wait_ge(parts_out[u % 2], 16 * (u // 2))
                nc.scalar.copy(parts[:, u % 2, 0, :], temp[:, FULL, u % 2, :]).then_inc(part0, 1)
                if u >= 2:
                    act.wait_ge(norms, u - 1)
                nc.scalar.activation(temp[:, SQ, u % 2, :], temp[:, FULL, u % 2, :], ACT.Square).then_inc(square, 1)
                act.wait_ge(rest1, u + 1)
                nc.scalar.copy(parts[:, u % 2, 1, :], temp[:, REST, u % 2, :]).then_inc(part1, 1)

        def prepare_vector(dve):
            dve.wait_ge(aw_in, 64)
            dve.wait_ge(rope_in, 32)

            def third(u):
                dve.wait_ge(part1, u + 1)
                nc.vector.tensor_tensor(parts[:, u % 2, 2, :], temp[:, REST, u % 2, :], parts[:, u % 2, 1, :], ALU.subtract).then_inc(part2, 1)

            for u in range(UNITS):
                c_, b = u // 2, u % 2
                cols = slice(c_ * CH, (c_ + 1) * CH)
                rot, rots, lin = ((3, 4, 5), (6, 7, 0))[b]
                names = (("kr", "krs", "uk"), ("qr", "qrs", "uq"))[b]
                bias = [ab[:, AB[n]:AB[n] + 1] for n in names]
                dve.wait_ge(rot_ps, u + 1)
                if u >= 2:
                    dve.wait_ge(full_q, u - 1)
                chain(dve, nc.vector.scalar_tensor_tensor(temp[:, T1, b, :], PS[:, rot, :], bias[0], cosT[:, cols], ALU.add, ALU.mult))
                nc.vector.scalar_tensor_tensor(temp[:, T2, b, :], PS[:, rots, :], bias[1], sinT[:, cols], ALU.add, ALU.mult)
                dve.wait_ge(lin_ps, u + 1)
                nc.vector.scalar_tensor_tensor(temp[:, T1, b, :], PS[:, lin, :], bias[2], temp[:, T1, b, :], ALU.add, ALU.add).then_inc(mixed, 1)
                if u >= 1:
                    third(u - 1)
            third(UNITS - 1)
            for g in range(4):
                dve.wait_ge(v_ps, g + 1)
                nc.vector.tensor_tensor(V[:, 4 * g:4 * g + 4, :], PS[:, 2 + g % 2, :].rearrange("p (i d) -> p i d", d=D),
                                        bc(bv_rows[:, :].unsqueeze(1), [P, 4, D]), ALU.add).then_inc(v_done, 1)
            dve.wait_ge(norms, UNITS)
            nc.vector.tensor_reduce(nmax[:, :], PS[:, 1, :], AX.X, ALU.max).then_inc(nmax_done, 1)
            dve.wait_ge(nmax_T, 1)
            chain(dve, nc.vector.tensor_reduce(nrow[:, :], PS[0:1, 2, 0:P].rearrange("p (c m) -> p m c", m=2 * H), AX.X, ALU.max))
            chain(dve, nc.vector.tensor_tensor(bound[:, :], nrow[:, 0:H], nrow[:, H:], ALU.mult))
            chain(dve, nc.vector.tensor_reduce(largest[:, :], bound[:, :], AX.X, ALU.max))
            nc.vector.tensor_scalar(safe[:, :], largest[:, :], (SCORE_SAFE / SCORE_SCALE) ** 2, None, ALU.is_le).then_inc(safe_done, 1)

        def pads_gpsimd(pool):
            nc.gpsimd.memset(vslot[:, :, :, :], 0.0).then_inc(pads, 1)
            nc.gpsimd.memset(zeros48[:, :].bitcast(F32), 0.0).then_inc(pads, 1)
            pool.wait_ge(pads, 2)
            nc.gpsimd.memset(qslot[64:P, :, :].bitcast(F32), 0.0)
            nc.gpsimd.memset(kslot[64:P, :, :].bitcast(F32), 0.0).then_inc(pads, 1)
            pool.wait_ge(pads, 3)
            nc.gpsimd.memset(vslot[:, :, :, HD:HD + 1], 1.0).then_inc(pads, 1)

        def prepare_gpsimd(pool):
            for u in range(UNITS):
                b = u % 2
                pool.wait_ge(mixed, u + 1)
                if u >= 2:
                    pool.wait_ge(square, u - 1)
                nc.gpsimd.tensor_tensor(temp[:, FULL, b, :], temp[:, T1, b, :], temp[:, T2, b, :], ALU.add).then_inc(full_q, 1)
                pool.wait_ge(part0, u + 1)
                if u >= 2:
                    pool.wait_ge(part2, u - 1)
                nc.gpsimd.tensor_tensor(temp[:, REST, b, :], temp[:, FULL, b, :], parts[:, b, 0, :], ALU.subtract).then_inc(rest1, 1)

        def load_head(sp, h, r, done):
            rows = slice(HD * h, HD * h + HD) if isinstance(h, int) else bass.ds(h * HD, HD)
            for i in range(PARTS):
                for j in range(PARTS):
                    to = slice(24 * i + 8 * j, 24 * i + 8 * j + 8)
                    sp.dma_start(kslot[to, r, :], qk_dram[0][j, rows, :]).then_inc(done, 16)
                    sp.dma_start(qslot[to, r, :], qk_dram[1][i, rows, :]).then_inc(done, 16)

        def load_shift(sp, h, r):
            src = shift_dram[:, h, :] if isinstance(h, int) else shift_dram[:, bass.ds(h, 1), :].rearrange("a h n -> a (h n)")
            sp.dma_start(qslot[SHIFT_ROW:SHIFT_ROW + PARTS, r, :], src).then_inc(shift_in[r], 16)

        HEAD_DMAS = 2 * PARTS * PARTS

        def unbounded(engine_type, eng, ready):
            eng.wait_ge(ready, 1)
            flag = nc.values_load(safe[0:1, 0:1], engines=[engine_type], min_val=0, max_val=1,
                                  skip_runtime_bounds_check_because="a comparison's result")
            return eng.If(flag == 0)

        MAX_SLOT = SLOTS - 1

        def maxima_sync(sp):
            with sp.Fori(0, H) as h:
                sp.wait_ge(m_max, h * NT + 1)
                load_head(sp, h, MAX_SLOT, m_head)
            sp.wait_ge(m_shift, 1)
            sp.dma_start(shift_dram.rearrange("a (b g) (i q) -> (g i) a b q", b=2, q=P), sparts[:, :, :, :]).then_inc(m_out, 16)
            sp.wait_ge(m_out, 16)

        def maxima_tensor(pe):
            with pe.Fori(0, H) as h:
                pe.wait_ge(m_head, (h + 1) * (16 * HEAD_DMAS))
                for i in range(NT):
                    pe.wait_ge(m_max, h * NT + i if i >= 1 else h * NT + 1)
                    for k in range(NC):
                        last = nc.tensor.matmul(PS[:, 4 * (i % 2) + k, :], qslot[0:KR, MAX_SLOT, i * P:(i + 1) * P],
                                                kslot[0:KR, MAX_SLOT, k * CH:(k + 1) * CH], start=True, stop=True)
                    last.then_inc(m_score, 1)
            pe.wait_ge(m_max, H * NT + 1)
            for b in range(2):
                last = nc.tensor.transpose(PS[:, 0, b * P:(b + 1) * P], smax[:, b, :], ident)
            last.then_inc(m_T, 1)
            pe.wait_ge(m_shift, 1)

        def maxima_vector(dve):
            nc.vector.memset(snext[:, :, :], 0.0).then_inc(m_max, 1)
            flat = smax[:, :, :].rearrange("p b n -> p (b n)")
            with dve.Fori(0, H) as h:
                for i in range(NT):
                    b = 4 * (i % 2)
                    dve.wait_ge(m_score, h * NT + (i + 1))
                    nc.vector.tensor_reduce(flat[:, bass.ds(h * NT + i, 1)], PS[:, b:b + 4, :], AX.XY, ALU.max).then_inc(m_max, 1)
            dve.wait_ge(m_T, 1)
            nc.vector.tensor_scalar(snext[:, :, :], PS[:, 0, 0:2 * P].rearrange("p (b n) -> p b n", b=2), -1.0, None, ALU.mult).then_inc(m_step, 1)
            for a in range(PARTS):
                dve.wait_ge(m_step, 2 * a + 1)
                nc.vector.tensor_copy(sparts[:, a, :, :], snext[:, :, :]).then_inc(m_step, 1)
                dve.wait_ge(m_step, 2 * a + 2)
                nc.vector.tensor_tensor(snext[:, :, :], snext[:, :, :], sparts[:, a, :, :], ALU.subtract).then_inc(m_step, 1)
            dve.wait_ge(m_step, 2 * PARTS + 1)
            nc.vector.tensor_copy(nmax[:, :], nmax[:, :]).then_inc(m_shift, 1)

        def attention_sync(sp):
            sp.wait_ge(pads, 3)
            sp.wait_ge(consts_cast, 1)
            for r in range(SLOTS):
                sp.dma_start(kslot[SHIFT_ROW:SHIFT_ROW + PARTS, r, :].rearrange("a (i n) -> a i n", n=P),
                             ones_b[0:PARTS, :].unsqueeze(1).to_broadcast([PARTS, NT, P])).then_inc(const_rows, 16)
            sp.dma_start(shift_dram.rearrange("a h n -> (a h) n"), zeros48[:, :]).then_inc(const_rows, 16)
            for u in range(UNITS):
                c_, b = u // 2, u % 2
                sp.wait_ge(part2, u + 1)
                sp.dma_start(qk_dram[b][:, :, c_ * CH:(c_ + 1) * CH].rearrange("a p n -> p a n"), parts[:, b, :, :]).then_inc(parts_out[b], 16)
            sp.wait_ge(parts_out[0], 16 * NC)
            sp.wait_ge(parts_out[1], 16 * NC)
            sp.wait_ge(const_rows, 16 * (SLOTS + 1))
            for h in range(SLOTS - 1):
                load_head(sp, h, h, head_in[h])
            with unbounded(mybir.EngineType.SP, sp, safe_done):
                maxima_sync(sp)
            for h in range(SLOTS - 1):
                load_shift(sp, h, h)
            load_head(sp, SLOTS - 1, SLOTS - 1, head_in[SLOTS - 1])
            load_shift(sp, SLOTS - 1, SLOTS - 1)
            with sp.Fori(1, H // SLOTS) as n:
                for r in range(SLOTS):
                    sp.wait_ge(score, (n * SLOTS + (r - SLOTS + 1)) * 32)
                    load_head(sp, n * SLOTS + r, r, head_in[r])
                    load_shift(sp, n * SLOTS + r, r)
            sp.wait_ge(score, (H - SLOTS) * 32)
            load_head(sp, H - 1, 0, head_in[0])
            load_shift(sp, H - 1, 0)

        BODY = SLOTS * NT

        def attention_tensor(pe):
            def scores(u0, v, half):
                h, kt, r = v // NT, v % NT, (v // NT) % SLOTS
                g = 2 * v + half
                fixed = isinstance(u0, int)
                if kt == 0 and half == 0:
                    count = (u0 // BODY + v // BODY + 1) if fixed else (u0 + 1 + v // BODY)
                    pe.wait_ge(head_in[r], count * (16 * HEAD_DMAS))
                    pe.wait_ge(shift_in[r], count * 16)
                G = (2 * u0 if fixed else u0 * (2 * BODY)) + g
                if not (fixed and G < GB):
                    pe.wait_ge(exped, G - GB + 1)
                for k in range(2):
                    last = nc.tensor.matmul(PS[:, 2 * (g % GB) + k, :], kslot[0:KR, r, kt * P:(kt + 1) * P],
                                            qslot[0:KR, r, (2 * half + k) * CH:(2 * half + k + 1) * CH], start=True, stop=True)
                last.then_inc(score, 1)

            def values(u0, v):
                fixed = isinstance(u0, int)
                kt = v % NT
                r = (v // NT) % SLOTS
                U = (u0 if fixed else u0 * BODY) + v
                if kt == 0:
                    hh = (u0 // NT if fixed else u0 * SLOTS) + v // NT
                    pe.wait_ge(head_v, hh + 1)
                    if not (fixed and hh == 0):
                        pe.wait_ge(o_copied, hh)
                pe.wait_ge(exped, U * 2 + 2)
                for q in range(NC):
                    last = nc.tensor.matmul(PS[32 * q:32 * q + 32, 6, :], vslot[:, r, kt, :], EXP[:, v % SLOTS, q * CH:(q + 1) * CH],
                                            start=(kt == 0), stop=(kt == NT - 1))
                last.then_inc(pv, 1)

            def transpose_out(u0, v):
                fixed = isinstance(u0, int)
                hh = (u0 // NT if fixed else u0 * SLOTS) + v // NT
                pe.wait_ge(o_copied, hh + 1)
                if not (fixed and hh == 0):
                    pe.wait_ge(o_norm, hh)
                for k in range(4):
                    last = nc.tensor.transpose(PS[:, 7, k * P:(k + 1) * P], Osb[:, k * P:(k + 1) * P], ident)
                last.then_inc(o_T, 1)

            def step(u0, v, left=2):
                if left >= 1:
                    scores(u0, v + 1, 1)
                if not (isinstance(u0, int) and u0 + v == 0):
                    values(u0, v - 1)
                if v % NT == 3 and not (isinstance(u0, int) and u0 + v < NT):
                    transpose_out(u0, v - NT)
                if left >= 2:
                    scores(u0, v + 2, 0)

            pe.wait_ge(v_done, 4)
            pe.wait_ge(pads, 4)
            pe.wait_ge(const_rows, 16 * (SLOTS + 1))
            with unbounded(mybir.EngineType.PE, pe, safe_done):
                maxima_tensor(pe)
            scores(0, 0, 0)
            scores(0, 0, 1)
            scores(0, 1, 0)
            for v in range(BODY):
                step(0, v)
            with pe.Fori(1, H // SLOTS) as n:
                for v in range(BODY):
                    step(n, v)
            last = (H // SLOTS) * BODY
            for v in range(NT):
                step(last, v, left=NT - 1 - v)
            values(last, NT - 1)
            transpose_out(last, 0)

        def attention_scalar(act):
            def exps(u0, v):
                fixed = isinstance(u0, int)
                U = (u0 if fixed else u0 * BODY) + v
                for half in range(2):
                    g = 2 * v + half
                    act.wait_ge(score, U * 2 + (half + 1))
                    if half == 0 and not (fixed and U < SLOTS):
                        act.wait_ge(pv, U - SLOTS + 1)
                    b = 2 * (g % GB)
                    nc.scalar.activation(EXP[:, v % SLOTS, half * 2 * CH:(half + 1) * 2 * CH].rearrange("p (b n) -> p b n", b=2),
                                         PS[:, b:b + 2, :], ACT.Exp, scale=SCORE_SCALE).then_inc(exped, 1)

            for v in range(BODY):
                exps(0, v)
            with act.Fori(1, H // SLOTS) as n:
                for v in range(BODY):
                    exps(n, v)
            for v in range(NT):
                exps((H // SLOTS) * BODY, v)

        def attention_vector(dve):
            def head_values(h, r):
                if not (isinstance(h, int) and h < SLOTS):
                    dve.wait_ge(pv, (h - SLOTS + 1) * NT)
                cols = slice(HD * h, HD * h + HD) if isinstance(h, int) else bass.ds(h * HD, HD)
                nc.vector.tensor_copy(vslot[:, r, :, 0:HD], V[:, :, cols]).then_inc(head_v, 1)

            def finish(h):
                dve.wait_ge(pv, (h + 1) * NT)
                if not (isinstance(h, int) and h == 0):
                    dve.wait_ge(o_T, h)
                nc.vector.tensor_copy(Osb[:, :], PS[:, 6, :]).then_inc(o_copied, 1)

            def divide(h):
                cols = slice(HD * h, HD * h + HD) if isinstance(h, int) else bass.ds(h * HD, HD)
                t = PS[:, 7, :].rearrange("p (s c m) -> p s c m", s=4, m=32)
                dve.wait_ge(o_T, h + 1)
                nc.vector.reciprocal(denom[:, :, :], t[:, :, :, HD]).then_inc(denom_done, 1)
                dve.wait_ge(denom_done, h + 1)
                nc.vector.tensor_tensor(A[:, :, cols].rearrange("p (c s) d -> p s c d", s=4), t[:, :, :, 0:HD],
                                        bc(denom[:, :, :].unsqueeze(3), [P, 4, 4, HD]), ALU.mult).then_inc(o_norm, 1)

            dve.wait_ge(v_done, 4)
            dve.wait_ge(pads, 4)
            for h in range(SLOTS):
                head_values(h, h)
            with unbounded(mybir.EngineType.DVE, dve, safe_done):
                maxima_vector(dve)
            for r in range(SLOTS):
                finish(r)
                divide(r)
                head_values(SLOTS + r, r)
            with dve.Fori(1, H // SLOTS - 1) as n:
                for r in range(SLOTS):
                    finish(n * SLOTS + r)
                    divide(n * SLOTS + r)
                    head_values((n + 1) * SLOTS + r, r)
            for h in range(H - SLOTS - 1, H):
                finish(h)
                divide(h)
                if h == H - SLOTS - 1:
                    head_values(H - 1, 0)

        def project_tensor(pe):
            pe.wait_ge(o_norm, H)
            pe.wait_ge(exped, 2 * H * NT)
            for g in range(4):
                if g >= 2:
                    pe.wait_ge(a_Tc, g - 1)
                for k in range(4):
                    last = nc.tensor.transpose(PS[:, g % 2, k * P:(k + 1) * P], A[:, 4 * g + k, :], ident)
                last.then_inc(a_T, 1)
                if g >= 1:
                    project(pe, g - 1)
            project(pe, 3)

        def project(pe, g):
            pe.wait_ge(a_Tc, g + 1)
            if g >= 2:
                pe.wait_ge(x_attn, g - 1)
            for k in range(4):
                i = 4 * g + k
                last = nc.tensor.matmul(PS[:, 2 + g % 2, k * P:(k + 1) * P], AT[:, i * P:(i + 1) * P], aw[:, AW["wo"], :], start=True, stop=True)
            last.then_inc(proj, 1)

        def project_scalar(act):
            for g in range(4):
                act.wait_ge(a_T, g + 1)
                nc.scalar.copy(AT[:, g * CH:(g + 1) * CH], PS[:, g % 2, :]).then_inc(a_Tc, 1)

        def project_vector(dve):
            dve.wait_ge(bias_o, 1)
            for g in range(4):
                dve.wait_ge(proj, g + 1)
                nc.vector.tensor_tensor(X[:, 4 * g:4 * g + 4, :], PS[:, 2 + g % 2, :].rearrange("p (i d) -> p i d", d=D),
                                        X[:, 4 * g:4 * g + 4, :], ALU.add).then_inc(x_attn, 1)

        x_rows = ins["L0_attn_x"][0].rearrange("(p i) d -> p i d", i=NT)
        out_rows = out[0].rearrange("(p i) d -> p i d", i=NT)

        block = ctx.enter_context(nc.Block())

        @block.sync
        def _(sp):
            for q in range(4):
                sp.dma_start(X[:, 4 * q:4 * q + 4, :], x_rows[:, 4 * q:4 * q + 4, :]).then_inc(x_in[q], 16)
            sp.dma_start(cst[:, :], const).then_inc(const_in, 16)
            sp.dma_start(Wr[:, :], ins["L0_ffn_Wr"]).then_inc(wr_in, 16)
            sp.dma_start(Wgu[:, :, 0:F], ins["L0_ffn_Wg"].rearrange("e h i -> h e i")).then_inc(wexp_in, 16)
            sp.dma_start(Wgu[:, :, F:], ins["L0_ffn_Wu"].rearrange("e h i -> h e i")).then_inc(wexp_in, 16)
            for n, (a, w) in enumerate(FCH):
                sp.dma_start(Wd[0:w, :, n, :], ins["L0_ffn_Wd"][:, a:a + w, :].rearrange("e p d -> p e d")).then_inc(wexp_in, 16)
            ffn_sync(sp, S[0], 0)
            attention_sync(sp)
            ffn_sync(sp, S[1], 1)
            for q in range(4):
                sp.wait_ge(S[1].xq, q + 1)
                sp.dma_start(out_rows[:, 4 * q:4 * q + 4, :], X[:, 4 * q:4 * q + 4, :]).then_inc(out_done, 16)
            sp.wait_ge(out_done, 64)

        @block.vector
        def _(dve):
            layernorm_vector(dve, S[0].ln, lambda i: dve.wait_ge(x_in[i // 4], 16) if i % 4 == 0 else None)
            dve.wait_ge(const_in, 16)
            nc.vector.tensor_copy(lower_b[:, :], c("lower"))
            nc.vector.tensor_copy(ones_b[:, :], c("ones")).then_inc(consts_cast, 1)
            chain(dve, nc.vector.tensor_copy(iota_h[:, :], c("iota")))
            route_vector(dve, S[0])
            experts_vector(dve, S[0])
            combine_vector(dve, S[0])
            layernorm_vector(dve, aln, lambda i: dve.wait_ge(S[0].xq, i // 4 + 1) if i % 4 == 0 else None)
            prepare_vector(dve)
            attention_vector(dve)
            project_vector(dve)
            layernorm_vector(dve, S[1].ln, lambda i: dve.wait_ge(x_attn, i // 4 + 1) if i % 4 == 0 else None)
            route_vector(dve, S[1])
            experts_vector(dve, S[1])
            combine_vector(dve, S[1])

        @block.scalar
        def _(act):
            act.dma_start(cosT[:, :], rope_cos).then_inc(rope_in, 16)
            act.dma_start(sinT[:, :], rope_sin).then_inc(rope_in, 16)
            act.dma_start(aw[:, :, :], attn_w).then_inc(aw_in, 16)
            act.dma_start(ab[:, :], attn_b).then_inc(aw_in, 16)
            act.dma_start(bv_rows[:, :], attn_rows[0:1, :].to_broadcast([P, D])).then_inc(aw_in, 16)
            act.dma_start(bo_rows[:, :], attn_rows[1:2, :].to_broadcast([P, D])).then_inc(aw_in, 16)
            layernorm_scalar(act, S[0].ln)
            route_scalar(act, S[0])
            experts_scalar(act, S[0])
            layernorm_scalar(act, aln)
            prepare_scalar(act)
            attention_scalar(act)
            project_scalar(act)
            layernorm_scalar(act, S[1].ln)
            route_scalar(act, S[1])
            experts_scalar(act, S[1])

        @block.tensor
        def _(pe):
            pe.wait_ge(const_in, 16)
            layernorm_tensor(pe, S[0].ln)
            pe.wait_ge(wr_in, 16)
            route_tensor(pe, S[0])
            experts_tensor(pe, S[0])
            layernorm_tensor(pe, aln)
            prepare_tensor(pe)
            attention_tensor(pe)
            project_tensor(pe)
            layernorm_tensor(pe, S[1].ln)
            route_tensor(pe, S[1])
            experts_tensor(pe, S[1])

        @block.gpsimd
        def _(pool):
            pads_gpsimd(pool)
            experts_gpsimd(pool, S[0], 0)
            prepare_gpsimd(pool)
            pool.wait_ge(aln.xn, NT)
            nc.gpsimd.tensor_tensor(X[:, :, :], X[:, :, :], bc(bo_rows[:, :].unsqueeze(1), [P, NT, D]), ALU.add).then_inc(bias_o, 1)
            experts_gpsimd(pool, S[1], 1)


def kernel(**inputs):
    import concourse.bacc as bacc
    from concourse.bass_utils import run_bass_kernel_spmd

    nc = bacc.Bacc("TRN2", target_bir_lowering=False, num_devices=1)
    arrays = {}

    def given(name, a):
        arrays[name] = np.ascontiguousarray(a)
        return nc.dram_tensor(name, arrays[name].shape, F32, kind="ExternalInput").ap()

    ins = {n: given("in_" + n, inputs[n]) for n in ("L0_attn_x", "L0_ffn_Wr", "L0_ffn_Wg", "L0_ffn_Wu", "L0_ffn_Wd")}
    weights, biases, rows = pack_attention({n: a for n, a in inputs.items() if n.startswith("L0_attn_") and n != "L0_attn_x"})
    cos, sin = rope_arrays()
    out = nc.dram_tensor("out", (1, T, D), F32, kind="ExternalOutput").ap()
    macaron_block(nc, ins, given("const", constant_array()), given("rope_cos", cos), given("rope_sin", sin),
                  given("attn_w", weights), given("attn_b", biases), given("attn_rows", rows), out)
    return run_bass_kernel_spmd(nc, [arrays], core_ids=[0]).results[0]["out"]
```

```python
from contextlib import ExitStack

import numpy as np

import concourse.bass as bass
from concourse import mybir

F32 = mybir.dt.float32
F16 = mybir.dt.float16
BF16 = mybir.dt.bfloat16
I32 = mybir.dt.int32
ALU = mybir.AluOpType
ACT = mybir.ActivationFunctionType
AX = mybir.AxisListType

P = 128
T = 2048
D = 128
NT = T // P
E = 9
F = 352
K2 = 2
SLOT_TILES = (K2 * T + E * (P - 1)) // P
FCH = [(0, 128), (128, 128), (256, 96)]
HC = len(FCH)
LN_EPS = 1e-5
SCORE_SAFE = 60.0
RING = 4
NO_ROW = K2 * T
POOL_TILES = (3, 7, 11)

H = 16
HD = 8
DQ = 64
ROPE_BASE = 10000.0
SCORE_SCALE = float(1.0 / np.sqrt(np.float32(H + 64 + DQ)))
CH = 512
NC = T // CH
PARTS = 3
ROWS = PARTS * PARTS * HD
SHIFT_ROW = ROWS
KR = 96
SLOTS = 3
GB = 3
AW = {n: i for i, n in enumerate(["ct", "uq", "qr", "qrs", "uk", "kr", "krs", "uv", "wo"])}
AB = {n: i for i, n in enumerate(["ct", "uq", "qr", "qrs", "uk", "kr", "krs"])}

CONST_COLS = {}
_at = 0
for _n, _w in [("ident", P), ("lower", P), ("ones", P), ("iota", P), ("emark", E), ("jramp", SLOT_TILES),
               ("thresh", NT * K2), ("tri", E * E), ("token1", K2 * NT), ("hsum", 2 * 32)]:
    CONST_COLS[_n] = (_at, _w)
    _at += _w
CONST_W = _at


def constant_array():
    c = np.zeros((P, CONST_W), np.float32)

    def put(name, value):
        a, w = CONST_COLS[name]
        c[:, a:a + w] = value

    p = np.arange(P)
    put("ident", np.eye(P))
    put("lower", (p[:, None] < p[None, :]))
    put("ones", 1.0)
    put("iota", p[None, :])
    put("emark", np.arange(E)[None, :] - E)
    put("jramp", np.arange(SLOT_TILES)[None, :])
    put("thresh", P * np.arange(NT * K2)[None, :])
    e = np.arange(E)
    put("tri", (e[None, :] < e[:, None]).reshape(1, -1))
    put("token1", np.tile(NT * p[:, None] + np.arange(NT)[None, :] + 1, (1, K2)))
    head = (p[:, None] // HD == np.arange(H)[None, :])
    none = np.zeros((P, H))
    put("hsum", np.concatenate([head, none, none, head], axis=1))
    return c


def rope_arrays():
    ids = np.arange(D // 2, dtype=np.float32)
    theta = (np.float32(ROPE_BASE) ** (np.float32(-2.0) * ids) / np.float32(D // 2)).astype(np.float32)
    col = np.arange(T)
    pos = (NT * (col % P) + col // P).astype(np.float32)
    r = (pos[None, :] * np.repeat(theta, 2)[:, None]).astype(np.float32)
    sign = np.where(np.arange(D) % 2 == 0, -1.0, 1.0)[:, None]
    return np.cos(r).astype(np.float32), (sign * np.sin(r)).astype(np.float32)


def pack_attention(g):
    def at(w, row):
        full = np.zeros((P, D), np.float32)
        full[row:row + w.shape[0]] = w
        return full

    def swap(w):
        return w.reshape(w.shape[:-1] + (D // 2, 2))[..., ::-1].reshape(w.shape)

    g = {n.replace("L0_attn_", ""): np.asarray(v) for n, v in g.items()}
    w = [np.concatenate([g["Wd_q_w"], g["Wd_kv_w"]], axis=1), at(g["Wu_q_w"], 0), at(g["Wq_r_w"], 0), at(swap(g["Wq_r_w"]), 0),
         at(g["Wu_k_w"], DQ), g["Wk_r_w"], swap(g["Wk_r_w"]), at(g["Wu_v_w"], DQ), g["Wo_w"]]
    b = [np.concatenate([g["Wd_q_b"], g["Wd_kv_b"]]), g["Wu_q_b"], g["Wq_r_b"], swap(g["Wq_r_b"]),
         g["Wu_k_b"], g["Wk_r_b"], swap(g["Wk_r_b"])]
    return (np.ascontiguousarray(np.stack(w, axis=1)), np.ascontiguousarray(np.stack(b, axis=1)),
            np.ascontiguousarray(np.stack([g["Wu_v_b"], g["Wo_b"]])))


def macaron_block(nc, ins, const, rope_cos, rope_sin, attn_w, attn_b, attn_rows, out):
    with ExitStack() as ctx:
        def sb(name, shape, dt):
            return ctx.enter_context(nc.sbuf_tensor(name, shape, dt))

        def sem(name):
            return ctx.enter_context(nc.semaphore(name))

        def dram(name, shape, dt):
            return nc.dram_tensor(name, shape, dt, kind="Internal").ap()

        cst = sb("cst", [P, CONST_W], F32)
        X = sb("X", [P, NT, D], F32)
        XN = sb("XN", [P, NT, D], F32)
        XNT = sb("XNT", [P, T], F32)
        Wr = sb("Wr", [P, E], F32)
        Wgu = sb("Wgu", [P, E, 2 * F], F32)
        Wd = sb("Wd", [P, E, 3, D], F32)
        stats = sb("stats", [P, NT, 6], F32)
        mv = sb("mv", [P, NT, 2], F32)
        var = sb("var", [P, NT], F32)
        rstd = sb("rstd", [P, NT], F32)
        newt = sb("newt", [P, NT], F32)
        lower_b = sb("lower_b", [P, P], BF16)
        ones_b = sb("ones_b", [P, P], BF16)
        slot_h = sb("slot_h", [P, P, K2 * NT], F16)
        tile_h = sb("tile_h", [P, SLOT_TILES, K2 * NT], F16)
        token_h = sb("token_h", [P, K2 * NT], F16)
        place_h = sb("place_h", [P, 2, K2 * NT], F16)
        row_any = sb("row_any", [P, SLOT_TILES], F32)
        row_1st = sb("row_1st", [P, SLOT_TILES], F32)
        row_none = sb("row_none", [P, SLOT_TILES], F32)
        warm = sb("warm", [P, 1], F32)
        zeros_b = sb("zeros_b", [P, CH], BF16)
        L = sb("L", [P, NT, E], F32)
        tmpE = sb("tmpE", [P, K2, NT, E], F32)
        pick = sb("pick", [P, K2, NT, E], F32)
        top = sb("top", [P, K2, NT], F32)
        first = sb("first", [P, K2, NT], F32)
        both = sb("both", [P, NT, E], BF16)
        wts = sb("wts", [P, K2, NT], F32)
        tot = sb("tot", [P, E], F32)
        over = sb("over", [P, E, NT * K2], F32)
        ntile = sb("ntile", [P, E], F32)
        tri_p = sb("tri_p", [P, E, E], F32)
        tbase = sb("tbase", [P, E], F32)
        tend = sb("tend", [P, E], F32)
        passed = sb("passed", [P, SLOT_TILES, E], F32)
        texp = sb("texp", [P, SLOT_TILES], F32)
        woff = sb("woff", [P, 2, SLOT_TILES], I32)
        slot = sb("slot", [P, NT, E], F32)
        pos = sb("pos", [P, K2 * NT], F32)
        posi = sb("posi", [P, 3, K2 * NT], I32)
        OA = sb("OA", [P, SLOT_TILES, K2 * NT], F16)
        idx = sb("idx", [P, 2, SLOT_TILES], I32)
        xg = sb("xg", [P, RING, D], F32)
        xgT = sb("xgT", [P, 2, P], F32)
        sg = sb("sg", [P, 2, HC * P], F32)
        hidT = sb("hidT", [P, 2, HC, P], F32)
        wcur = sb("wcur", [P, 2, 2, HC * P], F32)
        yt = sb("yt", [P, RING, D], F32)
        shared = sb("shared", [P, SLOTS * T], F32)
        Y = shared[:, 0:K2 * T].rearrange("p (k i d) -> p k i d", k=K2, d=D)
        OB = shared[:, K2 * T:].bitcast(F16).rearrange("p (q n) -> p q n", q=P)
        temp = shared[:, 0:8 * CH].rearrange("p (a b n) -> p a b n", a=4, b=2)
        EXP = shared[:, :].rearrange("p (b n) -> p b n", n=T)
        cosT = sb("cosT", [P, T], F32)
        sinT = sb("sinT", [P, T], F32)
        aw = sb("aw", [P, len(AW), D], F32)
        ab = sb("ab", [P, len(AB)], F32)
        bv_rows = sb("bv_rows", [P, D], F32)
        bo_rows = sb("bo_rows", [P, D], F32)
        ct = sb("ct", [P, T], F32)
        parts = wcur[:, :, :, :].rearrange("p b g n -> p (b g n)").bitcast(BF16).rearrange("p (b a n) -> p b a n", b=2, a=PARTS)
        V = sb("V", [P, NT, D], F32)
        qslot = sb("qslot", [P, SLOTS, T], BF16)
        kslot = sb("kslot", [P, SLOTS, T], BF16)
        vslot = sb("vslot", [P, SLOTS, NT, 32], F32)
        square_b = sb("square_b", [P, 2, CH], BF16)
        hsum_b = sb("hsum_b", [P, 2 * 32], BF16)
        nmax = sb("nmax", [P, 1], F32)
        nrow = sb("nrow", [1, 2 * H], F32)
        bound = sb("bound", [1, H], F32)
        largest = sb("largest", [1, 1], F32)
        safe = sb("safe", [1, 1], I32)
        smax = sb("smax", [P, 2, P], F32)
        snext = sb("snext", [P, 2, P], F32)
        sparts = sb("sparts", [P, PARTS, 2, P], BF16)
        zeros48 = sb("zeros48", [PARTS * H, P], BF16)
        Oq = sb("Oq", [P, CH], F32)
        denom = sb("denom", [P, NT], F32)
        A = XN
        AT = XNT

        PS = ctx.enter_context(nc.psum_tensor("PS", [P, 8, CH], F32))

        xn_dram = [dram(f"xn_dram{f}", [T, D], F32) for f in range(2)]
        k_dram = dram("k_dram", [P, PARTS, T], BF16)
        q_dram = dram("q_dram", [H, PARTS, HD, T], BF16)
        shift_dram = dram("shift_dram", [PARTS, H, T], BF16)
        y_dram = [dram(f"y_dram{f}", [K2 * T, D], F32) for f in range(2)]

        def c(name):
            a, w = CONST_COLS[name]
            return cst[:, a:a + w]

        ident = c("ident")

        const_in = sem("const_in")
        x_in = [sem(f"x_in{q}") for q in range(4)]
        denom_done = sem("denom_done")
        wr_in = sem("wr_in")
        wexp_in = sem("wexp_in")
        consts_cast = sem("consts_cast")
        vstep = sem("vstep")

        class LnSems:
            def __init__(self, n):
                self.var = sem(f"{n}_var")
                self.sd = sem(f"{n}_sd")
                self.rstd = sem(f"{n}_rstd")
                self.xn = sem(f"{n}_xn")
                self.xn4 = sem(f"{n}_xn4")
                self.T = sem(f"{n}_T")
                self.xnT = sem(f"{n}_xnT")

        class FfnSems:
            def __init__(self, n):
                self.ln = LnSems(n)
                self.xn_out = sem(f"{n}_xn_out")
                self.logits = sem(f"{n}_logits")
                self.top2 = sem(f"{n}_top2")
                self.exp2 = sem(f"{n}_exp2")
                self.both = sem(f"{n}_both")
                self.ranks = sem(f"{n}_ranks")
                self.woff = sem(f"{n}_woff")
                self.onehot = sem(f"{n}_onehot")
                self.slots = sem(f"{n}_slots")
                self.idx = sem(f"{n}_idx")
                self.wts = sem(f"{n}_wts")
                self.z = sem(f"{n}_z")
                self.xg = [sem(f"{n}_xg{s}") for s in range(RING)]
                self.xgT_ps = sem(f"{n}_xgT_ps")
                self.xgT = sem(f"{n}_xgT")
                self.wcur = sem(f"{n}_wcur")
                self.gate = sem(f"{n}_gate")
                self.up = sem(f"{n}_up")
                self.silu = sem(f"{n}_silu")
                self.hid = sem(f"{n}_hid")
                self.y_ps = sem(f"{n}_y_ps")
                self.y = sem(f"{n}_y")
                self.y_out = [sem(f"{n}_y_out{s}") for s in range(RING)]
                self.y_in = [sem(f"{n}_y_in{q}") for q in range(4)]
                self.x1 = sem(f"{n}_x1")
                self.xq = sem(f"{n}_xq")
                self.xq3 = sem(f"{n}_xq3")

        S = [FfnSems("f0"), FfnSems("f1")]
        aln = LnSems("ln_a")
        rope_in = sem("rope_in")
        aw_in = sem("aw_in")
        ct_ps = sem("ct_ps")
        ct_done = sem("ct_done")
        rot_ps = sem("rot_ps")
        lin_ps = sem("lin_ps")
        mixed = sem("mixed")
        full_q = sem("full_q")
        part0 = sem("part0")
        rest1 = sem("rest1")
        full_last = sem("full_last")
        rest_last = sem("rest_last")
        part1 = sem("part1")
        part2 = sem("part2")
        square = sem("square")
        norms = sem("norms")
        parts_out = [sem(f"parts_out{b}") for b in range(2)]
        v_ps = sem("v_ps")
        v_done = sem("v_done")
        pads = sem("pads")
        nmax_done = sem("nmax_done")
        nmax_T = sem("nmax_T")
        safe_done = sem("safe_done")
        const_rows = sem("const_rows")
        shift_in = [sem(f"shift_in{r}") for r in range(SLOTS)]
        m_head = sem("m_head")
        m_score = sem("m_score")
        m_max = sem("m_max")
        m_T = sem("m_T")
        m_step = sem("m_step")
        m_shift = sem("m_shift")
        m_out = sem("m_out")
        head_in = [sem(f"head_in{r}") for r in range(SLOTS)]
        first_q = sem("first_q")
        first_k = sem("first_k")
        head_v = sem("head_v")
        score = sem("score")
        exped = sem("exped")
        pv = sem("pv")
        o_copied = sem("o_copied")
        o_norm = sem("o_norm")
        bias_o = sem("bias_o")
        a_T = sem("a_T")
        a_Tc = sem("a_Tc")
        proj = sem("proj")
        x_attn = sem("x_attn")
        out_done = sem("out_done")
        vcount = [0]

        def chain(dve, inst):
            inst.then_inc(vstep, 1)
            vcount[0] += 1
            dve.wait_ge(vstep, vcount[0])

        def layernorm_vector(dve, s, x_ready, order=range(NT)):
            for n, i in enumerate(order):
                x_ready(n)
                last = nc.vector.bn_stats(stats[:, i, :], X[:, i, :])
            chain(dve, last)
            for i in range(NT):
                last = nc.vector.bn_aggr(mv[:, i, :], stats[:, i, :])
            chain(dve, last)
            chain(dve, nc.vector.tensor_scalar(var[:, :], mv[:, :, 1], LN_EPS, None, ALU.add))
            nc.vector.tensor_copy(newt[:, :], var[:, :]).then_inc(s.var, 1)
            dve.wait_ge(s.sd, 1)
            chain(dve, nc.vector.reciprocal(rstd[:, :], newt[:, :]))
            chain(dve, nc.vector.tensor_tensor(newt[:, :], rstd[:, :], rstd[:, :], ALU.mult))
            chain(dve, nc.vector.tensor_tensor(newt[:, :], newt[:, :], var[:, :], ALU.mult))
            chain(dve, nc.vector.tensor_scalar(newt[:, :], newt[:, :], -0.5, 1.5, ALU.mult, ALU.add))
            nc.vector.tensor_tensor(rstd[:, :], rstd[:, :], newt[:, :], ALU.mult).then_inc(s.rstd, 1)
            dve.wait_ge(s.rstd, 1)
            for i in range(NT):
                if i not in POOL_TILES:
                    nc.vector.tensor_scalar(XN[:, i, :], X[:, i, :], mv[:, i, 0:1], rstd[:, i:i + 1],
                                            ALU.subtract, ALU.mult).then_inc(s.xn, 1)

        def layernorm_gpsimd(pool, s):
            pool.wait_ge(s.rstd, 1)
            for i in POOL_TILES:
                nc.gpsimd.tensor_scalar(XN[:, i, :], X[:, i, :], mv[:, i, 0:1], rstd[:, i:i + 1],
                                        ALU.subtract, ALU.mult).then_inc(s.xn4, 1)

        def layernorm_scalar(act, s):
            act.wait_ge(s.var, 1)
            nc.scalar.activation(newt[:, :], newt[:, :], ACT.Sqrt).then_inc(s.sd, 1)
            for g in range(4):
                act.wait_ge(s.T, g + 1)
                nc.scalar.copy(XNT[:, g * CH:(g + 1) * CH], PS[:, g % 2, :]).then_inc(s.xnT, 1)

        def keep_warm(count, bank=7):
            for _ in range(count):
                nc.tensor.matmul(PS[:, bank, :], zeros_b[:, 0:P], zeros_b[:, :], start=True, stop=True)

        def layernorm_tensor(pe, s, behind=None):
            for g in range(4):
                if g >= 2:
                    pe.wait_ge(s.xnT, g - 1)
                for k in range(4):
                    if 4 * g + k in POOL_TILES:
                        pe.wait_ge(s.xn4, g + 1)
                    else:
                        pe.wait_ge(s.xn, 3 * g + k + 1)
                    last = nc.tensor.transpose(PS[:, g % 2, k * P:(k + 1) * P], XN[:, 4 * g + k, :], ident)
                last.then_inc(s.T, 1)
                if behind and g >= 1:
                    behind(g - 1)
            if behind:
                behind(3)

        def bc(ap, shape):
            return ap.to_broadcast(shape)

        def route_vector(dve, s):
            dve.wait_ge(s.logits, 1)
            logits = PS[:, 2, 0:NT * E].rearrange("p (i e) -> p i e", e=E)
            for k in range(K2):
                src = (logits, L[:, :, :])[k]
                chain(dve, nc.vector.tensor_reduce(top[:, k, :], src, AX.X, ALU.max))
                chain(dve, nc.vector.tensor_tensor(tmpE[:, k], src, bc(top[:, k, :].unsqueeze(2), [P, NT, E]), ALU.is_equal))
                chain(dve, nc.vector.tensor_tensor(tmpE[:, k], tmpE[:, k], bc(c("emark").unsqueeze(1), [P, NT, E]), ALU.mult))
                chain(dve, nc.vector.tensor_reduce(first[:, k, :], tmpE[:, k], AX.X, ALU.min))
                chain(dve, nc.vector.tensor_tensor(pick[:, k], bc(c("emark").unsqueeze(1), [P, NT, E]),
                                                   bc(first[:, k, :].unsqueeze(2), [P, NT, E]), ALU.is_equal))
                if k == 0:
                    chain(dve, nc.vector.scalar_tensor_tensor(L[:, :, :], pick[:, 0], -3.0e38, logits, ALU.mult, ALU.add))
            nc.vector.tensor_tensor(both[:, :, :], pick[:, 0], pick[:, 1], ALU.add).then_inc(s.both, 1)
            nc.vector.tensor_tensor(wts[:, 1, :], top[:, 1, :], top[:, 0, :], ALU.subtract).then_inc(s.top2, 1)
            dve.wait_ge(s.ranks, 1)
            chain(dve, nc.vector.tensor_reduce(tot[:, :], PS[:, 4, 0:NT * E].rearrange("p (i e) -> p e i", e=E), AX.X, ALU.add))
            chain(dve, nc.vector.tensor_tensor(over[:, :, :], bc(tot[:, :].unsqueeze(2), [P, E, NT * K2]),
                                               bc(c("thresh").unsqueeze(1), [P, E, NT * K2]), ALU.is_gt))
            chain(dve, nc.vector.tensor_reduce(ntile[:, :], over[:, :, :], AX.X, ALU.add))
            chain(dve, nc.vector.tensor_tensor(tri_p[:, :, :], c("tri").rearrange("p (a b) -> p a b", b=E),
                                               bc(ntile[:, :].unsqueeze(1), [P, E, E]), ALU.mult))
            chain(dve, nc.vector.tensor_reduce(tbase[:, :], tri_p[:, :, :], AX.X, ALU.add))
            nc.vector.tensor_tensor(tend[:, :], tbase[:, :], ntile[:, :], ALU.add)
            chain(dve, nc.vector.tensor_scalar(tbase[:, :], tbase[:, :], float(P), None, ALU.mult))
            chain(dve, nc.vector.tensor_tensor(slot[:, :, :], PS[:, 3, 0:NT * E].rearrange("p (i e) -> p i e", e=E),
                                               bc(tbase[:, :].unsqueeze(1), [P, NT, E]), ALU.add))
            for k in range(K2):
                last = nc.vector.tensor_tensor(tmpE[:, k], pick[:, k], slot[:, :, :], ALU.mult)
            chain(dve, last)
            chain(dve, nc.vector.tensor_reduce(pos[:, :], tmpE[:, :, :, :].rearrange("p k i e -> p (k i) e"), AX.X, ALU.add))
            chain(dve, nc.vector.tensor_copy(posi[:, 0, :], pos[:, :]))
            nc.vector.tensor_scalar(posi[:, 1, :], posi[:, 0, :], 7, None, ALU.arith_shift_right)
            chain(dve, nc.vector.tensor_scalar(posi[:, 2, :], posi[:, 0, :], P - 1, None, ALU.bitwise_and))
            chain(dve, nc.vector.tensor_copy(place_h[:, :, :], posi[:, 1:3, :]))
            n = K2 * NT
            chain(dve, nc.vector.tensor_tensor(OA[:, :, :], tile_h[:, :, :], bc(place_h[:, 0:1, :], [P, SLOT_TILES, n]), ALU.is_equal))
            nc.vector.tensor_tensor(OA[:, :, :], OA[:, :, :], bc(token_h[:, :].unsqueeze(1), [P, SLOT_TILES, n]), ALU.mult)
            for g in range(K2):
                q = slice(g * NT, (g + 1) * NT)
                nc.vector.tensor_tensor(OB[:, :, q], slot_h[:, :, q], bc(place_h[:, 1:2, q], [P, P, NT]), ALU.is_equal).then_inc(s.onehot, 1)
            chain(dve, nc.vector.tensor_tensor(passed[:, :, :], bc(tend[:, :].unsqueeze(1), [P, SLOT_TILES, E]),
                                               bc(c("jramp").unsqueeze(2), [P, SLOT_TILES, E]), ALU.is_le))
            chain(dve, nc.vector.tensor_reduce(texp[:, :], passed[:, :, :], AX.X, ALU.add))
            nc.vector.tensor_scalar(woff[:, 0, :], texp[:, :], float(E - 1), float(2 * F), ALU.min, ALU.mult)
            nc.vector.tensor_scalar(woff[:, 1, :], texp[:, :], float(E - 1), float(3 * D), ALU.min, ALU.mult).then_inc(s.woff, 1)
            dve.wait_ge(s.slots, 1)
            row_0 = PS[:, 5, 0:SLOT_TILES]
            chain(dve, nc.vector.tensor_reduce(row_any[:, :], PS[:, 5, 0:K2 * SLOT_TILES].rearrange("p (k t) -> p t k", k=K2), AX.X, ALU.add))
            nc.vector.tensor_scalar(idx[:, 0, :], row_any[:, :], -1.0, 0.0, ALU.add, ALU.max).then_inc(s.idx, 1)
            nc.vector.tensor_scalar(row_1st[:, :], row_0, 0.0, float(T), ALU.is_gt, ALU.mult)
            chain(dve, nc.vector.tensor_scalar(row_none[:, :], row_any[:, :], 0.0, float(NO_ROW + 1), ALU.is_equal, ALU.mult))
            chain(dve, nc.vector.tensor_tensor(row_1st[:, :], row_1st[:, :], row_any[:, :], ALU.add))
            nc.vector.scalar_tensor_tensor(idx[:, 1, :], row_none[:, :], -1.0, row_1st[:, :], ALU.add, ALU.add).then_inc(s.idx, 1)
            dve.wait_ge(s.exp2, 1)
            chain(dve, nc.vector.tensor_scalar(wts[:, 0, :], wts[:, 1, :], 1.0, None, ALU.add))
            chain(dve, nc.vector.reciprocal(wts[:, 0, :], wts[:, 0, :]))
            chain(dve, nc.vector.tensor_scalar(wts[:, 0, :], wts[:, 0, :], 0.5, None, ALU.mult))
            nc.vector.tensor_tensor(wts[:, 1, :], wts[:, 1, :], wts[:, 0, :], ALU.mult).then_inc(s.wts, 1)

        def route_scalar(act, s):
            act.wait_ge(s.top2, 1)
            nc.scalar.activation(wts[:, 1, :], wts[:, 1, :], ACT.Exp).then_inc(s.exp2, 1)
            act.wait_ge(pads, 1)
            nc.scalar.activation(warm[:, :], warm[:, :], ACT.Silu)

        def route_logits(pe, s, g):
            pe.wait_ge(s.ln.xnT, g + 1)
            for i in range(4 * g, 4 * g + 4):
                last = nc.tensor.matmul(PS[:, 2, i * E:(i + 1) * E], XNT[:, i * P:(i + 1) * P], Wr[:, :], start=True, stop=True)
            if g == 3:
                last.then_inc(s.logits, 1)

        def route_tensor(pe, s):
            pe.wait_ge(s.both, 1)
            m = both[:, :, :].rearrange("p i e -> p (i e)")
            nc.tensor.matmul(PS[:, 4, 0:NT * E], ones_b[:, :], m, start=True, stop=True)
            nc.tensor.matmul(PS[:, 3, 0:NT * E], lower_b[:, :], m, start=True, stop=False)
            for d in range(1, NT):
                last = nc.tensor.matmul(PS[:, 3, d * E:NT * E], ones_b[:, :], m[:, 0:(NT - d) * E], start=False, stop=(d == NT - 1))
            last.then_inc(s.ranks, 1)
            n = K2 * NT
            for q in range(n):
                k = q // NT
                if q % NT == 0:
                    pe.wait_ge(s.onehot, k + 1)
                last = nc.tensor.matmul(PS[:, 5, k * SLOT_TILES:(k + 1) * SLOT_TILES], OB[:, :, q], OA[:, :, q],
                                        start=(q % NT == 0), stop=(q % NT == NT - 1))
            last.then_inc(s.slots, 1)
            keep_warm(11)

        def load_offset(engine, which, j):
            return nc.values_load(woff[0:1, which, j:j + 1] if isinstance(j, int) else woff[0:1, which, bass.ds(j, 1)],
                                  engines=[engine], min_val=0, max_val=(E - 1) * (2 * F, 3 * D)[which],
                                  skip_runtime_bounds_check_because="the offset was clamped to the last expert's")

        def tile_transpose_x(pe, s, j, r):
            pe.wait_ge(s.xg[r % RING], (j - r % RING) * (16 // RING) + 16)
            nc.tensor.transpose(PS[:, 0, 0:P], xg[:, r % RING, :], ident).then_inc(s.xgT_ps, 1)

        def tile_gate_up(pe, s, j, r):
            pe.wait_ge(s.wcur, j + 1)
            pe.wait_ge(s.xgT, j + 1)
            for bank, half, done in ((GATE_BANK[r % 2], 0, s.gate), (UP_BANK[r % 2], 1, s.up)):
                for n in range(HC):
                    last = nc.tensor.matmul(PS[:, bank, n * P:(n + 1) * P], wcur[:, r % 2, half, n * P:(n + 1) * P], xgT[:, r % 2, :],
                                            start=True, stop=True)
                last.then_inc(done, 1)

        def tile_down(pe, s, j, r, off):
            wd = Wd[:, :, :, :].rearrange("p e n d -> p (e n d)")
            pe.wait_ge(s.hid, j + 1)
            for n, (a, w) in enumerate(FCH):
                last = nc.tensor.matmul(PS[:, Y_BANK[r % 2], 0:D], hidT[0:w, r % 2, n, :], wd[0:w, bass.ds(off + n * D, D)],
                                        start=(n == 0), stop=(n == HC - 1))
            last.then_inc(s.y_ps, 1)

        GATE_BANK, UP_BANK, Y_BANK = (1, 6), (2, 7), (3, 4)

        def experts_tensor(pe, s):
            pe.wait_ge(s.woff, 1)
            tile_transpose_x(pe, s, 0, 0)
            pe.wait_ge(wexp_in, 5 * 16)
            tile_gate_up(pe, s, 0, 0)
            tile_transpose_x(pe, s, 1, 1)

            def tile(j, r, more=2):
                down = load_offset(mybir.EngineType.PE, 1, j)
                if more >= 1:
                    tile_gate_up(pe, s, j + 1, r + 1)
                if more >= 2:
                    tile_transpose_x(pe, s, j + 2, r + 2)
                tile_down(pe, s, j, r, down)

            STEP = 2 * RING
            with pe.Fori(0, SLOT_TILES // STEP - 1) as n:
                for r in range(STEP):
                    tile(n * STEP + r, r)
            for r in range(STEP):
                tile(SLOT_TILES - STEP + r, r, more=min(2, STEP - 1 - r))

        def experts_scalar(act, s):
            def copy_x(j, r):
                act.wait_ge(s.xgT_ps, j + 1)
                if not (isinstance(j, int) and j < 2):
                    act.wait_ge(s.up, j - 1)
                nc.scalar.copy(xgT[:, r % 2, :], PS[:, 0, 0:P]).then_inc(s.xgT, 1)

            def silu(j, r):
                act.wait_ge(s.gate, j + 1)
                if not (isinstance(j, int) and j < 2):
                    act.wait_ge(s.hid, j - 1)
                nc.scalar.activation(sg[:, r % 2, :], PS[:, GATE_BANK[r % 2], 0:HC * P], ACT.Silu).then_inc(s.silu, 1)

            def tile(j, r, more=2):
                if more >= 1:
                    silu(j + 1, r + 1)
                if more >= 2:
                    copy_x(j + 2, r + 2)
                act.wait_ge(s.y_ps, j + 1)
                if not (isinstance(j, int) and j < RING):
                    act.wait_ge(s.y_out[r % RING], (j - r) * (16 // RING))
                nc.scalar.copy(yt[:, r % RING, :], PS[:, Y_BANK[r % 2], 0:D]).then_inc(s.y, 1)

            copy_x(0, 0)
            silu(0, 0)
            copy_x(1, 1)
            for r in range(RING):
                tile(r, r)
            with act.Fori(1, SLOT_TILES // RING - 1) as n:
                for r in range(RING):
                    tile(n * RING + r, r)
            for r in range(RING):
                tile(SLOT_TILES - RING + r, r, more=min(2, RING - 1 - r))

        def experts_vector(dve, s):
            def mult(j, r):
                dve.wait_ge(s.up, j + 1)
                dve.wait_ge(s.silu, j + 1)
                nc.vector.tensor_tensor(hidT[:, r % 2, :, :].rearrange("p n t -> p (n t)"), PS[:, UP_BANK[r % 2], 0:HC * P],
                                        sg[:, r % 2, :], ALU.mult).then_inc(s.hid, 1)

            def copy_weights(j, r):
                off = load_offset(mybir.EngineType.DVE, 0, j)
                w = Wgu[:, :, :].rearrange("p e n -> p (e n)")
                nc.vector.tensor_copy(wcur[:, r % 2, :, 0:F], w[:, bass.ds(off, 2 * F)].rearrange("p (g n) -> p g n", g=2)).then_inc(s.wcur, 1)

            nc.vector.memset(wcur[:, :, :, F:], 0.0)
            dve.wait_ge(s.woff, 1)
            dve.wait_ge(wexp_in, 5 * 16)
            for r in range(2):
                copy_weights(r, r)
            with dve.Fori(0, SLOT_TILES // 2 - 1) as n:
                for r in range(2):
                    mult(n * 2 + r, r)
                    copy_weights(n * 2 + (r + 2), r)
            for r in range(2):
                mult(SLOT_TILES - 2 + r, r)

        def experts_gpsimd(pool, s, f):
            def gather(j):
                if j >= RING:
                    pool.wait_ge(s.xgT_ps, j - RING + 1)
                nc.gpsimd.indirect_dma_start(xg[:, j % RING, :], None, xn_dram[f], bass.IndirectOffsetOnAxis(idx[:, 0, j:j + 1], 0)
                                             ).then_inc(s.xg[j % RING], 16)

            def scatter(j):
                pool.wait_ge(s.y, j + 1)
                nc.gpsimd.indirect_dma_start(y_dram[f], bass.IndirectOffsetOnAxis(idx[:, 1, j:j + 1], 0), yt[:, j % RING, :], None,
                                             bounds_check=NO_ROW - 1, oob_is_err=False).then_inc(s.y_out[j % RING], 16)

            pool.wait_ge(s.idx, 1)
            pool.wait_ge(s.xn_out, 16)
            for j in range(RING):
                gather(j)
            pool.wait_ge(s.idx, 2)
            for j in range(SLOT_TILES):
                if j + RING < SLOT_TILES:
                    gather(j + RING)
                scatter(j)

        def ffn_sync(sp, s, f):
            sp.wait_ge(s.ln.xn, NT - len(POOL_TILES))
            sp.wait_ge(s.ln.xn4, len(POOL_TILES))
            sp.dma_start(xn_dram[f].rearrange("(p i) d -> p i d", i=NT), XN[:, :, :]).then_inc(s.xn_out, 16)
            for r in range(RING):
                sp.wait_ge(s.y_out[r], 16 * SLOT_TILES // RING)
            yv = y_dram[f].rearrange("(k p i) d -> p k i d", k=K2, i=NT)
            for q in range(4):
                for k in range(K2):
                    sp.dma_start(Y[:, k, 4 * q:4 * q + 4, :], yv[:, 1 - k, 4 * q:4 * q + 4, :]).then_inc(s.y_in[q], 16)

        def combine_scalar(act, s):
            act.wait_ge(s.wts, 1)
            for q in range(4):
                act.wait_ge(s.y_in[q], 32)
                for i in range(4 * q, 4 * q + 4):
                    last = nc.scalar.activation(Y[:, 1, i, :], Y[:, 1, i, :], ACT.Copy, scale=wts[:, 1, i:i + 1])
                last.then_inc(s.z, 1)

        def combine_vector(dve, s, q):
            dve.wait_ge(s.wts, 1)
            dve.wait_ge(s.y_in[q], 32)
            for i in range(4 * q, 4 * q + 4):
                last = nc.vector.scalar_tensor_tensor(X[:, i, :], Y[:, 0, i, :], wts[:, 0, i:i + 1], X[:, i, :], ALU.mult, ALU.add)
            if q < 3:
                last.then_inc(s.x1, 1)
            else:
                dve.wait_ge(s.z, 4)
                chain(dve, last)
                nc.vector.tensor_tensor(X[:, 12:16, :], X[:, 12:16, :], Y[:, 1, 12:16, :], ALU.add).then_inc(s.xq3, 1)

        def x_updated(eng, s, q):
            if q < 3:
                eng.wait_ge(s.xq, q + 1)
            else:
                eng.wait_ge(s.xq3, 1)

        def combine_gpsimd(pool, s):
            for q in range(3):
                pool.wait_ge(s.z, q + 1)
                pool.wait_ge(s.x1, q + 1)
                nc.gpsimd.tensor_tensor(X[:, 4 * q:4 * q + 4, :], X[:, 4 * q:4 * q + 4, :], Y[:, 1, 4 * q:4 * q + 4, :], ALU.add).then_inc(s.xq, 1)

        def ahead(dve, update, wait_done):
            def x_ready(i):
                if i % 4 == 0:
                    if i == 0:
                        update(0)
                    if i // 4 + 1 < 4:
                        update(i // 4 + 1)
                    wait_done(i // 4)
            return x_ready

        UNITS = 2 * NC
        T1, T2, FULL, REST = range(4)

        def prepare_product(bank, w, rhs):
            return nc.tensor.matmul(PS[:, bank, :], aw[:, AW[w], :], rhs, start=True, stop=True)

        def prepare_first(pe, g):
            if g == 0:
                pe.wait_ge(aw_in, 64)
                pe.wait_ge(aln.xnT, 1)
                prepare_product(2, "ct", XNT[:, 0:CH]).then_inc(ct_ps, 1)
                prepare_product(3, "kr", XNT[:, 0:CH])
            elif g == 1:
                prepare_product(4, "krs", XNT[:, 0:CH]).then_inc(rot_ps, 1)

        def prepare_tensor(pe):
            mm = prepare_product

            def values_product(c_):
                for i in range(4 * c_, 4 * c_ + 4):
                    last = nc.tensor.matmul(PS[:, 2, i % 4 * P:(i % 4 + 1) * P], ct[:, i * P:(i + 1) * P], aw[:, AW["uv"], :],
                                            start=True, stop=True)
                last.then_inc(v_ps, 1)

            def norm(u):
                c_, half = u // 2, u % 2
                pe.wait_ge(square, u + 1)
                hs = hsum_b[:, 32 * half:32 * half + 32]
                nc.tensor.matmul(PS[32 * c_:32 * c_ + 32, 1, :], hs, square_b[:, u % 2, :],
                                 start=(half == 0), stop=(half == 1)).then_inc(norms, 1)

            for c_ in range(NC):
                cols = slice(c_ * CH, (c_ + 1) * CH)
                if c_ >= 1:
                    pe.wait_ge(mixed, 2 * c_ - 1)
                    mm(3, "kr", XNT[:, cols])
                    mm(4, "krs", XNT[:, cols]).then_inc(rot_ps, 1)
                pe.wait_ge(ct_done, c_ + 1)
                mm(5, "uk", ct[:, cols]).then_inc(lin_ps, 1)
                if c_ < NC - 1:
                    values_product(c_)
                if c_ >= 1:
                    pe.wait_ge(mixed, 2 * c_)
                else:
                    pe.wait_ge(aln.xnT, NC)
                mm(6, "qr", ct[:, cols])
                mm(7, "qrs", ct[:, cols]).then_inc(rot_ps, 1)
                mm(0, "uq", ct[:, cols]).then_inc(lin_ps, 1)
                if c_ == NC - 1:
                    values_product(c_)
                if c_ + 1 < NC:
                    pe.wait_ge(v_done, c_ + 1)
                    mm(2, "ct", XNT[:, (c_ + 1) * CH:(c_ + 2) * CH]).then_inc(ct_ps, 1)
                if c_ >= 1:
                    norm(2 * c_ - 2)
                    norm(2 * c_ - 1)
            pe.wait_ge(mixed, UNITS - 1)
            keep_warm(4, 4)
            norm(UNITS - 2)
            keep_warm(8, 4)
            norm(UNITS - 1)
            keep_warm(10, 4)
            pe.wait_ge(nmax_done, 1)
            pe.wait_ge(v_done, NC)
            nc.tensor.transpose(PS[0:1, 2, 0:P], nmax[:, :], ident).then_inc(nmax_T, 1)
            keep_warm(8, 4)

        def prepare_scalar(act):
            act.wait_ge(aw_in, 64)

            def compressed(c_):
                act.wait_ge(ct_ps, c_ + 1)
                nc.scalar.activation(ct[:, c_ * CH:(c_ + 1) * CH], PS[:, 2, :], ACT.Identity, bias=ab[:, AB["ct"]:AB["ct"] + 1]).then_inc(ct_done, 1)

            compressed(0)
            for u in range(UNITS):
                if u % 2 == 1 and u // 2 + 1 < NC:
                    compressed(u // 2 + 1)
                if u < UNITS - 1:
                    act.wait_ge(full_q, u + 1)
                else:
                    act.wait_ge(full_last, 1)
                if u >= 2:
                    act.wait_ge(parts_out[u % 2], (16, 16 * PARTS)[u % 2] * (u // 2))
                nc.scalar.copy(parts[:, u % 2, 0, :], temp[:, FULL, u % 2, :]).then_inc(part0, 1)
                if u >= 2:
                    act.wait_ge(norms, u - 1)
                nc.scalar.activation(square_b[:, u % 2, :], temp[:, FULL, u % 2, :], ACT.Square).then_inc(square, 1)
                if u < UNITS - 1:
                    act.wait_ge(rest1, u + 1)
                else:
                    act.wait_ge(rest_last, 1)
                nc.scalar.copy(parts[:, u % 2, 1, :], temp[:, REST, u % 2, :]).then_inc(part1, 1)

        def prepare_vector(dve):
            dve.wait_ge(aw_in, 64)
            dve.wait_ge(rope_in, 32)

            def third(u):
                dve.wait_ge(part1, u + 1)
                nc.vector.tensor_tensor(parts[:, u % 2, 2, :], temp[:, REST, u % 2, :], parts[:, u % 2, 1, :], ALU.subtract).then_inc(part2, 1)

            for u in range(UNITS):
                c_, b = u // 2, u % 2
                cols = slice(c_ * CH, (c_ + 1) * CH)
                rot, rots, lin = ((3, 4, 5), (6, 7, 0))[b]
                names = (("kr", "krs", "uk"), ("qr", "qrs", "uq"))[b]
                bias = [ab[:, AB[n]:AB[n] + 1] for n in names]
                dve.wait_ge(rot_ps, u + 1)
                if u >= 2:
                    dve.wait_ge(full_q, u - 1)
                chain(dve, nc.vector.scalar_tensor_tensor(temp[:, T1, b, :], PS[:, rot, :], bias[0], cosT[:, cols], ALU.add, ALU.mult))
                nc.vector.scalar_tensor_tensor(temp[:, T2, b, :], PS[:, rots, :], bias[1], sinT[:, cols], ALU.add, ALU.mult)
                dve.wait_ge(lin_ps, u + 1)
                last = nc.vector.scalar_tensor_tensor(temp[:, T1, b, :], PS[:, lin, :], bias[2], temp[:, T1, b, :], ALU.add, ALU.add)
                last.then_inc(mixed, 1)
                if u == UNITS - 1:
                    dve.wait_ge(mixed, UNITS)
                    dve.wait_ge(square, u - 1)
                    nc.vector.tensor_tensor(temp[:, FULL, b, :], temp[:, T1, b, :], temp[:, T2, b, :], ALU.add).then_inc(full_last, 1)
                if b == (1 if c_ == NC - 1 else 0):
                    dve.wait_ge(v_ps, c_ + 1)
                    nc.vector.tensor_tensor(V[:, 4 * c_:4 * c_ + 4, :], PS[:, 2, :].rearrange("p (i d) -> p i d", d=D),
                                            bc(bv_rows[:, :].unsqueeze(1), [P, 4, D]), ALU.add).then_inc(v_done, 1)
                if u >= 1:
                    third(u - 1)
            dve.wait_ge(part0, UNITS)
            nc.vector.tensor_tensor(temp[:, REST, 1, :], temp[:, FULL, 1, :], parts[:, 1, 0, :], ALU.subtract).then_inc(rest_last, 1)
            third(UNITS - 1)
            dve.wait_ge(norms, UNITS)
            nc.vector.tensor_reduce(nmax[:, :], PS[:, 1, :], AX.X, ALU.max).then_inc(nmax_done, 1)
            dve.wait_ge(nmax_T, 1)
            chain(dve, nc.vector.tensor_reduce(nrow[:, :], PS[0:1, 2, 0:P].rearrange("p (c m) -> p m c", m=2 * H), AX.X, ALU.max))
            chain(dve, nc.vector.tensor_tensor(bound[:, :], nrow[:, 0:H], nrow[:, H:], ALU.mult))
            chain(dve, nc.vector.tensor_reduce(largest[:, :], bound[:, :], AX.X, ALU.max))
            nc.vector.tensor_scalar(safe[:, :], largest[:, :], (SCORE_SAFE / SCORE_SCALE) ** 2, None, ALU.is_le).then_inc(safe_done, 1)

        def pads_gpsimd(pool):
            nc.gpsimd.memset(warm[:, :], 0.0)
            nc.gpsimd.memset(zeros_b[:, :].bitcast(F32), 0.0).then_inc(pads, 1)
            nc.gpsimd.memset(vslot[:, :, :, :], 0.0).then_inc(pads, 1)
            nc.gpsimd.memset(zeros48[:, :].bitcast(F32), 0.0).then_inc(pads, 1)
            pool.wait_ge(pads, 3)
            nc.gpsimd.memset(qslot[64:P, :, :].bitcast(F32), 0.0)
            nc.gpsimd.memset(kslot[64:P, :, :].bitcast(F32), 0.0).then_inc(pads, 1)
            pool.wait_ge(pads, 4)
            nc.gpsimd.memset(vslot[:, :, :, HD:HD + 1], 1.0).then_inc(pads, 1)

        def prepare_gpsimd(pool):
            for u in range(UNITS - 1):
                b = u % 2
                pool.wait_ge(mixed, u + 1)
                if u >= 2:
                    pool.wait_ge(square, u - 1)
                nc.gpsimd.tensor_tensor(temp[:, FULL, b, :], temp[:, T1, b, :], temp[:, T2, b, :], ALU.add).then_inc(full_q, 1)
                pool.wait_ge(part0, u + 1)
                if u >= 2:
                    pool.wait_ge(part2, u - 1)
                nc.gpsimd.tensor_tensor(temp[:, REST, b, :], temp[:, FULL, b, :], parts[:, b, 0, :], ALU.subtract).then_inc(rest1, 1)

        def load_head(sp, h, r, done):
            load_k(sp, h, r, slice(0, T), done)
            load_q(sp, h, r, slice(0, T), done)

        def load_k(sp, h, r, cols, done):
            rows = slice(HD * h, HD * h + HD) if isinstance(h, int) else bass.ds(h * HD, HD)
            k = k_dram[rows, :, cols].rearrange("d j n -> (d j) n").unsqueeze(0)
            sp.dma_start(kslot[0:ROWS, r, cols], k.to_broadcast([PARTS, HD * PARTS, cols.stop - cols.start])).then_inc(done, 16)

        def load_q(sp, h, r, cols, done):
            head = slice(h, h + 1) if isinstance(h, int) else bass.ds(h, 1)
            q = q_dram[head, :, :, cols].rearrange("h i d n -> (h i d) n").unsqueeze(1)
            sp.dma_start(qslot[0:ROWS, r, cols], q.to_broadcast([PARTS * HD, PARTS, cols.stop - cols.start])).then_inc(done, 16)

        def load_shift(sp, h, r, done):
            src = shift_dram[:, h, :] if isinstance(h, int) else shift_dram[:, bass.ds(h, 1), :].rearrange("a h n -> a (h n)")
            sp.dma_start(qslot[SHIFT_ROW:SHIFT_ROW + PARTS, r, :], src).then_inc(done, 16)

        HEAD_DMAS = 2

        def unbounded(engine_type, eng, ready):
            eng.wait_ge(ready, 1)
            flag = nc.values_load(safe[0:1, 0:1], engines=[engine_type], min_val=0, max_val=1,
                                  skip_runtime_bounds_check_because="a comparison's result")
            return eng.If(flag == 0)

        MAX_SLOT = SLOTS - 1

        def maxima_sync(sp):
            with sp.Fori(0, H) as h:
                sp.wait_ge(m_max, h * NT + 1)
                load_head(sp, h, MAX_SLOT, m_head)
            sp.wait_ge(m_max, H * NT + 1)
            sp.wait_ge(m_shift, 1)
            sp.dma_start(shift_dram.rearrange("a (b g) (i q) -> (g i) a b q", b=2, q=P), sparts[:, :, :, :]).then_inc(m_out, 16)
            sp.wait_ge(m_out, 16)
            for h in range(SLOTS):
                load_shift(sp, h, h, m_out)
            sp.wait_ge(m_out, 16 * (1 + SLOTS))

        def maxima_tensor(pe):
            with pe.Fori(0, H) as h:
                pe.wait_ge(m_head, (h + 1) * (16 * HEAD_DMAS))
                for i in range(NT):
                    pe.wait_ge(m_max, h * NT + i if i >= 1 else h * NT + 1)
                    for k in range(NC):
                        last = nc.tensor.matmul(PS[:, 4 * (i % 2) + k, :], qslot[0:KR, MAX_SLOT, i * P:(i + 1) * P],
                                                kslot[0:KR, MAX_SLOT, k * CH:(k + 1) * CH], start=True, stop=True)
                    last.then_inc(m_score, 1)
            pe.wait_ge(m_max, H * NT + 1)
            for b in range(2):
                last = nc.tensor.transpose(PS[:, 0, b * P:(b + 1) * P], smax[:, b, :], ident)
            last.then_inc(m_T, 1)
            pe.wait_ge(m_out, 16 * (1 + SLOTS))

        def maxima_vector(dve):
            nc.vector.memset(snext[:, :, :], 0.0).then_inc(m_max, 1)
            flat = smax[:, :, :].rearrange("p b n -> p (b n)")
            with dve.Fori(0, H) as h:
                for i in range(NT):
                    b = 4 * (i % 2)
                    dve.wait_ge(m_score, h * NT + (i + 1))
                    nc.vector.tensor_reduce(flat[:, bass.ds(h * NT + i, 1)], PS[:, b:b + 4, :], AX.XY, ALU.max).then_inc(m_max, 1)
            dve.wait_ge(m_T, 1)
            nc.vector.tensor_scalar(snext[:, :, :], PS[:, 0, 0:2 * P].rearrange("p (b n) -> p b n", b=2), -1.0, None, ALU.mult).then_inc(m_step, 1)
            for a in range(PARTS):
                dve.wait_ge(m_step, 2 * a + 1)
                nc.vector.tensor_copy(sparts[:, a, :, :], snext[:, :, :]).then_inc(m_step, 1)
                dve.wait_ge(m_step, 2 * a + 2)
                nc.vector.tensor_tensor(snext[:, :, :], snext[:, :, :], sparts[:, a, :, :], ALU.subtract).then_inc(m_step, 1)
            dve.wait_ge(m_step, 2 * PARTS + 1)
            nc.vector.tensor_copy(nmax[:, :], nmax[:, :]).then_inc(m_shift, 1)

        def attention_sync(sp):
            early, tail = slice(0, (NC - 1) * CH), slice((NC - 1) * CH, T)
            sp.wait_ge(pads, 4)
            sp.wait_ge(consts_cast, 1)
            for r in range(SLOTS):
                sp.dma_start(kslot[SHIFT_ROW:SHIFT_ROW + PARTS, r, :].rearrange("a (i n) -> a i n", n=P),
                             ones_b[0:PARTS, :].unsqueeze(1).to_broadcast([PARTS, NT, P])).then_inc(const_rows, 16)
            sp.dma_start(shift_dram.rearrange("a h (i n) -> (a h) i n", n=P),
                         zeros48[:, :].unsqueeze(1).to_broadcast([PARTS * H, NT, P])).then_inc(const_rows, 16)
            for u in range(UNITS):
                c_, b = u // 2, u % 2
                cols = slice(c_ * CH, (c_ + 1) * CH)
                if b == 0:
                    if c_ == NC - 1:
                        sp.wait_ge(const_rows, 16 * (SLOTS + 1))
                        sp.wait_ge(parts_out[0], 16 * (NC - 1))
                        load_k(sp, 0, 0, early, head_in[0])
                        sp.wait_ge(parts_out[1], 16 * PARTS * (NC - 1))
                        load_q(sp, 0, 0, early, head_in[0])
                    sp.wait_ge(part2, u + 1)
                    sp.dma_start(k_dram[:, :, cols], parts[:, b, :, :]).then_inc(parts_out[b], 16)
                else:
                    last = c_ == NC - 1
                    for a, done in enumerate((part0, part1, part2)):
                        sp.wait_ge(done, u + 1)
                        if last:
                            sp.dma_start(qslot[PARTS * HD * a:PARTS * HD * (a + 1), 0, cols],
                                         parts[0:HD, b, a:a + 1, :].to_broadcast([HD, PARTS, CH])).then_inc(first_q, 16)
                        sp.dma_start(q_dram[:, a, :, cols], parts[:, b, a, :]).then_inc(parts_out[b], 16)
            sp.wait_ge(parts_out[1], 16 * PARTS * NC)
            sp.wait_ge(parts_out[0], 16 * NC)
            load_k(sp, 0, 0, tail, first_k)
            load_head(sp, 1, 1, head_in[1])
            with unbounded(mybir.EngineType.SP, sp, safe_done):
                maxima_sync(sp)
            load_head(sp, SLOTS - 1, SLOTS - 1, head_in[SLOTS - 1])
            with sp.Fori(1, H // SLOTS) as n:
                for r in range(SLOTS):
                    sp.wait_ge(score, (n * SLOTS + (r - SLOTS + 1)) * 32)
                    load_head(sp, n * SLOTS + r, r, head_in[r])
                    load_shift(sp, n * SLOTS + r, r, shift_in[r])
            sp.wait_ge(score, (H - SLOTS) * 32)
            load_head(sp, H - 1, 0, head_in[0])
            load_shift(sp, H - 1, 0, shift_in[0])

        BODY = SLOTS * NT

        def attention_tensor(pe):
            def scores(u0, v, half):
                h, kt, r = v // NT, v % NT, (v // NT) % SLOTS
                g = 2 * v + half
                fixed = isinstance(u0, int)
                if fixed and u0 + v == (NC - 1) * CH // P and half == 0:
                    pe.wait_ge(first_k, 16)
                if kt == 0 and half == 0:
                    before = (u0 // BODY if fixed else u0) + v // BODY
                    pe.wait_ge(head_in[r], before * (16 * HEAD_DMAS) + 16 * HEAD_DMAS)
                    if not (fixed and before == 0):
                        pe.wait_ge(shift_in[r], before * 16)
                    elif r == 0:
                        pe.wait_ge(first_q, 16 * PARTS)
                G = (2 * u0 if fixed else u0 * (2 * BODY)) + g
                if not (fixed and G < GB):
                    pe.wait_ge(exped, G - GB + 1)
                for k in range(2):
                    last = nc.tensor.matmul(PS[:, 2 * (g % GB) + k, :], kslot[0:KR, r, kt * P:(kt + 1) * P],
                                            qslot[0:KR, r, (2 * half + k) * CH:(2 * half + k + 1) * CH], start=True, stop=True)
                last.then_inc(score, 1)

            def values(u0, v):
                fixed = isinstance(u0, int)
                kt = v % NT
                r = (v // NT) % SLOTS
                U = (u0 if fixed else u0 * BODY) + v
                if kt == 0:
                    hh = (u0 // NT if fixed else u0 * SLOTS) + v // NT
                    pe.wait_ge(head_v, hh + 1)
                    if not (fixed and hh == 0):
                        pe.wait_ge(o_copied, hh)
                pe.wait_ge(exped, U * 2 + 2)
                for q in range(NC):
                    last = nc.tensor.matmul(PS[32 * q:32 * q + 32, 6, :], vslot[:, r, kt, :], EXP[:, v % SLOTS, q * CH:(q + 1) * CH],
                                            start=(kt == 0), stop=(kt == NT - 1))
                last.then_inc(pv, 1)

            def step(u0, v, left=2):
                if left >= 1:
                    scores(u0, v + 1, 1)
                if not (isinstance(u0, int) and u0 + v == 0):
                    values(u0, v - 1)
                if left >= 2:
                    scores(u0, v + 2, 0)

            pe.wait_ge(v_done, 4)
            pe.wait_ge(pads, 5)
            pe.wait_ge(const_rows, 16 * (SLOTS + 1))
            with unbounded(mybir.EngineType.PE, pe, safe_done):
                maxima_tensor(pe)
            scores(0, 0, 0)
            scores(0, 0, 1)
            scores(0, 1, 0)
            for v in range(BODY):
                step(0, v)
            with pe.Fori(1, H // SLOTS) as n:
                for v in range(BODY):
                    step(n, v)
            last = (H // SLOTS) * BODY
            for v in range(NT):
                step(last, v, left=NT - 1 - v)
            values(last, NT - 1)

        def attention_scalar(act):
            def exps(u0, v):
                fixed = isinstance(u0, int)
                U = (u0 if fixed else u0 * BODY) + v
                for half in range(2):
                    g = 2 * v + half
                    act.wait_ge(score, U * 2 + (half + 1))
                    if half == 0 and not (fixed and U < SLOTS):
                        act.wait_ge(pv, U - SLOTS + 1)
                    b = 2 * (g % GB)
                    nc.scalar.activation(EXP[:, v % SLOTS, half * 2 * CH:(half + 1) * 2 * CH].rearrange("p (b n) -> p b n", b=2),
                                         PS[:, b:b + 2, :], ACT.Exp, scale=SCORE_SCALE).then_inc(exped, 1)

            for v in range(BODY):
                exps(0, v)
            with act.Fori(1, H // SLOTS) as n:
                for v in range(BODY):
                    exps(n, v)
            for v in range(NT):
                exps((H // SLOTS) * BODY, v)

        def attention_vector(dve):
            def head_values(h, r):
                if not (isinstance(h, int) and h < SLOTS):
                    dve.wait_ge(pv, (h - SLOTS + 1) * NT)
                cols = slice(HD * h, HD * h + HD) if isinstance(h, int) else bass.ds(h * HD, HD)
                nc.vector.tensor_copy(vslot[:, r, :, 0:HD], V[:, :, cols]).then_inc(head_v, 1)

            def finish(h):
                dve.wait_ge(pv, (h + 1) * NT)
                if not (isinstance(h, int) and h == 0):
                    dve.wait_ge(o_norm, h)
                nc.vector.transpose(Oq[:, :], PS[:, 6, :]).then_inc(o_copied, 1)

            def divide(h):
                cols = slice(HD * h, HD * h + HD) if isinstance(h, int) else bass.ds(h * HD, HD)
                t = Oq[:, :].rearrange("p (c m) -> p c m", m=32)
                dve.wait_ge(o_copied, h + 1)
                nc.vector.reciprocal(denom[:, :], t[:, :, HD]).then_inc(denom_done, 1)
                dve.wait_ge(denom_done, h + 1)
                nc.vector.tensor_tensor(A[:, :, cols], t[:, :, 0:HD], bc(denom[:, :].unsqueeze(2), [P, NT, HD]), ALU.mult).then_inc(o_norm, 1)

            dve.wait_ge(v_done, 4)
            dve.wait_ge(pads, 5)
            for h in range(SLOTS):
                head_values(h, h)
            with unbounded(mybir.EngineType.DVE, dve, safe_done):
                maxima_vector(dve)
            for r in range(SLOTS):
                finish(r)
                divide(r)
                head_values(SLOTS + r, r)
            with dve.Fori(1, H // SLOTS - 1) as n:
                for r in range(SLOTS):
                    finish(n * SLOTS + r)
                    divide(n * SLOTS + r)
                    head_values((n + 1) * SLOTS + r, r)
            for h in range(H - SLOTS - 1, H):
                finish(h)
                divide(h)
                if h == H - SLOTS - 1:
                    head_values(H - 1, 0)

        def project_tensor(pe):
            pe.wait_ge(o_norm, H)
            pe.wait_ge(exped, 2 * H * NT)
            for g in range(4):
                if g >= 2:
                    pe.wait_ge(a_Tc, g - 1)
                for k in range(4):
                    last = nc.tensor.transpose(PS[:, g % 2, k * P:(k + 1) * P], A[:, 4 * g + k, :], ident)
                last.then_inc(a_T, 1)
                if g >= 1:
                    project(pe, g - 1)
            project(pe, 3)

        def project(pe, g):
            pe.wait_ge(a_Tc, g + 1)
            if g >= 2:
                pe.wait_ge(x_attn, g - 1)
            for k in range(4):
                i = 4 * k + g
                last = nc.tensor.matmul(PS[:, 2 + g % 2, k * P:(k + 1) * P], AT[:, i * P:(i + 1) * P], aw[:, AW["wo"], :], start=True, stop=True)
            last.then_inc(proj, 1)

        def project_scalar(act):
            for g in range(4):
                act.wait_ge(a_T, g + 1)
                nc.scalar.copy(AT[:, :].rearrange("p (q c t) -> p c q t", q=4, t=32)[:, 4 * g:4 * g + 4],
                               PS[:, g % 2, :].rearrange("p (c q t) -> p c q t", c=4, t=32)).then_inc(a_Tc, 1)

        def project_vector(dve, g):
            dve.wait_ge(proj, g + 1)
            x = X[:, :, :].rearrange("p (k g) d -> p g k d", g=4)[:, g]
            nc.vector.tensor_tensor(x, PS[:, 2 + g % 2, :].rearrange("p (i d) -> p i d", d=D), x, ALU.add).then_inc(x_attn, 1)

        x_rows = ins["L0_attn_x"][0].rearrange("(p i) d -> p i d", i=NT)
        out_rows = out[0].rearrange("(p i) d -> p i d", i=NT)

        block = ctx.enter_context(nc.Block())

        @block.sync
        def _(sp):
            for q in range(4):
                sp.dma_start(X[:, 4 * q:4 * q + 4, :], x_rows[:, 4 * q:4 * q + 4, :]).then_inc(x_in[q], 16)
            sp.dma_start(cst[:, :], const).then_inc(const_in, 16)
            sp.dma_start(Wr[:, :], ins["L0_ffn_Wr"]).then_inc(wr_in, 16)
            sp.dma_start(Wgu[:, :, 0:F], ins["L0_ffn_Wg"].rearrange("e h i -> h e i")).then_inc(wexp_in, 16)
            sp.dma_start(Wgu[:, :, F:], ins["L0_ffn_Wu"].rearrange("e h i -> h e i")).then_inc(wexp_in, 16)
            for n, (a, w) in enumerate(FCH):
                sp.dma_start(Wd[0:w, :, n, :], ins["L0_ffn_Wd"][:, a:a + w, :].rearrange("e p d -> p e d")).then_inc(wexp_in, 16)
            ffn_sync(sp, S[0], 0)
            attention_sync(sp)
            ffn_sync(sp, S[1], 1)
            for q in range(4):
                x_updated(sp, S[1], q)
                sp.dma_start(out_rows[:, 4 * q:4 * q + 4, :], X[:, 4 * q:4 * q + 4, :]).then_inc(out_done, 16)
            sp.wait_ge(out_done, 64)

        @block.vector
        def _(dve):
            layernorm_vector(dve, S[0].ln, lambda i: dve.wait_ge(x_in[i // 4], 16) if i % 4 == 0 else None)
            dve.wait_ge(const_in, 16)
            nc.vector.tensor_copy(lower_b[:, :], c("lower"))
            nc.vector.tensor_copy(hsum_b[:, :], c("hsum"))
            nc.vector.tensor_copy(ones_b[:, :], c("ones")).then_inc(consts_cast, 1)
            nc.vector.tensor_copy(token_h[:, :], c("token1"))
            nc.vector.tensor_copy(slot_h[:, :, :], bc(c("iota").unsqueeze(2), [P, P, K2 * NT]))
            chain(dve, nc.vector.tensor_copy(tile_h[:, :, :], bc(c("jramp").unsqueeze(2), [P, SLOT_TILES, K2 * NT])))
            route_vector(dve, S[0])
            experts_vector(dve, S[0])
            layernorm_vector(dve, aln, ahead(dve, lambda q: combine_vector(dve, S[0], q), lambda q: x_updated(dve, S[0], q)))
            prepare_vector(dve)
            attention_vector(dve)
            dve.wait_ge(bias_o, 1)
            layernorm_vector(dve, S[1].ln, ahead(dve, lambda g: project_vector(dve, g), lambda g: dve.wait_ge(x_attn, g + 1)),
                             [4 * k + g for g in range(4) for k in range(4)])
            route_vector(dve, S[1])
            experts_vector(dve, S[1])
            for q in range(4):
                combine_vector(dve, S[1], q)

        @block.scalar
        def _(act):
            layernorm_scalar(act, S[0].ln)
            route_scalar(act, S[0])
            act.dma_start(cosT[:, :], rope_cos).then_inc(rope_in, 16)
            act.dma_start(sinT[:, :], rope_sin).then_inc(rope_in, 16)
            act.dma_start(aw[:, :, :], attn_w).then_inc(aw_in, 16)
            act.dma_start(ab[:, :], attn_b).then_inc(aw_in, 16)
            act.dma_start(bv_rows[:, :], attn_rows[0:1, :].to_broadcast([P, D])).then_inc(aw_in, 16)
            act.dma_start(bo_rows[:, :], attn_rows[1:2, :].to_broadcast([P, D])).then_inc(aw_in, 16)
            experts_scalar(act, S[0])
            combine_scalar(act, S[0])
            layernorm_scalar(act, aln)
            prepare_scalar(act)
            attention_scalar(act)
            project_scalar(act)
            layernorm_scalar(act, S[1].ln)
            route_scalar(act, S[1])
            experts_scalar(act, S[1])
            combine_scalar(act, S[1])

        @block.tensor
        def _(pe):
            pe.wait_ge(pads, 2)
            pe.wait_ge(x_in[3], 16)
            keep_warm(9)
            pe.wait_ge(const_in, 16)
            pe.wait_ge(wr_in, 16)
            layernorm_tensor(pe, S[0].ln, lambda g: route_logits(pe, S[0], g))
            route_tensor(pe, S[0])
            experts_tensor(pe, S[0])
            pe.wait_ge(S[0].xq, 3)
            keep_warm(22)
            layernorm_tensor(pe, aln, lambda g: prepare_first(pe, g))
            prepare_tensor(pe)
            attention_tensor(pe)
            project_tensor(pe)
            keep_warm(28)
            layernorm_tensor(pe, S[1].ln, lambda g: route_logits(pe, S[1], g))
            route_tensor(pe, S[1])
            experts_tensor(pe, S[1])

        @block.gpsimd
        def _(pool):
            pads_gpsimd(pool)
            layernorm_gpsimd(pool, S[0].ln)
            experts_gpsimd(pool, S[0], 0)
            combine_gpsimd(pool, S[0])
            layernorm_gpsimd(pool, aln)
            prepare_gpsimd(pool)
            pool.wait_ge(aln.xn, NT - len(POOL_TILES))
            nc.gpsimd.tensor_tensor(X[:, :, :], X[:, :, :], bc(bo_rows[:, :].unsqueeze(1), [P, NT, D]), ALU.add).then_inc(bias_o, 1)
            layernorm_gpsimd(pool, S[1].ln)
            experts_gpsimd(pool, S[1], 1)
            combine_gpsimd(pool, S[1])


def kernel(**inputs):
    import concourse.bacc as bacc
    from concourse.bass_utils import run_bass_kernel_spmd

    nc = bacc.Bacc("TRN2", target_bir_lowering=False, num_devices=1)
    arrays = {}

    def given(name, a):
        arrays[name] = np.ascontiguousarray(a)
        return nc.dram_tensor(name, arrays[name].shape, F32, kind="ExternalInput").ap()

    ins = {n: given("in_" + n, inputs[n]) for n in ("L0_attn_x", "L0_ffn_Wr", "L0_ffn_Wg", "L0_ffn_Wu", "L0_ffn_Wd")}
    weights, biases, rows = pack_attention({n: a for n, a in inputs.items() if n.startswith("L0_attn_") and n != "L0_attn_x"})
    cos, sin = rope_arrays()
    out = nc.dram_tensor("out", (1, T, D), F32, kind="ExternalOutput").ap()
    macaron_block(nc, ins, given("const", constant_array()), given("rope_cos", cos), given("rope_sin", sin),
                  given("attn_w", weights), given("attn_b", biases), given("attn_rows", rows), out)
    return run_bass_kernel_spmd(nc, [arrays], core_ids=[0]).results[0]["out"]
```

```python
from contextlib import ExitStack

import numpy as np

import concourse.bass as bass
from concourse import mybir

F32 = mybir.dt.float32
F16 = mybir.dt.float16
BF16 = mybir.dt.bfloat16
I32 = mybir.dt.int32
ALU = mybir.AluOpType
ACT = mybir.ActivationFunctionType
AX = mybir.AxisListType

P = 128
T = 2048
D = 128
NT = T // P
E = 9
F = 352
K2 = 2
SLOT_TILES = (K2 * T + E * (P - 1)) // P
LATE = 4
FCH = [(0, 128), (128, 128), (256, 96)]
HC = len(FCH)
LN_EPS = 1e-5
SCORE_SAFE = 60.0
RING = 4
NO_ROW = K2 * T
SECOND, FIRST = 0, 1
ROUND = 1.5 * P * 2.0 ** 23
POOL_TILES = (3, 7, 11)

H = 16
HD = 8
DQ = 64
ROPE_BASE = 10000.0
SCORE_SCALE = float(1.0 / np.sqrt(np.float32(H + 64 + DQ)))
CH = 512
NC = T // CH
PARTS = 3
ROWS = PARTS * PARTS * HD
SHIFT_ROW = ROWS
KR = 96
SLOTS = 3
FOLDED = ["uq", "qr", "qrs", "uk"]
GB = 3
AW = {n: i for i, n in enumerate(["ct", "uq", "qr", "qrs", "uk", "kr", "krs", "uv", "wo"])}
AB = {n: i for i, n in enumerate(["ct", "uq", "qr", "qrs", "uk", "kr", "krs"])}

CONST_COLS = {}
_at = 0
for _n, _w in [("ident", P), ("lower", P), ("ones", P), ("iota", P), ("emark", E), ("jstart", SLOT_TILES),
               ("tri", E * E), ("token1", K2 * NT), ("hsum", 2 * 32)]:
    CONST_COLS[_n] = (_at, _w)
    _at += _w
CONST_W = _at


def constant_array():
    c = np.zeros((P, CONST_W), np.float32)

    def put(name, value):
        a, w = CONST_COLS[name]
        c[:, a:a + w] = value

    p = np.arange(P)
    put("ident", np.eye(P))
    put("lower", (p[:, None] < p[None, :]))
    put("ones", 1.0)
    put("iota", p[None, :])
    put("emark", np.arange(E)[None, :] - E)
    put("jstart", P * np.arange(SLOT_TILES)[None, :])
    e = np.arange(E)
    put("tri", (e[None, :] < e[:, None]).reshape(1, -1))
    put("token1", np.tile(NT * p[:, None] + np.arange(NT)[None, :] + 1, (1, K2)))
    head = (p[:, None] // HD == np.arange(H)[None, :])
    none = np.zeros((P, H))
    put("hsum", np.concatenate([head, none, none, head], axis=1))
    return c


def rope_arrays():
    ids = np.arange(D // 2, dtype=np.float32)
    theta = (np.float32(ROPE_BASE) ** (np.float32(-2.0) * ids) / np.float32(D // 2)).astype(np.float32)
    col = np.arange(T)
    pos = (NT * (col % P) + col // P).astype(np.float32)
    r = (pos[None, :] * np.repeat(theta, 2)[:, None]).astype(np.float32)
    sign = np.where(np.arange(D) % 2 == 0, -1.0, 1.0)[:, None]
    return np.cos(r).astype(np.float32), (sign * np.sin(r)).astype(np.float32)


def pack_attention(g):
    def at(w, row):
        full = np.zeros((P, D), np.float32)
        full[row:row + w.shape[0]] = w
        return full

    def swap(w):
        return w.reshape(w.shape[:-1] + (D // 2, 2))[..., ::-1].reshape(w.shape)

    g = {n.replace("L0_attn_", ""): np.asarray(v) for n, v in g.items()}
    w = [np.concatenate([g["Wd_q_w"], g["Wd_kv_w"]], axis=1), at(g["Wu_q_w"], 0), at(g["Wq_r_w"], 0), at(swap(g["Wq_r_w"]), 0),
         at(g["Wu_k_w"], DQ), g["Wk_r_w"], swap(g["Wk_r_w"]), at(g["Wu_v_w"], DQ), g["Wo_w"]]
    b = [np.concatenate([g["Wd_q_b"], g["Wd_kv_b"]]), g["Wu_q_b"], g["Wq_r_b"], swap(g["Wq_r_b"]),
         g["Wu_k_b"], g["Wk_r_b"], swap(g["Wk_r_b"])]
    return (np.ascontiguousarray(np.stack(w, axis=1)), np.ascontiguousarray(np.stack(b, axis=1)),
            np.ascontiguousarray(np.stack([g["Wu_v_b"], g["Wo_b"]])))


def macaron_block(nc, ins, const, rope_cos, rope_sin, attn_w, attn_b, attn_rows, out):
    with ExitStack() as ctx:
        def sb(name, shape, dt):
            return ctx.enter_context(nc.sbuf_tensor(name, shape, dt))

        def sem(name):
            return ctx.enter_context(nc.semaphore(name))

        def dram(name, shape, dt):
            return nc.dram_tensor(name, shape, dt, kind="Internal").ap()

        cst = sb("cst", [P, CONST_W], F32)
        X = sb("X", [P, NT, D], F32)
        XN = sb("XN", [P, NT, D], F32)
        XNT = sb("XNT", [P, T], F32)
        Wr = sb("Wr", [P, E], F32)
        Wgu = sb("Wgu", [P, E, 2 * F], F32)
        Wd = sb("Wd", [P, E, 3, D], F32)
        stats = sb("stats", [P, NT, 6], F32)
        mv = sb("mv", [P, NT, 2], F32)
        var = sb("var", [P, NT], F32)
        rstd = sb("rstd", [P, NT], F32)
        newt = sb("newt", [P, NT], F32)
        lower_b = sb("lower_b", [P, P], BF16)
        ones_b = sb("ones_b", [P, P], BF16)
        slot_h = sb("slot_h", [P, P, K2 * NT], F16)
        tile_h = sb("tile_h", [P, SLOT_TILES, K2 * NT], F16)
        token_h = sb("token_h", [P, K2 * NT], F16)
        place_h = sb("place_h", [P, 2, K2 * NT], F16)
        row_any = sb("row_any", [P, SLOT_TILES], F32)
        row_1st = sb("row_1st", [P, SLOT_TILES], F32)
        row_none = sb("row_none", [P, SLOT_TILES], F32)
        eps = sb("eps", [P, 1], F32)
        marker = sb("marker", [P, 1], F32)
        warm = sb("warm", [P, 1], F32)
        zeros_b = sb("zeros_b", [P, CH], BF16)
        L = sb("L", [P, NT, E], F32)
        tmpE = sb("tmpE", [P, K2, NT, E], F32)
        pick = sb("pick", [P, K2, NT, E], F32)
        top = sb("top", [P, K2, NT], F32)
        first = sb("first", [P, K2, NT], F32)
        both = sb("both", [P, NT, E], BF16)
        wts = sb("wts", [P, K2, NT], F32)
        tot = sb("tot", [P, E], F32)
        room = sb("room", [P, E], F32)
        tri_p = sb("tri_p", [P, E, E], F32)
        start = sb("start", [P, E], F32)
        end = sb("end", [P, E], F32)
        passed = sb("passed", [P, SLOT_TILES, E], F32)
        texp = sb("texp", [P, SLOT_TILES], F32)
        woff = sb("woff", [P, 2, SLOT_TILES], I32)
        slot = sb("slot", [P, NT, E], F32)
        pos = sb("pos", [P, K2 * NT], F32)
        first_slot = sb("first_slot", [P, K2 * NT], F32)
        OA = sb("OA", [P, SLOT_TILES, K2 * NT], F16)
        idx = sb("idx", [P, 2, SLOT_TILES], I32)
        few = sb("few", [P, 1], I32)
        xg = sb("xg", [P, RING, D], F32)
        xgT = sb("xgT", [P, 2, P], F32)
        sg = sb("sg", [P, 2, HC * P], F32)
        hidT = sb("hidT", [P, 2, HC, P], F32)
        wcur = sb("wcur", [P, 2, 2, HC * P], F32)
        yt = sb("yt", [P, RING, D], F32)
        shared = sb("shared", [P, SLOTS * T], F32)
        Y = shared[:, 0:K2 * T].rearrange("p (k i d) -> p k i d", k=K2, d=D)
        OB = shared[:, K2 * T:].bitcast(F16).rearrange("p (q n) -> p q n", q=P)
        temp = shared[:, 0:8 * CH].rearrange("p (a b n) -> p a b n", a=4, b=2)
        EXP = shared[:, :].rearrange("p (b n) -> p b n", n=T)
        cosT = sb("cosT", [P, T], F32)
        sinT = sb("sinT", [P, T], F32)
        aw = sb("aw", [P, len(AW), D], F32)
        ab = sb("ab", [P, len(AB)], F32)
        bv_rows = sb("bv_rows", [P, D], F32)
        bo_rows = sb("bo_rows", [P, D], F32)
        ctT = sb("ctT", [P, P], F32)
        bct = sb("bct", [P, P], F32)
        parts = wcur[:, :, :, :].rearrange("p b g n -> p (b g n)").bitcast(BF16).rearrange("p (b a n) -> p b a n", b=2, a=PARTS)
        V = sb("V", [P, NT, D], F32)
        qslot = sb("qslot", [P, SLOTS, T], BF16)
        kslot = sb("kslot", [P, SLOTS, T], BF16)
        vslot = sb("vslot", [P, SLOTS, NT, 32], F32)
        square_b = sb("square_b", [P, 2, CH], BF16)
        hsum_b = sb("hsum_b", [P, 2 * 32], BF16)
        nmax = sb("nmax", [P, 1], F32)
        nrow = sb("nrow", [1, 2 * H], F32)
        bound = sb("bound", [1, H], F32)
        largest = sb("largest", [1, 1], F32)
        safe = sb("safe", [1, 1], I32)
        smax = sb("smax", [P, 2, P], F32)
        snext = sb("snext", [P, 2, P], F32)
        sparts = sb("sparts", [P, PARTS, 2, P], BF16)
        zeros48 = sb("zeros48", [PARTS * H, P], BF16)
        Oq = sb("Oq", [P, CH], F32)
        denom = sb("denom", [P, NT], F32)
        A = XN
        AT = XNT

        PS = ctx.enter_context(nc.psum_tensor("PS", [P, 8, CH], F32))

        xn_dram = [dram(f"xn_dram{f}", [T, D], F32) for f in range(2)]
        k_dram = dram("k_dram", [P, PARTS, T], BF16)
        q_dram = dram("q_dram", [H, PARTS, HD, T], BF16)
        shift_dram = dram("shift_dram", [PARTS, H, T], BF16)
        y_dram = [dram(f"y_dram{f}", [K2 * T, D], F32) for f in range(2)]

        def c(name):
            a, w = CONST_COLS[name]
            return cst[:, a:a + w]

        ident = c("ident")

        const_in = sem("const_in")
        x_in = [sem(f"x_in{q}") for q in range(4)]
        denom_done = sem("denom_done")
        wr_in = sem("wr_in")
        wexp_in = sem("wexp_in")
        consts_cast = sem("consts_cast")
        vstep = sem("vstep")

        class LnSems:
            def __init__(self, n):
                self.var = sem(f"{n}_var")
                self.sd = sem(f"{n}_sd")
                self.rstd = sem(f"{n}_rstd")
                self.xn = sem(f"{n}_xn")
                self.xn4 = sem(f"{n}_xn4")
                self.T = sem(f"{n}_T")
                self.xnT = sem(f"{n}_xnT")

        PIECES = 8
        PT = NT // PIECES
        y_in = [sem(f"y_in{q}") for q in range(PIECES)]

        class FfnSems:
            def __init__(self, n):
                self.ln = LnSems(n)
                self.xn_out = sem(f"{n}_xn_out")
                self.logits = sem(f"{n}_logits")
                self.top2 = sem(f"{n}_top2")
                self.exp2 = sem(f"{n}_exp2")
                self.both = sem(f"{n}_both")
                self.ranks = sem(f"{n}_ranks")
                self.woff = sem(f"{n}_woff")
                self.onehot = sem(f"{n}_onehot")
                self.slots = sem(f"{n}_slots")
                self.idx = sem(f"{n}_idx")
                self.wts = sem(f"{n}_wts")
                self.z = sem(f"{n}_z")
                self.xg = [sem(f"{n}_xg{s}") for s in range(RING)]
                self.xgT_ps = sem(f"{n}_xgT_ps")
                self.xgT = sem(f"{n}_xgT")
                self.wcur = sem(f"{n}_wcur")
                self.gate = sem(f"{n}_gate")
                self.up = sem(f"{n}_up")
                self.silu = sem(f"{n}_silu")
                self.hid = sem(f"{n}_hid")
                self.y_ps = sem(f"{n}_y_ps")
                self.y = sem(f"{n}_y")
                self.y_out = [sem(f"{n}_y_out{s}") for s in range(RING)]
                self.y_done = sem(f"{n}_y_done")
                self.y_in = y_in
                self.x1 = sem(f"{n}_x1")
                self.xq = sem(f"{n}_xq")
                self.x_last = sem(f"{n}_x_last")

        S = [FfnSems("f0"), FfnSems("f1")]
        aln = LnSems("ln_a")
        rope_in = sem("rope_in")
        aw_in = sem("aw_in")
        bct_done = sem("bct_done")
        fold_ps = sem("fold_ps")
        fold_b = sem("fold_b")
        folded = sem("folded")
        rot_ps = sem("rot_ps")
        lin_ps = sem("lin_ps")
        mixed = sem("mixed")
        full_q = sem("full_q")
        part0 = sem("part0")
        rest1 = sem("rest1")
        last_unit = sem("last_unit")
        part1 = sem("part1")
        part2 = sem("part2")
        square = sem("square")
        norms = sem("norms")
        parts_out = [sem(f"parts_out{b}") for b in range(2)]
        v_ps = sem("v_ps")
        v_done = sem("v_done")
        pads = sem("pads")
        nmax_done = sem("nmax_done")
        nmax_T = sem("nmax_T")
        safe_done = sem("safe_done")
        const_rows = sem("const_rows")
        shift_in = [sem(f"shift_in{r}") for r in range(SLOTS)]
        m_head = sem("m_head")
        m_score = sem("m_score")
        m_max = sem("m_max")
        m_T = sem("m_T")
        m_step = sem("m_step")
        m_out = sem("m_out")
        head_in = [sem(f"head_in{r}") for r in range(SLOTS)]
        first_q = sem("first_q")
        first_k = sem("first_k")
        head_v = sem("head_v")
        score = sem("score")
        exped = sem("exped")
        pv = sem("pv")
        o_copied = sem("o_copied")
        o_norm = sem("o_norm")
        bias_o = sem("bias_o")
        a_T = sem("a_T")
        a_Tc = sem("a_Tc")
        proj = sem("proj")
        x_attn = sem("x_attn")
        out_done = sem("out_done")
        vcount = [0]

        def chain(dve, inst):
            inst.then_inc(vstep, 1)
            vcount[0] += 1
            dve.wait_ge(vstep, vcount[0])

        def layernorm_vector(dve, s, x_ready, order=range(NT)):
            for n, i in enumerate(order):
                x_ready(n)
                last = nc.vector.bn_stats(stats[:, i, :], X[:, i, :])
            chain(dve, last)
            for i in range(NT):
                last = nc.vector.bn_aggr(mv[:, i, :], stats[:, i, :])
            last.then_inc(s.var, 1)
            dve.wait_ge(s.var, 1)
            nc.vector.tensor_scalar(var[:, :], mv[:, :, 1], LN_EPS, None, ALU.add)
            dve.wait_ge(s.sd, 1)
            chain(dve, nc.vector.reciprocal(rstd[:, :], newt[:, :]))
            chain(dve, nc.vector.tensor_tensor(newt[:, :], rstd[:, :], rstd[:, :], ALU.mult))
            chain(dve, nc.vector.tensor_tensor(newt[:, :], newt[:, :], var[:, :], ALU.mult))
            chain(dve, nc.vector.tensor_scalar(newt[:, :], newt[:, :], -0.5, 1.5, ALU.mult, ALU.add))
            nc.vector.tensor_tensor(rstd[:, :], rstd[:, :], newt[:, :], ALU.mult).then_inc(s.rstd, 1)
            dve.wait_ge(s.rstd, 1)
            for i in range(NT):
                if i not in POOL_TILES:
                    nc.vector.tensor_scalar(XN[:, i, :], X[:, i, :], mv[:, i, 0:1], rstd[:, i:i + 1],
                                            ALU.subtract, ALU.mult).then_inc(s.xn, 1)

        def layernorm_gpsimd(pool, s):
            pool.wait_ge(s.rstd, 1)
            for i in POOL_TILES:
                nc.gpsimd.tensor_scalar(XN[:, i, :], X[:, i, :], mv[:, i, 0:1], rstd[:, i:i + 1],
                                        ALU.subtract, ALU.mult).then_inc(s.xn4, 1)

        def layernorm_scalar(act, s):
            act.wait_ge(s.var, 1)
            nc.scalar.activation(newt[:, :], mv[:, :, 1], ACT.Sqrt, bias=eps[:, :]).then_inc(s.sd, 1)
            for g in range(4):
                act.wait_ge(s.T, g + 1)
                nc.scalar.copy(XNT[:, g * CH:(g + 1) * CH], PS[:, g % 2, :]).then_inc(s.xnT, 1)

        def keep_warm(count, bank=7):
            for _ in range(count):
                nc.tensor.matmul(PS[:, bank, :], zeros_b[:, 0:P], zeros_b[:, :], start=True, stop=True)

        def layernorm_tensor(pe, s, behind=None):
            for g in range(4):
                if g >= 2:
                    pe.wait_ge(s.xnT, g - 1)
                for k in range(4):
                    if 4 * g + k in POOL_TILES:
                        pe.wait_ge(s.xn4, g + 1)
                    else:
                        pe.wait_ge(s.xn, 3 * g + k + 1)
                    last = nc.tensor.transpose(PS[:, g % 2, k * P:(k + 1) * P], XN[:, 4 * g + k, :], ident)
                last.then_inc(s.T, 1)
                if behind and g >= 1:
                    behind(g - 1)
            if behind:
                behind(3)

        def bc(ap, shape):
            return ap.to_broadcast(shape)

        def route_vector(dve, s):
            dve.wait_ge(s.logits, 1)
            logits = PS[:, 2, 0:NT * E].rearrange("p (i e) -> p i e", e=E)
            for k in range(K2):
                src = (logits, L[:, :, :])[k]
                chain(dve, nc.vector.tensor_reduce(top[:, k, :], src, AX.X, ALU.max))
                chain(dve, nc.vector.tensor_tensor(tmpE[:, k], src, bc(top[:, k, :].unsqueeze(2), [P, NT, E]), ALU.is_equal))
                chain(dve, nc.vector.tensor_tensor(tmpE[:, k], tmpE[:, k], bc(c("emark").unsqueeze(1), [P, NT, E]), ALU.mult))
                chain(dve, nc.vector.tensor_reduce(first[:, k, :], tmpE[:, k], AX.X, ALU.min))
                chain(dve, nc.vector.tensor_tensor(pick[:, k], bc(c("emark").unsqueeze(1), [P, NT, E]),
                                                   bc(first[:, k, :].unsqueeze(2), [P, NT, E]), ALU.is_equal))
                if k == 0:
                    chain(dve, nc.vector.scalar_tensor_tensor(L[:, :, :], pick[:, 0], -3.0e38, logits, ALU.mult, ALU.add))
            nc.vector.tensor_tensor(both[:, :, :], pick[:, 0], pick[:, 1], ALU.add).then_inc(s.both, 1)
            nc.vector.tensor_tensor(wts[:, 1, :], top[:, 1, :], top[:, 0, :], ALU.subtract).then_inc(s.top2, 1)
            dve.wait_ge(s.ranks, 1)
            chain(dve, nc.vector.tensor_reduce(tot[:, :], PS[:, 4, 0:NT * E].rearrange("p (i e) -> p e i", e=E), AX.X, ALU.add))
            chain(dve, nc.vector.tensor_scalar(room[:, :], tot[:, :], (P - 1) / 2, ROUND, ALU.add, ALU.add))
            chain(dve, nc.vector.tensor_scalar(room[:, :], room[:, :], -ROUND, None, ALU.add))
            chain(dve, nc.vector.tensor_tensor(tri_p[:, :, :], c("tri").rearrange("p (a b) -> p a b", b=E),
                                               bc(room[:, :].unsqueeze(1), [P, E, E]), ALU.mult))
            chain(dve, nc.vector.tensor_reduce(start[:, :], tri_p[:, :, :], AX.X, ALU.add))
            nc.vector.tensor_tensor(end[:, :], start[:, :], room[:, :], ALU.add)
            chain(dve, nc.vector.tensor_tensor(slot[:, :, :], PS[:, 3, 0:NT * E].rearrange("p (i e) -> p i e", e=E),
                                               bc(start[:, :].unsqueeze(1), [P, NT, E]), ALU.add))
            chain(dve, nc.vector.tensor_tensor(tmpE[:, :, :, :].rearrange("p k i e -> p k (i e)"), pick[:, :, :, :].rearrange("p k i e -> p k (i e)"),
                                               bc(slot[:, :, :].rearrange("p i e -> p (i e)").unsqueeze(1), [P, K2, NT * E]), ALU.mult))
            chain(dve, nc.vector.tensor_reduce(pos[:, :], tmpE[:, :, :, :].rearrange("p k i e -> p (k i) e"), AX.X, ALU.add))
            chain(dve, nc.vector.tensor_scalar(first_slot[:, :], pos[:, :], -(P - 1) / 2, ROUND, ALU.add, ALU.add))
            chain(dve, nc.vector.tensor_scalar(place_h[:, 0, :], first_slot[:, :], -ROUND, None, ALU.add))
            nc.vector.tensor_tensor(place_h[:, 1, :], pos[:, :], place_h[:, 0, :], ALU.subtract)
            n = K2 * NT
            chain(dve, nc.vector.tensor_tensor(OA[:, :, :], tile_h[:, :, :], bc(place_h[:, 0:1, :], [P, SLOT_TILES, n]), ALU.is_equal))
            nc.vector.tensor_tensor(OA[:, :, :], OA[:, :, :], bc(token_h[:, :].unsqueeze(1), [P, SLOT_TILES, n]), ALU.mult)
            for g in range(K2):
                q = slice(g * NT, (g + 1) * NT)
                nc.vector.tensor_tensor(OB[:, :, q], slot_h[:, :, q], bc(place_h[:, 1:2, q], [P, P, NT]), ALU.is_equal).then_inc(s.onehot, 1)
            dve.wait_ge(s.slots, 1)
            row_0 = PS[:, 5, 0:SLOT_TILES]
            chain(dve, nc.vector.tensor_reduce(row_any[:, :], PS[:, 5, 0:K2 * SLOT_TILES].rearrange("p (k t) -> p t k", k=K2), AX.X, ALU.add))
            nc.vector.tensor_scalar(idx[:, 0, :], row_any[:, :], -1.0, 0.0, ALU.add, ALU.max).then_inc(s.idx, 1)
            chain(dve, nc.vector.tensor_tensor(passed[:, :, :], bc(end[:, :].unsqueeze(1), [P, SLOT_TILES, E]),
                                               bc(c("jstart").unsqueeze(2), [P, SLOT_TILES, E]), ALU.is_le))
            chain(dve, nc.vector.tensor_reduce(texp[:, :], passed[:, :, :], AX.X, ALU.add))
            nc.vector.tensor_scalar(few[:, :], end[:, E - 1:E], float((SLOT_TILES - LATE) * P), None, ALU.is_le)
            nc.vector.tensor_scalar(woff[:, 0, :], texp[:, :], float(E - 1), float(2 * F), ALU.min, ALU.mult)
            nc.vector.tensor_scalar(woff[:, 1, :], texp[:, :], float(E - 1), float(3 * D), ALU.min, ALU.mult).then_inc(s.woff, 1)
            nc.vector.tensor_scalar(row_1st[:, :], row_0, 0.0, float(T), ALU.is_gt, ALU.mult)
            chain(dve, nc.vector.tensor_scalar(row_none[:, :], row_any[:, :], 0.0, float(NO_ROW + 1), ALU.is_equal, ALU.mult))
            chain(dve, nc.vector.tensor_tensor(row_1st[:, :], row_1st[:, :], row_any[:, :], ALU.add))
            nc.vector.scalar_tensor_tensor(idx[:, 1, :], row_none[:, :], -1.0, row_1st[:, :], ALU.add, ALU.add).then_inc(s.idx, 1)
            dve.wait_ge(s.exp2, 1)
            chain(dve, nc.vector.tensor_scalar(wts[:, 0, :], wts[:, 1, :], 1.0, None, ALU.add))
            chain(dve, nc.vector.reciprocal(wts[:, 0, :], wts[:, 0, :]))
            chain(dve, nc.vector.tensor_scalar(wts[:, 0, :], wts[:, 0, :], 0.5, None, ALU.mult))
            nc.vector.tensor_tensor(wts[:, 1, :], wts[:, 1, :], wts[:, 0, :], ALU.mult).then_inc(s.wts, 1)

        def route_scalar(act, s):
            act.wait_ge(s.top2, 1)
            nc.scalar.activation(wts[:, 1, :], wts[:, 1, :], ACT.Exp).then_inc(s.exp2, 1)
            act.wait_ge(pads, 1)
            nc.scalar.activation(warm[:, :], warm[:, :], ACT.Silu)

        def route_logits(pe, s, g):
            pe.wait_ge(s.ln.xnT, g + 1)
            for i in range(4 * g, 4 * g + 4):
                last = nc.tensor.matmul(PS[:, 2, i * E:(i + 1) * E], XNT[:, i * P:(i + 1) * P], Wr[:, :], start=True, stop=True)
            if g == 3:
                last.then_inc(s.logits, 1)

        def route_tensor(pe, s):
            pe.wait_ge(s.both, 1)
            m = both[:, :, :].rearrange("p i e -> p (i e)")
            nc.tensor.matmul(PS[:, 4, 0:NT * E], ones_b[:, :], m, start=True, stop=True)
            nc.tensor.matmul(PS[:, 3, 0:NT * E], lower_b[:, :], m, start=True, stop=False)
            for d in range(1, NT):
                last = nc.tensor.matmul(PS[:, 3, d * E:NT * E], ones_b[:, :], m[:, 0:(NT - d) * E], start=False, stop=(d == NT - 1))
            last.then_inc(s.ranks, 1)
            n = K2 * NT
            for q in range(n):
                k = q // NT
                if q % NT == 0:
                    pe.wait_ge(s.onehot, k + 1)
                last = nc.tensor.matmul(PS[:, 5, k * SLOT_TILES:(k + 1) * SLOT_TILES], OB[:, :, q], OA[:, :, q],
                                        start=(q % NT == 0), stop=(q % NT == NT - 1))
            last.then_inc(s.slots, 1)
            keep_warm(10)

        def load_offset(engine, which, j):
            return nc.values_load(woff[0:1, which, j:j + 1] if isinstance(j, int) else woff[0:1, which, bass.ds(j, 1)],
                                  engines=[engine], min_val=0, max_val=(E - 1) * (2 * F, 3 * D)[which],
                                  skip_runtime_bounds_check_because="the offset was clamped to the last expert's")

        MAIN_TILES = SLOT_TILES - LATE

        def load_few(engine):
            return nc.values_load(few[0:1, 0:1], engines=[engine], min_val=0, max_val=1,
                                  skip_runtime_bounds_check_because="a comparison's result")

        def tile_transpose_x(pe, s, j, r):
            pe.wait_ge(s.xg[r % RING], (j - r % RING) * (16 // RING) + 16)
            nc.tensor.transpose(PS[:, 0, 0:P], xg[:, r % RING, :], ident).then_inc(s.xgT_ps, 1)

        def tile_gate_up(pe, s, j, r):
            pe.wait_ge(s.wcur, j + 1)
            pe.wait_ge(s.xgT, j + 1)
            for bank, half, done in ((GATE_BANK[r % 2], 0, s.gate), (UP_BANK[r % 2], 1, s.up)):
                for n in range(HC):
                    last = nc.tensor.matmul(PS[:, bank, n * P:(n + 1) * P], wcur[:, r % 2, half, n * P:(n + 1) * P], xgT[:, r % 2, :],
                                            start=True, stop=True)
                last.then_inc(done, 1)

        def tile_down(pe, s, j, r, off):
            wd = Wd[:, :, :, :].rearrange("p e n d -> p (e n d)")
            pe.wait_ge(s.hid, j + 1)
            for n, (a, w) in enumerate(FCH):
                last = nc.tensor.matmul(PS[:, Y_BANK[r % 2], 0:D], hidT[0:w, r % 2, n, :], wd[0:w, bass.ds(off + n * D, D)],
                                        start=(n == 0), stop=(n == HC - 1))
            last.then_inc(s.y_ps, 1)

        GATE_BANK, UP_BANK, Y_BANK = (1, 6), (2, 7), (3, 4)

        def experts_tensor(pe, s):
            pe.wait_ge(s.woff, 1)
            tile_transpose_x(pe, s, 0, 0)
            pe.wait_ge(wexp_in, 5 * 16)
            tile_gate_up(pe, s, 0, 0)
            tile_transpose_x(pe, s, 1, 1)

            def tile(j, r, more=2):
                down = load_offset(mybir.EngineType.PE, 1, j)
                if more >= 1:
                    tile_gate_up(pe, s, j + 1, r + 1)
                if more >= 2:
                    tile_transpose_x(pe, s, j + 2, r + 2)
                tile_down(pe, s, j, r, down)

            STEP = 2 * RING
            with pe.Fori(0, MAIN_TILES // STEP) as n:
                for r in range(STEP):
                    tile(n * STEP + r, r)
            for j in range(MAIN_TILES // STEP * STEP, MAIN_TILES):
                tile(j, j % STEP, more=2 if j + 1 < MAIN_TILES else 0)
            with pe.If(load_few(mybir.EngineType.PE) == 0):
                tile_gate_up(pe, s, MAIN_TILES, MAIN_TILES)
                tile_transpose_x(pe, s, MAIN_TILES + 1, MAIN_TILES + 1)
                for j in range(MAIN_TILES, SLOT_TILES):
                    tile(j, j % STEP, more=min(2, SLOT_TILES - 1 - j))

        def experts_scalar(act, s):
            def copy_x(j, r):
                act.wait_ge(s.xgT_ps, j + 1)
                if not (isinstance(j, int) and j < 2):
                    act.wait_ge(s.up, j - 1)
                nc.scalar.copy(xgT[:, r % 2, :], PS[:, 0, 0:P]).then_inc(s.xgT, 1)

            def silu(j, r):
                act.wait_ge(s.gate, j + 1)
                if not (isinstance(j, int) and j < 2):
                    act.wait_ge(s.hid, j - 1)
                nc.scalar.activation(sg[:, r % 2, :], PS[:, GATE_BANK[r % 2], 0:HC * P], ACT.Silu).then_inc(s.silu, 1)

            def tile(j, r, more=2):
                if more >= 1:
                    silu(j + 1, r + 1)
                if more >= 2:
                    copy_x(j + 2, r + 2)
                act.wait_ge(s.y_ps, j + 1)
                if not (isinstance(j, int) and j < RING):
                    act.wait_ge(s.y_out[r % RING], (j - r) * (16 // RING))
                nc.scalar.copy(yt[:, r % RING, :], PS[:, Y_BANK[r % 2], 0:D]).then_inc(s.y, 1)

            copy_x(0, 0)
            silu(0, 0)
            copy_x(1, 1)
            for r in range(RING):
                tile(r, r)
            with act.Fori(1, MAIN_TILES // RING - 1) as n:
                for r in range(RING):
                    tile(n * RING + r, r)
            for j in range(MAIN_TILES - RING, MAIN_TILES):
                tile(j, j % RING, more=2 if j + 1 < MAIN_TILES else 0)
            act.wait_ge(s.woff, 1)
            with act.If(load_few(mybir.EngineType.Activation) == 0):
                silu(MAIN_TILES, MAIN_TILES)
                copy_x(MAIN_TILES + 1, MAIN_TILES + 1)
                for j in range(MAIN_TILES, SLOT_TILES):
                    tile(j, j % RING, more=min(2, SLOT_TILES - 1 - j))

        def experts_vector(dve, s):
            def mult(j, r):
                dve.wait_ge(s.up, j + 1)
                dve.wait_ge(s.silu, j + 1)
                nc.vector.tensor_tensor(hidT[:, r % 2, :, :].rearrange("p n t -> p (n t)"), PS[:, UP_BANK[r % 2], 0:HC * P],
                                        sg[:, r % 2, :], ALU.mult).then_inc(s.hid, 1)

            def copy_weights(j, r):
                off = load_offset(mybir.EngineType.DVE, 0, j)
                w = Wgu[:, :, :].rearrange("p e n -> p (e n)")
                nc.vector.tensor_copy(wcur[:, r % 2, :, 0:F], w[:, bass.ds(off, 2 * F)].rearrange("p (g n) -> p g n", g=2)).then_inc(s.wcur, 1)

            nc.vector.memset(wcur[:, :, :, F:], 0.0)
            dve.wait_ge(s.woff, 1)
            dve.wait_ge(wexp_in, 5 * 16)
            for r in range(2):
                copy_weights(r, r)
            with dve.Fori(0, MAIN_TILES // 2) as n:
                for r in range(2):
                    mult(n * 2 + r, r)
                    copy_weights(n * 2 + (r + 2), r)
            with dve.If(load_few(mybir.EngineType.DVE) == 0):
                for j in range(MAIN_TILES, SLOT_TILES):
                    mult(j, j % 2)
                    if j + 2 < SLOT_TILES:
                        copy_weights(j + 2, j % 2)

        def experts_gpsimd(pool, s, f):
            def gather(j):
                if j >= RING:
                    pool.wait_ge(s.xgT_ps, j - RING + 1)
                nc.gpsimd.indirect_dma_start(xg[:, j % RING, :], None, xn_dram[f], bass.IndirectOffsetOnAxis(idx[:, 0, j:j + 1], 0)
                                             ).then_inc(s.xg[j % RING], 16)

            def scatter(j):
                pool.wait_ge(s.y, j + 1)
                nc.gpsimd.indirect_dma_start(y_dram[f], bass.IndirectOffsetOnAxis(idx[:, 1, j:j + 1], 0), yt[:, j % RING, :], None,
                                             bounds_check=NO_ROW - 1, oob_is_err=False).then_inc(s.y_out[j % RING], 16)

            pool.wait_ge(s.idx, 1)
            pool.wait_ge(s.xn_out, 16)
            for j in range(RING):
                gather(j)
            pool.wait_ge(s.idx, 2)
            for j in range(MAIN_TILES):
                if j + RING < MAIN_TILES + 1:
                    gather(j + RING)
                scatter(j)
            pool.wait_ge(s.woff, 1)
            with pool.If(load_few(mybir.EngineType.Pool) == 0):
                for j in range(MAIN_TILES + 1, SLOT_TILES):
                    gather(j)
                for j in range(MAIN_TILES, SLOT_TILES):
                    scatter(j)
                for r in range(RING):
                    pool.wait_ge(s.y_out[r], 16 * SLOT_TILES // RING)
            for r in range(RING):
                pool.wait_ge(s.y_out[r], 16 * MAIN_TILES // RING)
            nc.gpsimd.memset(marker[:, :], 0.0).then_inc(s.y_done, 1)

        def ffn_sync(sp, s, f):
            sp.wait_ge(s.ln.xn, NT - len(POOL_TILES))
            sp.wait_ge(s.ln.xn4, len(POOL_TILES))
            sp.dma_start(xn_dram[f].rearrange("(p i) d -> p i d", i=NT), XN[:, :, :]).then_inc(s.xn_out, 16)
            sp.wait_ge(s.y_done, 1)
            yv = y_dram[f].rearrange("(k p i) d -> p k i d", k=K2, i=NT)
            for q in range(PIECES):
                i = piece(q)
                sp.dma_start(Y[:, :, i, :].rearrange("p k i d -> p k (i d)"), yv[:, :, i, :].rearrange("p k i d -> p k (i d)")).then_inc(s.y_in[q], 16)

        def piece(q):
            return slice(PT * q, PT * (q + 1))

        def combine_scalar(act, s, f):
            act.wait_ge(s.wts, 1)
            for q in range(PIECES):
                act.wait_ge(s.y_in[q], 16 * (f + 1))
                for i in range(PT * q, PT * (q + 1)):
                    last = nc.scalar.activation(Y[:, SECOND, i, :], Y[:, SECOND, i, :], ACT.Copy, scale=wts[:, 1, i:i + 1])
                last.then_inc(s.z, 1)

        def combine_vector(dve, s, f, q):
            dve.wait_ge(s.wts, 1)
            dve.wait_ge(s.y_in[q], 16 * (f + 1))
            for i in range(PT * q, PT * (q + 1)):
                last = nc.vector.scalar_tensor_tensor(X[:, i, :], Y[:, FIRST, i, :], wts[:, 0, i:i + 1], X[:, i, :], ALU.mult, ALU.add)
            if q < PIECES - 1:
                last.then_inc(s.x1, 1)
            else:
                dve.wait_ge(s.z, PIECES)
                chain(dve, last)
                nc.vector.tensor_tensor(X[:, piece(q), :], X[:, piece(q), :], Y[:, SECOND, piece(q), :], ALU.add).then_inc(s.x_last, 1)

        def x_updated(eng, s, q):
            if q < PIECES - 1:
                eng.wait_ge(s.xq, q + 1)
            else:
                eng.wait_ge(s.x_last, 1)

        def combine_gpsimd(pool, s):
            for q in range(PIECES - 1):
                pool.wait_ge(s.z, q + 1)
                pool.wait_ge(s.x1, q + 1)
                nc.gpsimd.tensor_tensor(X[:, piece(q), :], X[:, piece(q), :], Y[:, SECOND, piece(q), :], ALU.add).then_inc(s.xq, 1)

        def ahead(update, wait_done, tiles, lead):
            def x_ready(i):
                if i % tiles == 0:
                    if i == 0:
                        for q in range(lead):
                            update(q)
                    if i // tiles + lead < NT // tiles:
                        update(i // tiles + lead)
                    wait_done(i // tiles)
            return x_ready

        UNITS = 2 * NC
        T1, T2, FULL, REST = range(4)

        def fold_tensor(pe):
            pe.wait_ge(aw_in, 64)
            nc.tensor.transpose(PS[:, 5, 0:P], aw[:, AW["ct"], :], ident)
            for n, w in enumerate(FOLDED):
                nc.tensor.matmul(PS[:, 1, n:n + 1], aw[:, AW[w], :], ab[:, AB["ct"]:AB["ct"] + 1], start=True, stop=True)
            pe.wait_ge(bct_done, 1)
            nc.tensor.matmul(PS[:, 1, P:2 * P], bct[:, :], aw[:, AW["uv"], :], start=True, stop=True).then_inc(fold_ps, 1)
            pe.wait_ge(fold_b, 1)
            a = AW[FOLDED[0]]
            nc.tensor.matmul(PS[:, 2, :], ctT[:, :], aw[:, a:a + len(FOLDED), :].rearrange("p w d -> p (w d)"), start=True, stop=True)
            nc.tensor.matmul(PS[:, 6, 0:D], ctT[:, :], aw[:, AW["uv"], :], start=True, stop=True).then_inc(fold_ps, 1)

        def fold_vector(dve):
            dve.wait_ge(aw_in, 64)
            nc.vector.tensor_copy(bct[:, :], ab[:, AB["ct"]:AB["ct"] + 1].to_broadcast([P, P])).then_inc(bct_done, 1)
            dve.wait_ge(fold_ps, 1)
            nc.vector.tensor_copy(ctT[:, :], PS[:, 5, 0:P])
            a = AB[FOLDED[0]]
            nc.vector.tensor_tensor(bv_rows[:, :], bv_rows[:, :], PS[:, 1, P:2 * P], ALU.add)
            nc.vector.tensor_tensor(ab[:, a:a + len(FOLDED)], ab[:, a:a + len(FOLDED)], PS[:, 1, 0:len(FOLDED)], ALU.add).then_inc(fold_b, 1)
            dve.wait_ge(fold_ps, 2)
            a = AW[FOLDED[0]]
            nc.vector.tensor_copy(aw[:, AW["uv"], :], PS[:, 6, 0:D])
            nc.vector.tensor_copy(aw[:, a:a + len(FOLDED), :].rearrange("p w d -> p (w d)"), PS[:, 2, :]).then_inc(folded, 1)

        def prepare_product(bank, w, c_):
            return nc.tensor.matmul(PS[:, bank, :], aw[:, AW[w], :], XNT[:, c_ * CH:(c_ + 1) * CH], start=True, stop=True)

        def prepare_values(c_):
            for i in range(4 * c_, 4 * c_ + 4):
                last = nc.tensor.matmul(PS[:, 2, i % 4 * P:(i % 4 + 1) * P], XNT[:, i * P:(i + 1) * P], aw[:, AW["uv"], :],
                                        start=True, stop=True)
            last.then_inc(v_ps, 1)

        def prepare_first(pe, g):
            if g == 0:
                pe.wait_ge(folded, 1)
                pe.wait_ge(aln.xnT, 1)
                prepare_product(3, "kr", 0)
                prepare_product(4, "krs", 0).then_inc(rot_ps, 1)
            elif g == 1:
                prepare_product(5, "uk", 0).then_inc(lin_ps, 1)
                prepare_values(0)
            elif g == 2:
                prepare_product(6, "qr", 0)
                prepare_product(7, "qrs", 0).then_inc(rot_ps, 1)

        def prepare_tensor(pe):
            def norm(u):
                c_, half = u // 2, u % 2
                pe.wait_ge(square, u + 1)
                hs = hsum_b[:, 32 * half:32 * half + 32]
                nc.tensor.matmul(PS[32 * c_:32 * c_ + 32, 1, :], hs, square_b[:, u % 2, :],
                                 start=(half == 0), stop=(half == 1)).then_inc(norms, 1)

            pe.wait_ge(aln.xnT, NC)
            prepare_product(0, "uq", 0).then_inc(lin_ps, 1)
            for c_ in range(1, NC):
                pe.wait_ge(mixed, 2 * c_ - 1)
                prepare_product(3, "kr", c_)
                prepare_product(4, "krs", c_).then_inc(rot_ps, 1)
                prepare_product(5, "uk", c_).then_inc(lin_ps, 1)
                pe.wait_ge(v_done, c_)
                if c_ < NC - 1:
                    prepare_values(c_)
                pe.wait_ge(mixed, 2 * c_)
                prepare_product(6, "qr", c_)
                prepare_product(7, "qrs", c_).then_inc(rot_ps, 1)
                prepare_product(0, "uq", c_).then_inc(lin_ps, 1)
                if c_ == NC - 1:
                    prepare_values(c_)
                norm(2 * c_ - 2)
                norm(2 * c_ - 1)
            pe.wait_ge(mixed, UNITS - 1)
            norm(UNITS - 2)
            norm(UNITS - 1)
            pe.wait_ge(nmax_done, 1)
            pe.wait_ge(v_done, NC)
            nc.tensor.transpose(PS[0:1, 2, 0:P], nmax[:, :], ident).then_inc(nmax_T, 1)
            keep_warm(10, 4)

        def prepare_scalar(act):
            for u in range(UNITS):
                if u < UNITS - 1:
                    act.wait_ge(full_q, u + 1)
                else:
                    act.wait_ge(last_unit, 1)
                if u >= 2:
                    act.wait_ge(parts_out[u % 2], (16, 16 * PARTS)[u % 2] * (u // 2))
                nc.scalar.copy(parts[:, u % 2, 0, :], temp[:, FULL, u % 2, :]).then_inc(part0, 1)
                if u >= 2:
                    act.wait_ge(norms, u - 1)
                nc.scalar.activation(square_b[:, u % 2, :], temp[:, FULL, u % 2, :], ACT.Square).then_inc(square, 1)
                if u < UNITS - 1:
                    act.wait_ge(rest1, u + 1)
                else:
                    act.wait_ge(last_unit, 2)
                nc.scalar.copy(parts[:, u % 2, 1, :], temp[:, REST, u % 2, :]).then_inc(part1, 1)

        def prepare_vector(dve):
            dve.wait_ge(rope_in, 32)

            def third(u):
                dve.wait_ge(part1, u + 1)
                nc.vector.tensor_tensor(parts[:, u % 2, 2, :], temp[:, REST, u % 2, :], parts[:, u % 2, 1, :], ALU.subtract).then_inc(part2, 1)

            for u in range(UNITS):
                c_, b = u // 2, u % 2
                cols = slice(c_ * CH, (c_ + 1) * CH)
                rot, rots, lin = ((3, 4, 5), (6, 7, 0))[b]
                names = (("kr", "krs", "uk"), ("qr", "qrs", "uq"))[b]
                bias = [ab[:, AB[n]:AB[n] + 1] for n in names]
                dve.wait_ge(rot_ps, u + 1)
                if u >= 2:
                    dve.wait_ge(full_q, u - 1)
                chain(dve, nc.vector.scalar_tensor_tensor(temp[:, T1, b, :], PS[:, rot, :], bias[0], cosT[:, cols], ALU.add, ALU.mult))
                nc.vector.scalar_tensor_tensor(temp[:, T2, b, :], PS[:, rots, :], bias[1], sinT[:, cols], ALU.add, ALU.mult)
                dve.wait_ge(lin_ps, u + 1)
                last = nc.vector.scalar_tensor_tensor(temp[:, T1, b, :], PS[:, lin, :], bias[2], temp[:, T1, b, :], ALU.add, ALU.add)
                last.then_inc(mixed, 1)
                if u == UNITS - 1:
                    dve.wait_ge(mixed, UNITS)
                    dve.wait_ge(square, u - 1)
                    nc.vector.tensor_tensor(temp[:, FULL, b, :], temp[:, T1, b, :], temp[:, T2, b, :], ALU.add).then_inc(last_unit, 1)
                if b == (1 if c_ == NC - 1 else 0):
                    dve.wait_ge(v_ps, c_ + 1)
                    nc.vector.tensor_tensor(V[:, 4 * c_:4 * c_ + 4, :], PS[:, 2, :].rearrange("p (i d) -> p i d", d=D),
                                            bc(bv_rows[:, :].unsqueeze(1), [P, 4, D]), ALU.add).then_inc(v_done, 1)
                if 1 <= u < UNITS - 1:
                    third(u - 1)
            dve.wait_ge(part0, UNITS)
            nc.vector.tensor_tensor(temp[:, REST, 1, :], temp[:, FULL, 1, :], parts[:, 1, 0, :], ALU.subtract).then_inc(last_unit, 1)
            third(UNITS - 2)
            dve.wait_ge(norms, UNITS)
            nc.vector.tensor_reduce(nmax[:, :], PS[:, 1, :], AX.X, ALU.max).then_inc(nmax_done, 1)
            third(UNITS - 1)
            dve.wait_ge(nmax_T, 1)
            chain(dve, nc.vector.tensor_reduce(nrow[:, :], PS[0:1, 2, 0:P].rearrange("p (c m) -> p m c", m=2 * H), AX.X, ALU.max))
            chain(dve, nc.vector.tensor_tensor(bound[:, :], nrow[:, 0:H], nrow[:, H:], ALU.mult))
            chain(dve, nc.vector.tensor_reduce(largest[:, :], bound[:, :], AX.X, ALU.max))
            nc.vector.tensor_scalar(safe[:, :], largest[:, :], (SCORE_SAFE / SCORE_SCALE) ** 2, None, ALU.is_le).then_inc(safe_done, 1)

        def pads_gpsimd(pool):
            nc.gpsimd.memset(warm[:, :], 0.0)
            nc.gpsimd.memset(zeros_b[:, :].bitcast(F32), 0.0).then_inc(pads, 1)
            nc.gpsimd.memset(vslot[:, :, :, :], 0.0).then_inc(pads, 1)
            nc.gpsimd.memset(zeros48[:, :].bitcast(F32), 0.0).then_inc(pads, 1)
            pool.wait_ge(pads, 3)
            nc.gpsimd.memset(qslot[64:P, :, :].bitcast(F32), 0.0)
            nc.gpsimd.memset(kslot[64:P, :, :].bitcast(F32), 0.0).then_inc(pads, 1)
            pool.wait_ge(pads, 4)
            nc.gpsimd.memset(vslot[:, :, :, HD:HD + 1], 1.0).then_inc(pads, 1)

        def prepare_gpsimd(pool):
            for u in range(UNITS - 1):
                b = u % 2
                pool.wait_ge(mixed, u + 1)
                if u >= 2:
                    pool.wait_ge(square, u - 1)
                nc.gpsimd.tensor_tensor(temp[:, FULL, b, :], temp[:, T1, b, :], temp[:, T2, b, :], ALU.add).then_inc(full_q, 1)
                pool.wait_ge(part0, u + 1)
                if u >= 2:
                    pool.wait_ge(part2, u - 1)
                nc.gpsimd.tensor_tensor(temp[:, REST, b, :], temp[:, FULL, b, :], parts[:, b, 0, :], ALU.subtract).then_inc(rest1, 1)

        def load_head(sp, h, r, done):
            load_k(sp, h, r, slice(0, T), done)
            load_q(sp, h, r, slice(0, T), done)

        def load_k(sp, h, r, cols, done):
            rows = slice(HD * h, HD * h + HD) if isinstance(h, int) else bass.ds(h * HD, HD)
            k = k_dram[rows, :, cols].rearrange("d j n -> (d j) n").unsqueeze(0)
            sp.dma_start(kslot[0:ROWS, r, cols], k.to_broadcast([PARTS, HD * PARTS, cols.stop - cols.start])).then_inc(done, 16)

        def load_q(sp, h, r, cols, done):
            head = slice(h, h + 1) if isinstance(h, int) else bass.ds(h, 1)
            q = q_dram[head, :, :, cols].rearrange("h i d n -> (h i d) n").unsqueeze(1)
            sp.dma_start(qslot[0:ROWS, r, cols], q.to_broadcast([PARTS * HD, PARTS, cols.stop - cols.start])).then_inc(done, 16)

        def load_shift(sp, h, r, done):
            src = shift_dram[:, h, :] if isinstance(h, int) else shift_dram[:, bass.ds(h, 1), :].rearrange("a h n -> a (h n)")
            sp.dma_start(qslot[SHIFT_ROW:SHIFT_ROW + PARTS, r, :], src).then_inc(done, 16)

        HEAD_DMAS = 2

        def unbounded(engine_type, eng, ready):
            eng.wait_ge(ready, 1)
            flag = nc.values_load(safe[0:1, 0:1], engines=[engine_type], min_val=0, max_val=1,
                                  skip_runtime_bounds_check_because="a comparison's result")
            return eng.If(flag == 0)

        MAX_SLOT = SLOTS - 1

        def maxima_sync(sp):
            with sp.Fori(0, H) as h:
                sp.wait_ge(m_max, h * NT + 1)
                load_head(sp, h, MAX_SLOT, m_head)
            sp.wait_ge(m_max, H * NT + 1)
            sp.wait_ge(m_step, 2 * PARTS + 1)
            sp.dma_start(shift_dram.rearrange("a (b g) (i q) -> (g i) a b q", b=2, q=P), sparts[:, :, :, :]).then_inc(m_out, 16)
            sp.wait_ge(m_out, 16)
            for h in range(SLOTS):
                load_shift(sp, h, h, m_out)
            sp.wait_ge(m_out, 16 * (1 + SLOTS))

        def maxima_tensor(pe):
            with pe.Fori(0, H) as h:
                pe.wait_ge(m_head, (h + 1) * (16 * HEAD_DMAS))
                for i in range(NT):
                    pe.wait_ge(m_max, h * NT + i if i >= 1 else h * NT + 1)
                    for k in range(NC):
                        last = nc.tensor.matmul(PS[:, 4 * (i % 2) + k, :], qslot[0:KR, MAX_SLOT, i * P:(i + 1) * P],
                                                kslot[0:KR, MAX_SLOT, k * CH:(k + 1) * CH], start=True, stop=True)
                    last.then_inc(m_score, 1)
            pe.wait_ge(m_max, H * NT + 1)
            for b in range(2):
                last = nc.tensor.transpose(PS[:, 0, b * P:(b + 1) * P], smax[:, b, :], ident)
            last.then_inc(m_T, 1)
            pe.wait_ge(m_out, 16 * (1 + SLOTS))

        def maxima_vector(dve):
            nc.vector.memset(snext[:, :, :], 0.0).then_inc(m_max, 1)
            flat = smax[:, :, :].rearrange("p b n -> p (b n)")
            with dve.Fori(0, H) as h:
                for i in range(NT):
                    b = 4 * (i % 2)
                    dve.wait_ge(m_score, h * NT + (i + 1))
                    nc.vector.tensor_reduce(flat[:, bass.ds(h * NT + i, 1)], PS[:, b:b + 4, :], AX.XY, ALU.max).then_inc(m_max, 1)
            dve.wait_ge(m_T, 1)
            nc.vector.tensor_scalar(snext[:, :, :], PS[:, 0, 0:2 * P].rearrange("p (b n) -> p b n", b=2), -1.0, None, ALU.mult).then_inc(m_step, 1)
            for a in range(PARTS):
                dve.wait_ge(m_step, 2 * a + 1)
                nc.vector.tensor_copy(sparts[:, a, :, :], snext[:, :, :]).then_inc(m_step, 1)
                dve.wait_ge(m_step, 2 * a + 2)
                nc.vector.tensor_tensor(snext[:, :, :], snext[:, :, :], sparts[:, a, :, :], ALU.subtract).then_inc(m_step, 1)

        def attention_sync(sp):
            early, tail = slice(0, (NC - 1) * CH), slice((NC - 1) * CH, T)
            sp.wait_ge(pads, 4)
            sp.wait_ge(consts_cast, 1)
            for r in range(SLOTS):
                sp.dma_start(kslot[SHIFT_ROW:SHIFT_ROW + PARTS, r, :].rearrange("a (i n) -> a i n", n=P),
                             ones_b[0:PARTS, :].unsqueeze(1).to_broadcast([PARTS, NT, P])).then_inc(const_rows, 16)
            sp.dma_start(shift_dram.rearrange("a h (i n) -> (a h) i n", n=P),
                         zeros48[:, :].unsqueeze(1).to_broadcast([PARTS * H, NT, P])).then_inc(const_rows, 16)
            for u in range(UNITS):
                c_, b = u // 2, u % 2
                cols = slice(c_ * CH, (c_ + 1) * CH)
                if b == 0:
                    if c_ == NC - 1:
                        sp.wait_ge(const_rows, 16 * (SLOTS + 1))
                        sp.wait_ge(parts_out[0], 16 * (NC - 1))
                        load_k(sp, 0, 0, early, head_in[0])
                        sp.wait_ge(parts_out[1], 16 * PARTS * (NC - 1))
                        load_q(sp, 0, 0, early, head_in[0])
                    sp.wait_ge(part2, u + 1)
                    sp.dma_start(k_dram[:, :, cols], parts[:, b, :, :]).then_inc(parts_out[b], 16)
                else:
                    last = c_ == NC - 1
                    for a, done in enumerate((part0, part1, part2)):
                        sp.wait_ge(done, u + 1)
                        if last:
                            sp.dma_start(qslot[PARTS * HD * a:PARTS * HD * (a + 1), 0, cols],
                                         parts[0:HD, b, a:a + 1, :].to_broadcast([HD, PARTS, CH])).then_inc(first_q, 16)
                        sp.dma_start(q_dram[:, a, :, cols], parts[:, b, a, :]).then_inc(parts_out[b], 16)
            sp.wait_ge(parts_out[1], 16 * PARTS * NC)
            sp.wait_ge(parts_out[0], 16 * NC)
            load_k(sp, 0, 0, tail, first_k)
            load_head(sp, 1, 1, head_in[1])
            with unbounded(mybir.EngineType.SP, sp, safe_done):
                maxima_sync(sp)
            load_head(sp, SLOTS - 1, SLOTS - 1, head_in[SLOTS - 1])
            with sp.Fori(1, H // SLOTS) as n:
                for r in range(SLOTS):
                    sp.wait_ge(score, (n * SLOTS + (r - SLOTS + 1)) * 32)
                    load_head(sp, n * SLOTS + r, r, head_in[r])
                    load_shift(sp, n * SLOTS + r, r, shift_in[r])
            sp.wait_ge(score, (H - SLOTS) * 32)
            load_head(sp, H - 1, 0, head_in[0])
            load_shift(sp, H - 1, 0, shift_in[0])

        BODY = SLOTS * NT

        def attention_tensor(pe):
            def scores(u0, v, half):
                h, kt, r = v // NT, v % NT, (v // NT) % SLOTS
                g = 2 * v + half
                fixed = isinstance(u0, int)
                if fixed and u0 + v == (NC - 1) * CH // P and half == 0:
                    pe.wait_ge(first_k, 16)
                if kt == 0 and half == 0:
                    before = (u0 // BODY if fixed else u0) + v // BODY
                    pe.wait_ge(head_in[r], before * (16 * HEAD_DMAS) + 16 * HEAD_DMAS)
                    if not (fixed and before == 0):
                        pe.wait_ge(shift_in[r], before * 16)
                    elif r == 0:
                        pe.wait_ge(first_q, 16 * PARTS)
                G = (2 * u0 if fixed else u0 * (2 * BODY)) + g
                if not (fixed and G < GB):
                    pe.wait_ge(exped, G - GB + 1)
                for k in range(2):
                    last = nc.tensor.matmul(PS[:, 2 * (g % GB) + k, :], kslot[0:KR, r, kt * P:(kt + 1) * P],
                                            qslot[0:KR, r, (2 * half + k) * CH:(2 * half + k + 1) * CH], start=True, stop=True)
                last.then_inc(score, 1)

            def values(u0, v):
                fixed = isinstance(u0, int)
                kt = v % NT
                r = (v // NT) % SLOTS
                U = (u0 if fixed else u0 * BODY) + v
                if kt == 0:
                    hh = (u0 // NT if fixed else u0 * SLOTS) + v // NT
                    pe.wait_ge(head_v, hh + 1)
                    if not (fixed and hh == 0):
                        pe.wait_ge(o_copied, hh)
                pe.wait_ge(exped, U * 2 + 2)
                for q in range(NC):
                    last = nc.tensor.matmul(PS[32 * q:32 * q + 32, 6, :], vslot[:, r, kt, :], EXP[:, v % SLOTS, q * CH:(q + 1) * CH],
                                            start=(kt == 0), stop=(kt == NT - 1))
                last.then_inc(pv, 1)

            def step(u0, v, left=2):
                if left >= 1:
                    scores(u0, v + 1, 1)
                if not (isinstance(u0, int) and u0 + v == 0):
                    values(u0, v - 1)
                if left >= 2:
                    scores(u0, v + 2, 0)

            pe.wait_ge(v_done, 4)
            pe.wait_ge(pads, 5)
            pe.wait_ge(const_rows, 16 * (SLOTS + 1))
            with unbounded(mybir.EngineType.PE, pe, safe_done):
                maxima_tensor(pe)
            scores(0, 0, 0)
            scores(0, 0, 1)
            scores(0, 1, 0)
            for v in range(BODY):
                step(0, v)
            with pe.Fori(1, H // SLOTS) as n:
                for v in range(BODY):
                    step(n, v)
            last = (H // SLOTS) * BODY
            for v in range(NT):
                step(last, v, left=NT - 1 - v)
            values(last, NT - 1)

        def attention_scalar(act):
            def exps(u0, v):
                fixed = isinstance(u0, int)
                U = (u0 if fixed else u0 * BODY) + v
                for half in range(2):
                    g = 2 * v + half
                    act.wait_ge(score, U * 2 + (half + 1))
                    if half == 0 and not (fixed and U < SLOTS):
                        act.wait_ge(pv, U - SLOTS + 1)
                    b = 2 * (g % GB)
                    nc.scalar.activation(EXP[:, v % SLOTS, half * 2 * CH:(half + 1) * 2 * CH].rearrange("p (b n) -> p b n", b=2),
                                         PS[:, b:b + 2, :], ACT.Exp, scale=SCORE_SCALE).then_inc(exped, 1)

            for v in range(BODY):
                exps(0, v)
            with act.Fori(1, H // SLOTS) as n:
                for v in range(BODY):
                    exps(n, v)
            for v in range(NT):
                exps((H // SLOTS) * BODY, v)

        def attention_vector(dve):
            def head_values(h, r):
                if not (isinstance(h, int) and h < SLOTS):
                    dve.wait_ge(pv, (h - SLOTS + 1) * NT)
                cols = slice(HD * h, HD * h + HD) if isinstance(h, int) else bass.ds(h * HD, HD)
                nc.vector.tensor_copy(vslot[:, r, :, 0:HD], V[:, :, cols]).then_inc(head_v, 1)

            def finish(h):
                dve.wait_ge(pv, (h + 1) * NT)
                if not (isinstance(h, int) and h == 0):
                    dve.wait_ge(o_norm, h)
                nc.vector.transpose(Oq[:, :], PS[:, 6, :]).then_inc(o_copied, 1)

            def divide(h):
                cols = slice(HD * h, HD * h + HD) if isinstance(h, int) else bass.ds(h * HD, HD)
                t = Oq[:, :].rearrange("p (c m) -> p c m", m=32)
                dve.wait_ge(o_copied, h + 1)
                nc.vector.reciprocal(denom[:, :], t[:, :, HD]).then_inc(denom_done, 1)
                dve.wait_ge(denom_done, h + 1)
                nc.vector.tensor_tensor(A[:, :, cols], t[:, :, 0:HD], bc(denom[:, :].unsqueeze(2), [P, NT, HD]), ALU.mult).then_inc(o_norm, 1)

            dve.wait_ge(v_done, 4)
            dve.wait_ge(pads, 5)
            for h in range(SLOTS):
                head_values(h, h)
            with unbounded(mybir.EngineType.DVE, dve, safe_done):
                maxima_vector(dve)
            for r in range(SLOTS):
                finish(r)
                divide(r)
                head_values(SLOTS + r, r)
            with dve.Fori(1, H // SLOTS - 1) as n:
                for r in range(SLOTS):
                    finish(n * SLOTS + r)
                    divide(n * SLOTS + r)
                    head_values((n + 1) * SLOTS + r, r)
            for h in range(H - SLOTS - 1, H):
                finish(h)
                divide(h)
                if h == H - SLOTS - 1:
                    head_values(H - 1, 0)

        def project_tensor(pe):
            pe.wait_ge(o_norm, H)
            pe.wait_ge(exped, 2 * H * NT)
            for g in range(4):
                if g >= 2:
                    pe.wait_ge(a_Tc, g - 1)
                for k in range(4):
                    last = nc.tensor.transpose(PS[:, g % 2, k * P:(k + 1) * P], A[:, 4 * g + k, :], ident)
                last.then_inc(a_T, 1)
                if g >= 1:
                    project(pe, g - 1)
            project(pe, 3)

        def project(pe, g):
            pe.wait_ge(a_Tc, g + 1)
            if g >= 2:
                pe.wait_ge(x_attn, g - 1)
            for k in range(4):
                i = 4 * k + g
                last = nc.tensor.matmul(PS[:, 2 + g % 2, k * P:(k + 1) * P], AT[:, i * P:(i + 1) * P], aw[:, AW["wo"], :], start=True, stop=True)
            last.then_inc(proj, 1)

        def project_scalar(act):
            for g in range(4):
                act.wait_ge(a_T, g + 1)
                nc.scalar.copy(AT[:, :].rearrange("p (q c t) -> p c q t", q=4, t=32)[:, 4 * g:4 * g + 4],
                               PS[:, g % 2, :].rearrange("p (c q t) -> p c q t", c=4, t=32)).then_inc(a_Tc, 1)

        def project_vector(dve, g):
            dve.wait_ge(proj, g + 1)
            x = X[:, :, :].rearrange("p (k g) d -> p g k d", g=4)[:, g]
            nc.vector.tensor_tensor(x, PS[:, 2 + g % 2, :].rearrange("p (i d) -> p i d", d=D), x, ALU.add).then_inc(x_attn, 1)

        x_rows = ins["L0_attn_x"][0].rearrange("(p i) d -> p i d", i=NT)
        out_rows = out[0].rearrange("(p i) d -> p i d", i=NT)

        block = ctx.enter_context(nc.Block())

        @block.sync
        def _(sp):
            for q in range(4):
                sp.dma_start(X[:, 4 * q:4 * q + 4, :], x_rows[:, 4 * q:4 * q + 4, :]).then_inc(x_in[q], 16)
            sp.dma_start(cst[:, :], const).then_inc(const_in, 16)
            sp.dma_start(Wr[:, :], ins["L0_ffn_Wr"]).then_inc(wr_in, 16)
            sp.dma_start(Wgu[:, :, 0:F], ins["L0_ffn_Wg"].rearrange("e h i -> h e i")).then_inc(wexp_in, 16)
            sp.dma_start(Wgu[:, :, F:], ins["L0_ffn_Wu"].rearrange("e h i -> h e i")).then_inc(wexp_in, 16)
            for n, (a, w) in enumerate(FCH):
                sp.dma_start(Wd[0:w, :, n, :], ins["L0_ffn_Wd"][:, a:a + w, :].rearrange("e p d -> p e d")).then_inc(wexp_in, 16)
            ffn_sync(sp, S[0], 0)
            attention_sync(sp)
            ffn_sync(sp, S[1], 1)
            for q in range(PIECES):
                x_updated(sp, S[1], q)
                sp.dma_start(out_rows[:, piece(q), :], X[:, piece(q), :]).then_inc(out_done, 16)
            sp.wait_ge(out_done, 16 * PIECES)

        @block.vector
        def _(dve):
            nc.vector.memset(eps[:, :], LN_EPS)
            layernorm_vector(dve, S[0].ln, lambda i: dve.wait_ge(x_in[i // 4], 16) if i % 4 == 0 else None)
            dve.wait_ge(const_in, 16)
            nc.vector.tensor_copy(lower_b[:, :], c("lower"))
            nc.vector.tensor_copy(hsum_b[:, :], c("hsum"))
            nc.vector.tensor_copy(ones_b[:, :], c("ones")).then_inc(consts_cast, 1)
            nc.vector.tensor_copy(token_h[:, :], c("token1"))
            nc.vector.tensor_copy(slot_h[:, :, :], bc(c("iota").unsqueeze(2), [P, P, K2 * NT]))
            chain(dve, nc.vector.tensor_copy(tile_h[:, :, :], bc(c("jstart").unsqueeze(2), [P, SLOT_TILES, K2 * NT])))
            route_vector(dve, S[0])
            experts_vector(dve, S[0])
            fold_vector(dve)
            layernorm_vector(dve, aln, ahead(lambda q: combine_vector(dve, S[0], 0, q), lambda q: x_updated(dve, S[0], q), PT, 3))
            prepare_vector(dve)
            attention_vector(dve)
            dve.wait_ge(bias_o, 1)
            layernorm_vector(dve, S[1].ln, ahead(lambda g: project_vector(dve, g), lambda g: dve.wait_ge(x_attn, g + 1), 4, 1),
                             [4 * k + g for g in range(4) for k in range(4)])
            route_vector(dve, S[1])
            experts_vector(dve, S[1])
            for q in range(PIECES):
                combine_vector(dve, S[1], 1, q)

        @block.scalar
        def _(act):
            layernorm_scalar(act, S[0].ln)
            route_scalar(act, S[0])
            act.dma_start(cosT[:, :], rope_cos).then_inc(rope_in, 16)
            act.dma_start(sinT[:, :], rope_sin).then_inc(rope_in, 16)
            act.dma_start(aw[:, :, :], attn_w).then_inc(aw_in, 16)
            act.dma_start(ab[:, :], attn_b).then_inc(aw_in, 16)
            act.dma_start(bv_rows[:, :], attn_rows[0:1, :].to_broadcast([P, D])).then_inc(aw_in, 16)
            act.dma_start(bo_rows[:, :], attn_rows[1:2, :].to_broadcast([P, D])).then_inc(aw_in, 16)
            experts_scalar(act, S[0])
            combine_scalar(act, S[0], 0)
            layernorm_scalar(act, aln)
            prepare_scalar(act)
            attention_scalar(act)
            project_scalar(act)
            layernorm_scalar(act, S[1].ln)
            route_scalar(act, S[1])
            experts_scalar(act, S[1])
            combine_scalar(act, S[1], 1)

        @block.tensor
        def _(pe):
            pe.wait_ge(pads, 2)
            pe.wait_ge(x_in[3], 16)
            keep_warm(10)
            pe.wait_ge(const_in, 16)
            pe.wait_ge(wr_in, 16)
            layernorm_tensor(pe, S[0].ln, lambda g: route_logits(pe, S[0], g))
            route_tensor(pe, S[0])
            experts_tensor(pe, S[0])
            fold_tensor(pe)
            pe.wait_ge(S[0].xq, PIECES - 2)
            keep_warm(18)
            layernorm_tensor(pe, aln, lambda g: prepare_first(pe, g))
            prepare_tensor(pe)
            attention_tensor(pe)
            project_tensor(pe)
            keep_warm(28)
            layernorm_tensor(pe, S[1].ln, lambda g: route_logits(pe, S[1], g))
            route_tensor(pe, S[1])
            experts_tensor(pe, S[1])

        @block.gpsimd
        def _(pool):
            pads_gpsimd(pool)
            layernorm_gpsimd(pool, S[0].ln)
            experts_gpsimd(pool, S[0], 0)
            combine_gpsimd(pool, S[0])
            layernorm_gpsimd(pool, aln)
            prepare_gpsimd(pool)
            pool.wait_ge(aln.xn, NT - len(POOL_TILES))
            nc.gpsimd.tensor_tensor(X[:, :, :], X[:, :, :], bc(bo_rows[:, :].unsqueeze(1), [P, NT, D]), ALU.add).then_inc(bias_o, 1)
            layernorm_gpsimd(pool, S[1].ln)
            experts_gpsimd(pool, S[1], 1)
            combine_gpsimd(pool, S[1])


def kernel(**inputs):
    import concourse.bacc as bacc
    from concourse.bass_utils import run_bass_kernel_spmd

    nc = bacc.Bacc("TRN2", target_bir_lowering=False, num_devices=1)
    arrays = {}

    def given(name, a):
        arrays[name] = np.ascontiguousarray(a)
        return nc.dram_tensor(name, arrays[name].shape, F32, kind="ExternalInput").ap()

    ins = {n: given("in_" + n, inputs[n]) for n in ("L0_attn_x", "L0_ffn_Wr", "L0_ffn_Wg", "L0_ffn_Wu", "L0_ffn_Wd")}
    weights, biases, rows = pack_attention({n: a for n, a in inputs.items() if n.startswith("L0_attn_") and n != "L0_attn_x"})
    cos, sin = rope_arrays()
    out = nc.dram_tensor("out", (1, T, D), F32, kind="ExternalOutput").ap()
    macaron_block(nc, ins, given("const", constant_array()), given("rope_cos", cos), given("rope_sin", sin),
                  given("attn_w", weights), given("attn_b", biases), given("attn_rows", rows), out)
    return run_bass_kernel_spmd(nc, [arrays], core_ids=[0]).results[0]["out"]
```
